# Optimizing a Trainium2 kernel written in Bass

```python
import numpy as np
import jax
import jax.numpy as jnp

def _softmax(x, axis=-1):
    return jax.nn.softmax(x, axis=axis)

def _gelu(x):
    return jax.nn.gelu(x, approximate=True)

def _silu(x):
    return jax.nn.silu(x)

def _sigmoid(x):
    return jax.nn.sigmoid(x)

def _layernorm(x, axis=-1, eps=1e-05):
    m = jnp.mean(x, axis=axis, keepdims=True)
    v = jnp.var(x, axis=axis, keepdims=True)
    return (x - m) / jnp.sqrt(v + eps)

def _scatter_add(tgt, idx, src, axis=0):
    return tgt.at[idx].add(src)

def _segment_sum(src, seg, n):
    return jax.ops.segment_sum(src, seg, n)
kernel_name = 'mk_gnn_ffn_d1_gnn_r8_88466e'

def setup_inputs(seed: int=0):
    np.random.seed(seed)
    _w = jnp.asarray

    def _rec_inputs():
        import jax
        import jax.numpy as jnp
        _gk = jax.random.key(seed)
        x = -8.776e-05 + 1 * jax.random.normal(jax.random.fold_in(_gk, 1), (6250, 256), jnp.float32)
        _s = jax.random.randint(jax.random.fold_in(_gk, 2), (50000,), 0, 6250, jnp.int32)
        _d = jax.random.randint(jax.random.fold_in(_gk, 3), (50000,), 0, 6250, jnp.int32)
        _loop = jnp.arange(6250, dtype=jnp.int32)
        src = jnp.concatenate([_s, _d, _loop])
        dst = jnp.concatenate([_d, _s, _loop])
        _o = jnp.argsort(dst, stable=True)
        src = src[_o]
        dst = dst[_o]
        edge_attr_256 = 2.93046e-05 + 1.00006 * jax.random.normal(jax.random.fold_in(_gk, 11), (106250, 256), jnp.float32)
        return (x, src, dst, edge_attr_256)
    x, src, dst, edge_attr_256 = _rec_inputs()

    def _L0_gnn_setup():
        import jax, jax.numpy as jnp
        import numpy as np
        N, E, D = (2500, 40000, 256)
        H, C = (8, 32)
        key = jax.random.key(seed)
        ks = jax.random.split(key, 12)
        s = 1.0 / np.sqrt(D)
        return {'x': jax.random.normal(ks[0], (N, D), jnp.float32), 'edge_index': jax.random.randint(ks[1], (2, E), 0, N, jnp.int64), 'edge_attr': jax.random.normal(ks[2], (E, D), jnp.float32), 'Wq': jax.random.normal(ks[3], (D, H * C), jnp.float32) * s, 'bq': jnp.zeros((H * C,), jnp.float32), 'Wk': jax.random.normal(ks[4], (D, H * C), jnp.float32) * s, 'bk': jnp.zeros((H * C,), jnp.float32), 'Wv': jax.random.normal(ks[5], (D, H * C), jnp.float32) * s, 'bv': jnp.zeros((H * C,), jnp.float32), 'We': jax.random.normal(ks[6], (D, H * C), jnp.float32) * s, 'Ws': jax.random.normal(ks[7], (D, H * C), jnp.float32) * s, 'bs': jnp.zeros((H * C,), jnp.float32)}
    _L0_gnn_all = _L0_gnn_setup()
    _L0_gnn_in = {k: v for k, v in _L0_gnn_all.items() if k in ('Wq', 'bq', 'Wk', 'bk', 'Wv', 'bv', 'We', 'Ws', 'bs')}
    del _L0_gnn_all

    def _L0_ffn_setup():
        import jax, jax.numpy as jnp
        import numpy as np
        D_MODEL = 256
        EXPERT_DIM = 512
        NUM_EXPERTS = 8
        TOP_K = 2
        SEQ_LEN = 256
        BATCH = 2
        key = jax.random.key(seed)
        ks = jax.random.split(key, 8)
        s = 0.02
        x = jax.random.normal(ks[0], (SEQ_LEN, BATCH, D_MODEL), dtype=jnp.float32)
        Wg = jax.random.normal(ks[1], (D_MODEL, NUM_EXPERTS), dtype=jnp.float32) * s
        bg = jax.random.normal(ks[2], (NUM_EXPERTS,), dtype=jnp.float32) * s
        bias = jnp.zeros((NUM_EXPERTS,), dtype=jnp.float32)
        W1 = jax.random.normal(ks[3], (NUM_EXPERTS, D_MODEL, EXPERT_DIM), dtype=jnp.float32) * s
        b1 = jax.random.normal(ks[4], (NUM_EXPERTS, EXPERT_DIM), dtype=jnp.float32) * s
        W2 = jax.random.normal(ks[5], (NUM_EXPERTS, EXPERT_DIM, D_MODEL), dtype=jnp.float32) * s
        b2 = jax.random.normal(ks[6], (NUM_EXPERTS, D_MODEL), dtype=jnp.float32) * s
        return {'x': x, 'Wg': Wg, 'bg': bg, 'bias': bias, 'W1': W1, 'b1': b1, 'W2': W2, 'b2': b2}
    _L0_ffn_all = _L0_ffn_setup()
    _L0_ffn_in = {k: v for k, v in _L0_ffn_all.items() if k in ('Wg', 'bg', 'bias', 'W1', 'b1', 'W2', 'b2')}
    del _L0_ffn_all
    return {'x': x, 'src': src, 'dst': dst, 'edge_attr_256': edge_attr_256, 'L0_gnn_Wq': _L0_gnn_in['Wq'], 'L0_gnn_bq': _L0_gnn_in['bq'], 'L0_gnn_Wk': _L0_gnn_in['Wk'], 'L0_gnn_bk': _L0_gnn_in['bk'], 'L0_gnn_Wv': _L0_gnn_in['Wv'], 'L0_gnn_bv': _L0_gnn_in['bv'], 'L0_gnn_We': _L0_gnn_in['We'], 'L0_gnn_Ws': _L0_gnn_in['Ws'], 'L0_gnn_bs': _L0_gnn_in['bs'], 'L0_ffn_Wg': _L0_ffn_in['Wg'], 'L0_ffn_bg': _L0_ffn_in['bg'], 'L0_ffn_bias': _L0_ffn_in['bias'], 'L0_ffn_W1': _L0_ffn_in['W1'], 'L0_ffn_b1': _L0_ffn_in['b1'], 'L0_ffn_W2': _L0_ffn_in['W2'], 'L0_ffn_b2': _L0_ffn_in['b2']}

def reference(x, src, dst, edge_attr_256, L0_gnn_Wq, L0_gnn_bq, L0_gnn_Wk, L0_gnn_bk, L0_gnn_Wv, L0_gnn_bv, L0_gnn_We, L0_gnn_Ws, L0_gnn_bs, L0_ffn_Wg, L0_ffn_bg, L0_ffn_bias, L0_ffn_W1, L0_ffn_b1, L0_ffn_W2, L0_ffn_b2):
    import jax
    import jax.numpy as jnp

    def _L0_gnn_ref(x, edge_index, edge_attr, Wq, bq, Wk, bk, Wv, bv, We, Ws, bs):
        import jax, jax.numpy as jnp
        import numpy as np
        N, E, D = (2500, 40000, 256)
        H, C = (8, 32)
        n = x.shape[0]
        src, dst = (edge_index[0], edge_index[1])
        q = (x @ Wq + bq).reshape(n, H, C)
        k = (x @ Wk + bk).reshape(n, H, C)
        v = (x @ Wv + bv).reshape(n, H, C)
        e = (edge_attr @ We).reshape(-1, H, C)
        kj = k[src] + e
        alpha = jnp.einsum('ehc,ehc->eh', q[dst], kj) / jnp.sqrt(jnp.float32(C))
        amax = jax.ops.segment_max(alpha, dst, num_segments=n)
        ea = jnp.exp(alpha - amax[dst])
        denom = jax.ops.segment_sum(ea, dst, num_segments=n)
        alpha = ea / (denom[dst] + 1e-16)
        msg = (v[src] + e) * alpha[:, :, None]
        out = jax.ops.segment_sum(msg, dst, num_segments=n)
        out = out.reshape(n, H * C) + (x @ Ws + bs)
        return out

    def _L0_ffn_ref(x, Wg, bg, bias, W1, b1, W2, b2):
        import jax, jax.numpy as jnp
        import numpy as np
        D_MODEL = 256
        EXPERT_DIM = 512
        NUM_EXPERTS = 8
        TOP_K = 2
        SEQ_LEN = 256
        BATCH = 2
        x_flat = x.reshape(-1, D_MODEL)
        gate_logits = x_flat @ Wg + bg + bias
        topk_vals, topk_idx = jax.lax.top_k(gate_logits, TOP_K)
        topk_w = jax.nn.softmax(topk_vals, axis=-1)
        combine = (jax.nn.one_hot(topk_idx, NUM_EXPERTS, dtype=x.dtype) * topk_w[..., None]).sum(axis=1)
        h = jax.nn.relu(jnp.einsum('td,edh->teh', x_flat, W1) + b1)
        y = jnp.einsum('teh,ehd->ted', h, W2) + b2
        out = jnp.einsum('ted,te->td', y, combine)
        return out.reshape(x.shape)
    edge_index = jnp.stack([src, dst])
    x = x + _L0_gnn_ref(_layernorm(x, axis=-1), edge_index, edge_attr_256, L0_gnn_Wq, L0_gnn_bq, L0_gnn_Wk, L0_gnn_bk, L0_gnn_Wv, L0_gnn_bv, L0_gnn_We, L0_gnn_Ws, L0_gnn_bs)
    x = x + _L0_ffn_ref(_layernorm(x, axis=-1)[None], L0_ffn_Wg, L0_ffn_bg, L0_ffn_bias, L0_ffn_W1, L0_ffn_b1, L0_ffn_W2, L0_ffn_b2)[0]
    return x

_drawn_inputs = setup_inputs


def setup_inputs(seed=0):
    import zlib

    import numpy as np

    out = dict(_drawn_inputs(seed))
    spreads = {'L0_gnn_bq': (0.0, 0.1),
     'L0_gnn_bk': (0.0, 2.0),
     'L0_gnn_bv': (0.0, 0.1),
     'L0_gnn_bs': (0.0, 0.1),
     'L0_ffn_bias': (0.0, 0.27)}
    factors = {'L0_ffn_bg': 6.558, 'L0_ffn_b1': 21.366, 'L0_ffn_b2': 6.105}
    for name, (base, spread) in spreads.items():
        noise = np.random.default_rng([zlib.crc32(name.encode()), seed]).standard_normal(out[name].shape)
        drawn = base * np.exp(spread * noise) if base else spread * noise
        out[name] = jnp.asarray(drawn.astype(out[name].dtype))
    for name, factor in factors.items():
        out[name] = (out[name] * factor).astype(out[name].dtype)
    return out
```

```python
from contextlib import ExitStack

import concourse.bass as bass
from concourse import mybir

F32 = mybir.dt.float32
I32 = mybir.dt.int32
ALU = mybir.AluOpType
ACT = mybir.ActivationFunctionType
AX_X = mybir.AxisListType.X

P = 128
H = 8
CH = 16
BIG = 1.0e30
PAD_DST = 1 << 20
LN_EPS = 1e-5
N_KV = 4
N_A = 4
N_W = 4
TOP = 2


def ceil_div(a, b):
    return -(-a // b)


def gnn_ffn(nc, x, src, dst, edge_attr, Wq, bq, Wk, bk, Wv, bv, We, Ws, bs, Wg, bg, gbias, W1, b1, W2, b2, out):
    N, D = x.shape
    E = edge_attr.shape[0]
    C = D // H
    KD = D // P
    NT = ceil_div(N, P)
    ET = ceil_div(E, P)
    NTAIL = N - (NT - 1) * P
    ETAIL = E - (ET - 1) * P
    NR = NT * P
    NCH = ceil_div(NT + ET - 1, CH)
    NCH += 1 - NCH % 2
    IT = NCH * CH
    IB = ceil_div(IT, P)
    RB = ceil_div(ET, P)
    SCALE = float(C) ** -0.5
    CP = C + 1
    UW = H * CP
    NE, _, F = W1.shape
    KF = F // P
    NB = (NR * TOP + NE * (P - 1)) // P
    assert D == 2 * P and H * C == D and 0 < ETAIL < P and NT < P

    with ExitStack() as ctx:
        def sb(name, shape, dt=F32, c=ctx):
            return c.enter_context(nc.sbuf_tensor(name, shape, dt))

        def sem(name, c=ctx):
            return c.enter_context(nc.semaphore(name))

        def counters(c, **credits):
            sems = {n: sem(n, c) for n in credits}

            def at(name, i):
                return i + (credits[name] + 1)

            def grant(eng, *names):
                for n in names:
                    eng.sem_inc(sems[n], credits[n])

            return sems, at, grant

        def dram(name, shape, dt=F32):
            return nc.dram_tensor(name, shape, dt, kind="Internal").ap()

        src_rows = dram("src_rows", (ET, P), I32)
        sel_rows = dram("sel_rows", (ET, P), I32)
        run_rows = dram("run_rows", (ET, P), I32)
        run_table = dram("run_table", (IT, H, P))
        kv_table = dram("kv_table", (NR, 2 * D))
        skip_table = dram("skip_table", (NR, D))
        sorted_x = dram("sorted_x", (NB * P, D))
        sorted_y = dram("sorted_y", (NB * P, D))

        ident = sb("ident", [P, P])
        ones = sb("ones", [P, P])
        iota_free = sb("iota_free", [P, P])
        iota_part = sb("iota_part", [P, 1])
        src_idx = sb("src_idx", [P, IT], I32)
        dst_loc = sb("dst_loc", [P, IT])
        mask = sb("mask", [P, IT])
        item_node_tile = sb("item_node_tile", [1, IT], I32)
        item_row = sb("item_row", [1, IT], I32)
        chunk_tile = sb("chunk_tile", [P, NCH])

        with ExitStack() as c1:
            def sb1(name, shape, dt=F32):
                return sb(name, shape, dt, c1)

            def ps1(name, shape):
                return c1.enter_context(nc.psum_tensor(name, shape, F32))

            dst_sb = sb1("dst_sb", [P, RB, P], I32)
            lasts = sb1("lasts", [P, RB])
            thr_i = sb1("thr_i", [P, NT], I32)
            thr = sb1("thr", [P, NT])
            below = sb1("below", [P, NT, RB])
            below_n = sb1("below_n", [P, NT])
            step_at = sb1("step_at", [NT, 1])
            ii_i = sb1("ii_i", [P, IT], I32)
            ii = sb1("ii", [P, IT])
            ip_i = sb1("ip_i", [P, IB], I32)
            ip = sb1("ip", [P, IB])
            if_i = sb1("if_i", [P, P], I32)
            pp_i = sb1("pp_i", [P, 1], I32)
            stepped = sb1("stepped", [NT, IT])
            node_tile_rep = sb1("node_tile_rep", [P, IT])
            t_rep = sb1("t_rep", [P, IT])
            r_rep = sb1("r_rep", [P, IT])
            t_item = sb1("t_item", [P, IB])
            t_idx = sb1("t_idx", [P, IB], I32)
            pad_dst = sb1("pad_dst", [1, P], I32)
            pad_src = sb1("pad_src", [1, P], I32)
            pad_run = sb1("pad_run", [1, P], I32)
            last_dst = sb1("last_dst", [1, 1], I32)
            src_g = sb1("src_g", [P, IB, P], I32)
            sel_g = sb1("sel_g", [P, IB, P], I32)
            run_g = sb1("run_g", [P, IB, P], I32)
            src_f = sb1("src_f", [P, IB, P])
            sel_f = sb1("sel_f", [P, IB, P])
            run_f = sb1("run_f", [P, IB, P])
            m_lo = sb1("m_lo", [P, IT])
            m_hi = sb1("m_hi", [P, IT])
            ps_rep = [ps1(f"ps_rep{i}", [P, 512]) for i in range(2)]
            ps_small = ps1("ps_small", [P, 512])
            ps_src = ps1("ps_src", [P, 512])
            ps_sel = ps1("ps_sel", [P, 512])

            dst_loaded = sem("dst_loaded", c1)
            rows_written = sem("rows_written", c1)
            pads_set = sem("pads_set", c1)
            last_loaded = sem("last_loaded", c1)
            iotas = sem("iotas", c1)
            dve_step = sem("dve_step", c1)
            below_ready = sem("below_ready", c1)
            step_summed = sem("step_summed", c1)
            stepped_ready = sem("stepped_ready", c1)
            rep_ready = sem("rep_ready", c1)
            item_ready = sem("item_ready", c1)
            t_idx_ready = sem("t_idx_ready", c1)
            gathered = [sem(f"gathered_{n}", c1) for n in ("run", "src", "sel")]
            floats_ready = sem("floats_ready", c1)
            turned = sem("turned", c1)
            turned_copied = sem("turned_copied", c1)
            run_written = sem("run_written", c1)
            full = ET - 1
            pad = P - ETAIL
            IH = IT // 2
            assert IH <= 512

            def rows_in(b, total=IT):
                return min(P, total - b * P)

            block = c1.enter_context(nc.Block())

            @block.sync
            def _(sp):
                with nc.allow_non_contiguous_dma(reason="the short tail row of the edge lists"):
                    nb = full // P
                    if nb:
                        sp.dma_start(dst_sb[:, 0:nb, :], dst[0:nb * P * P].rearrange("(b p e) -> p b e", p=P, e=P)).then_inc(dst_loaded, 16)
                    sp.dma_start(dst_sb[0:full - nb * P, nb, :],
                                 dst[nb * P * P:full * P].rearrange("(p e) -> p e", e=P)).then_inc(dst_loaded, 16)
                    sp.dma_start(last_dst[:, :], dst[full * P - 1:full * P].rearrange("(t e) -> t e", t=1)).then_inc(last_loaded, 16)
                    sp.wait_ge(pads_set, 3)
                    for rows, edges in ((src_rows, src), (sel_rows, dst), (run_rows, dst)):
                        sp.dma_start(rows[0:full, :], edges[0:full * P].rearrange("(t e) -> t e", e=P)).then_inc(rows_written, 16)
                        sp.dma_start(rows[full:ET, pad:P], edges[full * P:E].rearrange("(t e) -> t e", t=1)).then_inc(rows_written, 16)
                    sp.dma_start(src_rows[full:ET, 0:pad], pad_src[0:1, 0:pad]).then_inc(rows_written, 16)
                    sp.dma_start(sel_rows[full:ET, 0:pad], pad_dst[0:1, 0:pad]).then_inc(rows_written, 16)
                    sp.dma_start(run_rows[full:ET, 0:pad],
                                 pad_run[0:1, 0:pad]).then_inc(rows_written, 16)
                    sp.wait_ge(floats_ready, 3)
                    for b in range(IB):
                        n = rows_in(b)
                        sp.dma_start(run_table[b * P:b * P + n, :, :],
                                     run_f[0:n, b:b + 1, :].to_broadcast([n, H, P])).then_inc(run_written, 16)
                    sp.wait_ge(run_written, 16 * IB)

            @block.gpsimd
            def _(pool):
                nc.gpsimd.memset(pad_src[:, :], 0).then_inc(pads_set, 1)
                nc.gpsimd.memset(pad_dst[:, :], PAD_DST).then_inc(pads_set, 1)
                pool.wait_ge(last_loaded, 16)
                nc.gpsimd.tensor_copy(pad_run[:, :], last_dst[:, :].to_broadcast([1, P])).then_inc(pads_set, 1)
                nc.gpsimd.iota(if_i[:, :], [[1, P]], base=0, channel_multiplier=0).then_inc(iotas, 1)
                nc.gpsimd.iota(pp_i[:, :], [[1, 1]], base=0, channel_multiplier=1).then_inc(iotas, 1)
                nc.gpsimd.iota(thr_i[:, :], [[P, NT]], base=P, channel_multiplier=0).then_inc(iotas, 1)
                nc.gpsimd.iota(ii_i[:, :], [[1, IT]], base=0, channel_multiplier=0).then_inc(iotas, 1)
                nc.gpsimd.iota(ip_i[:, :], [[P, IB]], base=0, channel_multiplier=1).then_inc(iotas, 1)
                pool.wait_ge(rows_written, 16 * 9)
                pool.wait_ge(t_idx_ready, 2)
                for rows, got, got_sem in ((run_rows, run_g, gathered[0]), (src_rows, src_g, gathered[1]),
                                           (sel_rows, sel_g, gathered[2])):
                    for b in range(IB):
                        n = rows_in(b)
                        nc.gpsimd.indirect_dma_start(
                            out=got[0:n, b, :], out_offset=None, in_=rows,
                            in_offset=bass.IndirectOffsetOnAxis(ap=t_idx[0:n, b:b + 1], axis=0)).then_inc(got_sem, 16)

            @block.vector
            def _(dve):
                count = [0]

                def then(ins):
                    count[0] += 1
                    ins.then_inc(dve_step, 1)
                    dve.wait_ge(dve_step, count[0])

                v = nc.vector
                v.memset(ones[:, :], 1.0)
                then(v.memset(lasts[:, :], 1.0e9))
                dve.wait_ge(iotas, 5)
                v.tensor_copy(iota_free[:, :], if_i[:, :])
                v.tensor_copy(thr[:, :], thr_i[:, :])
                v.tensor_copy(ii[:, :], ii_i[:, :])
                v.tensor_copy(ip[:, :], ip_i[:, :])
                then(v.tensor_copy(iota_part[:, :], pp_i[:, :]))
                v.tensor_scalar(ident[:, :], iota_free[:, :], iota_part[:, 0:1], None, ALU.is_equal)
                nb = full // P
                dve.wait_ge(dst_loaded, 16 * (2 if nb else 1))
                if nb:
                    v.tensor_copy(lasts[:, 0:nb], dst_sb[:, 0:nb, P - 1])
                then(v.tensor_copy(lasts[0:full - nb * P, nb:nb + 1], dst_sb[0:full - nb * P, nb, P - 1:P]))
                then(v.tensor_tensor(below[:, :, :], lasts[:, None, :].to_broadcast([P, NT, RB]),
                                     thr[:, :, None].to_broadcast([P, NT, RB]), ALU.is_lt))
                v.tensor_reduce(below_n[:, :], below[:, :, :], AX_X, ALU.add).then_inc(below_ready, 1)
                dve.wait_ge(step_summed, 1)
                then(v.tensor_scalar(step_at[:, :], ps_small[0:NT, 0:1], float(ET - 1), iota_part[0:NT, 0:1], ALU.min, ALU.add))
                v.tensor_scalar(stepped[:, :], ii[0:NT, :], step_at[:, 0:1], None, ALU.is_gt).then_inc(stepped_ready, 1)
                dve.wait_ge(item_ready, 1)
                nf = IT // P
                if nf:
                    v.tensor_tensor(t_item[:, 0:nf], ip[:, 0:nf], ps_small[:, 8:8 + nf], ALU.subtract)
                if IB > nf:
                    n = rows_in(nf)
                    v.tensor_tensor(t_item[0:n, nf:IB], ip[0:n, nf:IB], ps_small[0:n, 8 + nf:8 + IB], ALU.subtract)
                then(v.memset(dst_sb[:, 0, 0:1], 0))
                if nf:
                    v.tensor_scalar(t_idx[:, 0:nf], t_item[:, 0:nf], float(ET - 1), None, ALU.min).then_inc(t_idx_ready, 1)
                else:
                    dve.sem_inc(t_idx_ready, 1)
                if IB > nf:
                    v.tensor_scalar(t_idx[0:n, nf:IB], t_item[0:n, nf:IB], float(ET - 1), None, ALU.min).then_inc(t_idx_ready, 1)
                else:
                    dve.sem_inc(t_idx_ready, 1)
                dve.wait_ge(rep_ready, 1)
                v.tensor_copy(node_tile_rep[:, 0:IH], ps_rep[0][:, 0:IH])
                then(v.tensor_copy(node_tile_rep[:, IH:IT], ps_rep[1][:, 0:IH]))
                v.tensor_copy(item_node_tile[:, :], node_tile_rep[0:1, :])
                v.tensor_copy(chunk_tile[:, :], node_tile_rep[:, 0:IT:CH])
                then(v.tensor_tensor(t_rep[:, :], ii[:, :], node_tile_rep[:, :], ALU.subtract))
                then(v.tensor_scalar(r_rep[:, :], t_rep[:, :], float(P), float(E - P), ALU.mult, ALU.min))
                v.tensor_copy(item_row[:, :], r_rep[0:1, :])
                for k, (got, flt) in enumerate(((run_g, run_f), (src_g, src_f), (sel_g, sel_f))):
                    dve.wait_ge(gathered[k], 16 * IB)
                    if nf:
                        v.tensor_copy(flt[:, 0:nf, :], got[:, 0:nf, :]).then_inc(floats_ready, 1)
                    if IB > nf:
                        v.tensor_copy(flt[0:n, nf:IB, :], got[0:n, nf:IB, :]).then_inc(floats_ready, 1)
                for b in range(IB):
                    n = rows_in(b)
                    dve.wait_ge(turned, b + 1)
                    v.tensor_copy(src_idx[:, b * P:b * P + n], ps_src[:, 0:n])
                    v.scalar_tensor_tensor(out=dst_loc[:, b * P:b * P + n], in0=node_tile_rep[:, b * P:b * P + n],
                                           scalar=-float(P), in1=ps_sel[:, 0:n], op0=ALU.mult,
                                           op1=ALU.add).then_inc(turned_copied, 1)
                dve.wait_ge(turned_copied, IB)
                v.tensor_scalar(m_lo[:, :], dst_loc[:, :], 0.0, -BIG, ALU.is_lt, ALU.mult)
                then(v.tensor_scalar(m_hi[:, :], dst_loc[:, :], P - 0.5, -BIG, ALU.is_gt, ALU.mult))
                then(v.tensor_tensor(mask[:, :], m_lo[:, :], m_hi[:, :], ALU.add))

            nfl = 2 if IT % P and IT >= P else 1

            @block.tensor
            def _(pe):
                pe.wait_ge(below_ready, 1)
                nc.tensor.matmul(ps_small[0:NT, 0:1], below_n[:, :], ones[:, 0:1], start=True, stop=True).then_inc(step_summed, 1)
                pe.wait_ge(stepped_ready, 1)
                for b in range(IB):
                    n = rows_in(b)
                    last = nc.tensor.matmul(ps_small[0:n, 8 + b:9 + b], stepped[:, b * P:b * P + n], ones[0:NT, 0:1], start=True, stop=True)
                last.then_inc(item_ready, 1)
                for h in range(2):
                    last = nc.tensor.matmul(ps_rep[h][:, 0:IH], ones[0:NT, :], stepped[:, h * IH:(h + 1) * IH], start=True, stop=True)
                last.then_inc(rep_ready, 1)
                pe.wait_ge(floats_ready, 3 * nfl)
                for b in range(IB):
                    n = rows_in(b)
                    if b:
                        pe.wait_ge(turned_copied, b)
                    nc.tensor.transpose(ps_src[:, 0:n], src_f[0:n, b, :], ident[0:n, 0:n])
                    nc.tensor.transpose(ps_sel[:, 0:n], sel_f[0:n, b, :], ident[0:n, 0:n]).then_inc(turned, 1)

        c_keep = ctx.enter_context(ExitStack())
        assert NT * NE <= IT and TOP * NT <= IT and NB <= IT
        slot_i = src_idx[:, 0:TOP * NT].rearrange("p (k j) -> p k j", k=TOP)
        gate_w = dst_loc[:, 0:TOP * NT].rearrange("p (k j) -> p k j", k=TOP)
        logits = mask[:, 0:NT * NE].rearrange("p (j e) -> p j e", e=NE)
        block_expert = item_row[0:1, 0:NB]
        q_sb = sb("q_sb", [P, NT + 1, D], F32, c_keep)
        c_acc = c_keep.enter_context(ExitStack())
        acc = sb("acc", [P, NT + 1, UW], F32, c_acc)

        def flat(ap):
            return ap.rearrange("p j d -> p (j d)")

        with ExitStack() as c2:
            def sb2(name, shape, dt=F32):
                return sb(name, shape, dt, c2)

            def ps2(name, shape):
                return c2.enter_context(nc.psum_tensor(name, shape, F32))

            x_sb = sb2("x_sb", [P, NT, D])
            w4 = sb2("w4", [P, KD, 4 * D])
            b4 = sb2("b4", [P, 4 * D])
            stat = sb2("stat", [P, 6])
            mv = sb2("mv", [P, 2])
            vp = sb2("vp", [P, 1])
            sd = sb2("sd", [P, 1])
            r0 = sb2("r0", [P, 1])
            r1 = sb2("r1", [P, 1])
            r2 = sb2("r2", [P, 1])
            r3 = sb2("r3", [P, 1])
            rstd = sb2("rstd", [P, 1])
            xn = [sb2(f"xn{i}", [P, D]) for i in range(2)]
            xnT = [sb2(f"xnT{i}", [P, D]) for i in range(2)]
            kv_out = [sb2(f"kv_out{i}", [P, 2 * D]) for i in range(2)]
            skip_out = [sb2(f"skip_out{i}", [P, D]) for i in range(2)]
            ps_t = [ps2(f"ps_t{i}", [P, 512]) for i in range(2)]
            ps_p = [ps2(f"ps_p{i}", [P, 1024]) for i in range(2)]
            s, at, grant = counters(c2, loaded=0, ln_step=0, var_ready=0, sd_ready=0, xn_ready=0, xn_turned=2, xnT_ready=2,
                                    projected=2, q_out=2, kv_out_ready=2, skip_half=2, skip_out_ready=0, tail_zeroed=0,
                                    stored0=0, stored1=0, dve_pace=0)
            stored = [s["stored0"], s["stored1"]]
            block = c2.enter_context(nc.Block())

            def over_tiles(eng, emit):
                with eng.Fori(0, NT // 2) as g:
                    emit(g * 2, 0)
                    emit(g * 2 + 1, 1)
                if NT % 2:
                    emit(NT - 1, 0)

            @block.sync
            def _(sp):
                for i, w in enumerate((Wq, Wk, Wv, Ws)):
                    sp.dma_start(w4[:, :, i * D:(i + 1) * D], w.rearrange("(k p) n -> p k n", p=P)).then_inc(s["loaded"], 16)
                for i, b in enumerate((bq, bk, bv, bs)):
                    sp.dma_start(b4[:, i * D:(i + 1) * D],
                                 b.rearrange("(o n) -> o n", o=1).to_broadcast([P, D])).then_inc(s["loaded"], 16)
                sp.dma_start(x_sb[:, 0:NT - 1, :], x[0:(NT - 1) * P, :].rearrange("(j p) d -> p j d", p=P)).then_inc(s["loaded"], 16)
                sp.wait_ge(s["tail_zeroed"], 1)
                sp.dma_start(x_sb[0:NTAIL, NT - 1, :], x[(NT - 1) * P:N, :]).then_inc(s["loaded"], 16)

                def store(j, par):
                    sp.wait_ge(s["kv_out_ready"], at("kv_out_ready", j))
                    sp.dma_start(kv_table[bass.ds(j * P, P), :], kv_out[par][:, :]).then_inc(stored[par], 16)
                    sp.wait_ge(s["skip_out_ready"], at("skip_out_ready", j))
                    sp.dma_start(skip_table[bass.ds(j * P, P), :], skip_out[par][:, :]).then_inc(stored[par], 16)

                over_tiles(sp, store)
                sp.wait_ge(stored[0], 32 * ceil_div(NT, 2))
                sp.wait_ge(stored[1], 32 * (NT // 2))

            @block.scalar
            def _(act):
                grant(act, "xnT_ready")
                act_pace = s["dve_pace"]

                def tile(j, par):
                    act.wait_ge(s["var_ready"], at("var_ready", j))
                    act.sem_inc(act_pace, 1)
                    nc.scalar.activation(sd[:, :], vp[:, :], ACT.Sqrt).then_inc(s["sd_ready"], 1)
                    act.wait_ge(s["xn_turned"], at("xn_turned", j))
                    act.wait_ge(s["projected"], at("projected", j - 2))
                    nc.scalar.copy(xnT[par][:, :], ps_t[par][:, 0:D]).then_inc(s["xnT_ready"], 1)

                over_tiles(act, tile)

            @block.tensor
            def _(pe):
                grant(pe, "xn_turned", "projected")
                pe.wait_ge(s["loaded"], 16 * 10)

                def tile(j, par):
                    pe.wait_ge(s["xn_ready"], at("xn_ready", j))
                    pe.wait_ge(s["xnT_ready"], at("xnT_ready", j - 2))
                    for k in range(KD):
                        last = nc.tensor.transpose(ps_t[par][:, k * P:(k + 1) * P], xn[par][:, k * P:(k + 1) * P], ident[:, :])
                    last.then_inc(s["xn_turned"], 1)
                    pe.wait_ge(s["xnT_ready"], at("xnT_ready", j))
                    pe.wait_ge(s["q_out"], at("q_out", j - 2))
                    pe.wait_ge(s["kv_out_ready"], at("kv_out_ready", j - 2))
                    pe.wait_ge(s["skip_half"], at("skip_half", j - 2))
                    for h in range(2):
                        for k in range(KD):
                            last = nc.tensor.matmul(ps_p[par][:, h * 512:(h + 1) * 512], xnT[par][:, k * P:(k + 1) * P],
                                                    w4[:, k, h * 512:(h + 1) * 512], start=(k == 0), stop=(k == KD - 1))
                    last.then_inc(s["projected"], 1)

                over_tiles(pe, tile)

            LN_STEPS = 7

            @block.vector
            def _(dve):
                v = nc.vector
                grant(dve, "q_out", "kv_out_ready", "skip_half")
                v.memset(x_sb[:, NT - 1, :], 0.0).then_inc(s["tail_zeroed"], 1)
                v.memset(q_sb[:, NT, :], 0.0)
                dve.wait_ge(s["loaded"], 16 * 10)

                def layernorm(j, par):
                    n = [0]

                    def then(ins):
                        n[0] += 1
                        ins.then_inc(s["ln_step"], 1)
                        dve.wait_ge(s["ln_step"], j * LN_STEPS + n[0])
                        dve.sem_inc(s["dve_pace"], 1)

                    xj = flat(x_sb[:, :, :])[:, bass.ds(j * D, D)]
                    then(v.bn_stats(stat[:, :], xj))
                    then(v.bn_aggr(mv[:, :], stat[:, :]))
                    v.tensor_scalar(vp[:, :], mv[:, 1:2], LN_EPS, None, ALU.add).then_inc(s["var_ready"], 1)
                    dve.wait_ge(s["sd_ready"], at("sd_ready", j))
                    then(v.reciprocal(r0[:, :], sd[:, :]))
                    then(v.tensor_tensor(r1[:, :], r0[:, :], r0[:, :], ALU.mult))
                    then(v.tensor_tensor(r2[:, :], r1[:, :], vp[:, :], ALU.mult))
                    then(v.tensor_scalar(r3[:, :], r2[:, :], -0.5, 1.5, ALU.mult, ALU.add))
                    then(v.tensor_tensor(rstd[:, :], r0[:, :], r3[:, :], ALU.mult))
                    assert n[0] == LN_STEPS
                    dve.wait_ge(s["xn_turned"], at("xn_turned", j - 2))
                    v.tensor_scalar(xn[par][:, :], xj, mv[:, 0:1], rstd[:, 0:1], ALU.subtract, ALU.mult).then_inc(s["xn_ready"], 1)

                def evacuate(j, par, first=False):
                    if not first:
                        dve.wait_ge(stored[par], (j - par) * 16)
                    dve.wait_ge(s["projected"], at("projected", j))
                    v.tensor_tensor(kv_out[par][:, :], ps_p[par][:, D:3 * D], b4[:, D:3 * D], ALU.add).then_inc(s["kv_out_ready"], 1)
                    v.tensor_tensor(skip_out[par][:, :], ps_p[par][:, 3 * D:4 * D], b4[:, 3 * D:4 * D], ALU.add).then_inc(s["skip_half"], 1)
                    v.tensor_tensor(flat(q_sb[:, :, :])[:, bass.ds(j * D, D)], ps_p[par][:, 0:D], b4[:, 0:D], ALU.add).then_inc(s["q_out"], 1)
                    dve.wait_ge(s["skip_half"], at("skip_half", j))
                    v.tensor_tensor(skip_out[par][:, :], skip_out[par][:, :], flat(x_sb[:, :, :])[:, bass.ds(j * D, D)],
                                    ALU.add).then_inc(s["skip_out_ready"], 1)

                layernorm(0, 0)
                layernorm(1, 1)
                evacuate(0, 0, True)
                layernorm(2, 0)
                evacuate(1, 1, True)
                pairs = (NT - 3) // 2
                with dve.Fori(0, pairs) as g:
                    layernorm(g * 2 + 3, 1)
                    evacuate(g * 2 + 2, 0)
                    layernorm(g * 2 + 4, 0)
                    evacuate(g * 2 + 3, 1)
                for j in range(2 * pairs + 2, NT):
                    if j + 1 < NT:
                        layernorm(j + 1, (j + 1) % 2)
                    evacuate(j, j % 2)

        with ExitStack() as c3:
            def sb3(name, shape, dt=F32):
                return sb(name, shape, dt, c3)

            def ps3(name, shape):
                return c3.enter_context(nc.psum_tensor(name, shape, F32))

            KW = 2 * P + H
            we_sb = sb3("we_sb", [P, KD, D])
            a_ring = sb3("a_ring", [P, N_A, D])
            kv_ring = sb3("kv_ring", [P, N_KV, 2 * D])
            aT = [sb3(f"aT{i}", [P, D + P]) for i in range(2)]
            kq = [sb3(f"kq{i}", [P, D]) for i in range(2)]
            kqq = [sb3(f"kqq{i}", [P, D]) for i in range(2)]
            ve = sb3("ve", [P, 2, CH, UW])
            sel = sb3("sel", [P, 2, CH, P])
            alpha = [sb3(f"alpha{i}", [P, P]) for i in range(2)]
            w_ring = sb3("w_ring", [P, N_W, UW])
            idx_c = sb3("idx_c", [P, 2, CH], I32)
            loc_c = sb3("loc_c", [P, 2, CH])
            run_c = [sb3(f"run_c{i}", [P, P]) for i in range(2)]
            ea = [sb3(f"ea{i}", [P, P]) for i in range(2)]
            head_i = sb3("head_i", [P, 1], I32)
            head_m = sb3("head_m", [P, 1], I32)
            pp8_i = sb3("pp8_i", [P, 1], I32)
            head = sb3("head", [P, 1])
            part8 = sb3("part8", [P, 1])
            am = sb3("am", [P, P])
            resets = sb3("resets", [P, P + 1])
            off_first = sb3("off_first", [P, P])
            off_last = sb3("off_last", [P, P])
            key_f = sb3("key_f", [P, 1])
            key_l = sb3("key_l", [P, 1])
            key_prev = sb3("key_prev", [P, 1])
            max_prev = sb3("max_prev", [P, 1])
            diag_k = sb3("diag_k", [P, KW])
            diag_r = sb3("diag_r", [P, KW])
            diag_f = sb3("diag_f", [P, H])
            not_f = sb3("not_f", [P, KW])
            not_l = sb3("not_l", [P, KW])
            scan_f = sb3("scan_f", [P, P])
            scan_b = sb3("scan_b", [P, P])
            max_f = sb3("max_f", [P, 1])
            max_l = sb3("max_l", [P, 1])
            shifted = am
            keys2 = sb3("keys2", [P, 2])
            same = sb3("same", [P, 1])
            node_key = sb3("node_key", [P, 1])
            pick = sb3("pick", [P, 1])
            unpick = sb3("unpick", [P, 1])
            carry = sb3("carry", [P, H])
            carry_d = sb3("carry_d", [P, H])
            carry_e = sb3("carry_e", [P, H])
            factor = sb3("factor", [P, H])
            ps_t = [ps3(f"ps_t3{i}", [P, 512]) for i in range(2)]
            ps_e = [ps3(f"ps_e{i}", [P, 512]) for i in range(2)]
            ps_u = [ps3(f"ps_u{i}", [P, 512]) for i in range(2)]
            ps_ak = ps3("ps_ak", [P, 512])
            ps_rx = ps3("ps_rx", [P, 512])
            ps_a, ps_k = ps_ak[:, 0:P], ps_ak[:, P:P + KW]
            ps_r, ps_x, ps_f = ps_rx[:, 0:KW], ps_rx[:, KW:KW + P], ps_rx[:, KW + P:KW + P + H]

            s, at, grant = counters(c3, a_turned=N_A, aT_ready=2, e_ready=2, ke_added=N_KV, ve_added=N_KV, kq_ready=2,
                                    alpha_ready=0, sel_ready=0, weighted=2 * CH, summed=2 * CH, acc_added=2,
                                    idx_copied=0, loc_copied=0, am_ready=0, am_turned=0, keyed=0, r_ready=0,
                                    max_spread=0, f_ready=0, shifted_ready=0, shifted_turned=1, ea_ready=1,
                                    carry_ready=0, carry_exp=0, softmax_done=2,
                                    const_loaded=0, iotas=0, setup=0, sm_step=0,
                                    act_pace=0, pool_pace=0)
            a_loaded = [sem(f"a_loaded{i}", c3) for i in range(N_A)]
            kv_loaded = [sem(f"kv_loaded{i}", c3) for i in range(N_KV)]
            run_loaded = [sem(f"run_loaded{i}", c3) for i in range(2)]
            block = c3.enter_context(nc.Block())

            FIRST_SUM = 5

            def beside(i):
                if i < 4:
                    return [("softmax", i)]
                if i < FIRST_SUM:
                    return []
                n = CH - FIRST_SUM
                summed_at = [range((k - FIRST_SUM) * CH // n, (k - FIRST_SUM + 1) * CH // n) for k in range(CH)]
                out = [("softmax", 4)] if i == FIRST_SUM else []
                out += [("weigh", m) for m in summed_at[i]]
                if i > FIRST_SUM:
                    out += [("add", m) for m in summed_at[i - 1]]
                if i == CH - 1:
                    out += [("add", m) for m in summed_at[i]]
                return out

            def plan(scores, rest, lag=0):
                out = []
                for i in range(CH + lag):
                    if scores and i < CH:
                        out.append(("score", i))
                    if rest and i >= lag:
                        out += beside(i - lag)
                return out

            def over_chunks(eng, emit, lag=0):
                emit(0, 0, plan(True, False))
                with eng.Fori(0, (NCH - 1) // 2) as g:
                    emit(g * 2 + 1, 1, plan(True, True, lag))
                    emit(g * 2 + 2, 0, plan(True, True, lag))
                emit(NCH, NCH % 2, plan(False, True))

            @block.sync
            def _(sp):
                sp.dma_start(we_sb[:, :, :], We.rearrange("(k p) n -> p k n", p=P)).then_inc(s["const_loaded"], 16)

                def load(c, par, steps):
                    for kind, i in steps:
                        if kind != "score":
                            continue
                        if i == 0:
                            sp.wait_ge(s["softmax_done"], at("softmax_done", c - 2))
                            sp.dma_start(run_c[par][:, :],
                                         run_table[bass.ds(c * CH, CH), :, :].rearrange("i h e -> (i h) e")).then_inc(run_loaded[par], 16)
                        row = sp.value_load(item_row[0:1, bass.ds(c * CH + i, 1)], min_val=0, max_val=E - P)
                        sp.wait_ge(s["a_turned"], at("a_turned", c * CH + (i - N_A)))
                        sp.dma_start(a_ring[:, i % N_A, :], edge_attr[bass.ds(row, P), :]).then_inc(a_loaded[i % N_A], 16)

                over_chunks(sp, load)

            @block.gpsimd
            def _(pool):
                g = nc.gpsimd
                g.iota(pp8_i[:, :], [[1, 1]], base=0, channel_multiplier=H).then_inc(s["iotas"], 1)
                g.iota(head_i[:, :], [[1, 1]], base=0, channel_multiplier=1).then_inc(s["iotas"], 1)

                def gather(c, par, steps):
                    for kind, i in steps:
                        if kind != "score":
                            continue
                        if i == 0:
                            g.tensor_copy(idx_c[:, par, :], src_idx[:, bass.ds(c * CH, CH)]).then_inc(s["idx_copied"], 1)
                            g.tensor_copy(loc_c[:, par, :], dst_loc[:, bass.ds(c * CH, CH)]).then_inc(s["loc_copied"], 1)
                            pool.wait_ge(s["idx_copied"], at("idx_copied", c))
                            pool.sem_inc(s["pool_pace"], 1)
                            pool.wait_ge(s["loc_copied"], at("loc_copied", c))
                            pool.sem_inc(s["pool_pace"], 1)
                        pool.wait_ge(s["summed"], at("summed", c * CH + (i - 2 * CH)))
                        pool.sem_inc(s["pool_pace"], 1)
                        g.tensor_scalar(sel[:, par, i, :], iota_free[:, :], loc_c[:, par, i:i + 1], None,
                                        ALU.is_equal).then_inc(s["sel_ready"], 1)
                        pool.wait_ge(s["ve_added"], at("ve_added", c * CH + (i - N_KV)))
                        pool.sem_inc(s["pool_pace"], 1)
                        pool.wait_ge(s["ke_added"], at("ke_added", c * CH + (i - N_KV)))
                        pool.sem_inc(s["pool_pace"], 1)
                        g.indirect_dma_start(out=kv_ring[:, i % N_KV, :], out_offset=None, in_=kv_table,
                                             in_offset=bass.IndirectOffsetOnAxis(ap=idx_c[:, par, i:i + 1], axis=0)
                                             ).then_inc(kv_loaded[i % N_KV], 16)

                over_chunks(pool, gather)

            @block.scalar
            def _(act):
                grant(act, "aT_ready", "ea_ready")

                def emit(c, par, steps):
                    for kind, i in steps:
                        if kind == "score":
                            act.wait_ge(s["a_turned"], at("a_turned", c * CH + i))
                            act.wait_ge(s["e_ready"], at("e_ready", c * CH + (i - 2)))
                            nc.scalar.copy(aT[i % 2][:, :], ps_t[i % 2][:, 0:D + P]).then_inc(s["aT_ready"], 1)
                        elif kind == "softmax" and i == 4:
                            act.wait_ge(s["weighted"], at("weighted", (c - 2) * CH - 1))
                            act.sem_inc(s["act_pace"], 1)
                            act.wait_ge(s["shifted_turned"], at("shifted_turned", c - 1))
                            act.sem_inc(s["act_pace"], 1)
                            nc.scalar.activation(ea[1 - par][:, :], ps_x, ACT.Exp).then_inc(s["ea_ready"], 1)
                            act.wait_ge(s["carry_ready"], at("carry_ready", c - 1))
                            act.sem_inc(s["act_pace"], 1)
                            nc.scalar.activation(carry_e[:, :], carry_d[:, :], ACT.Exp).then_inc(s["carry_exp"], 1)

                over_chunks(act, emit)

            @block.tensor
            def _(pe):
                t = nc.tensor
                grant(pe, "a_turned", "e_ready", "summed", "shifted_turned")
                pe.wait_ge(s["const_loaded"], 16)

                def turn(c, par, i):
                    pe.wait_ge(a_loaded[i % N_A], c * (16 * CH // N_A) + 16 * (i // N_A + 1))
                    pe.wait_ge(s["sel_ready"], at("sel_ready", c * CH + i))
                    pe.wait_ge(s["aT_ready"], at("aT_ready", c * CH + (i - 2)))
                    for k in range(KD):
                        t.transpose(ps_t[i % 2][:, k * P:(k + 1) * P], a_ring[:, i % N_A, k * P:(k + 1) * P], ident[:, :])
                    t.transpose(ps_t[i % 2][:, D:D + P], sel[:, par, i, :], ident[:, :]).then_inc(s["a_turned"], 1)

                def project(c, i):
                    n = pe.value_load(item_node_tile[0:1, bass.ds(c * CH + i, 1)], min_val=0, max_val=NT)
                    pe.wait_ge(s["aT_ready"], at("aT_ready", c * CH + i))
                    pe.wait_ge(s["ve_added"], at("ve_added", c * CH + (i - 2)))
                    pe.wait_ge(s["kq_ready"], at("kq_ready", c * CH + (i - 2)))
                    for k in range(KD):
                        t.matmul(ps_e[i % 2][:, 0:D], aT[i % 2][:, k * P:(k + 1) * P], we_sb[:, k, :], start=(k == 0), stop=(k == KD - 1))
                    t.matmul(ps_e[i % 2][:, D:2 * D], aT[i % 2][:, D:D + P], flat(q_sb[:, :, :])[:, bass.ds(n * D, D)],
                             start=True, stop=True).then_inc(s["e_ready"], 1)

                def emit(c, par, steps):
                    for kind, i in steps:
                        if kind == "score":
                            if i == 0:
                                turn(c, par, 0)
                            if i + 1 < CH:
                                turn(c, par, i + 1)
                            project(c, i)
                        elif kind == "softmax" and i == 0:
                            pe.wait_ge(s["keyed"], at("keyed", c - 1))
                            t.matmul(ps_k, ones[:, :], diag_k[:, :], start=True, stop=True)
                            pe.wait_ge(s["am_ready"], at("am_ready", c - 1))
                            t.transpose(ps_a, am[:, :], ident[:, :]).then_inc(s["am_turned"], 1)
                        elif kind == "softmax" and i == 1:
                            pe.wait_ge(s["r_ready"], at("r_ready", c - 1))
                            t.matmul(ps_r, ones[:, :], diag_r[:, :], start=True, stop=True).then_inc(s["max_spread"], 1)
                        elif kind == "softmax" and i == 3:
                            pe.wait_ge(s["f_ready"], at("f_ready", c - 1))
                            t.matmul(ps_f, ones[:, :], diag_f[:, :], start=True, stop=True)
                            pe.wait_ge(s["shifted_ready"], at("shifted_ready", c - 1))
                            t.transpose(ps_x, shifted[:, :], ident[:, :]).then_inc(s["shifted_turned"], 1)
                        elif kind == "weigh":
                            m = (c - 1) * CH + i
                            pe.wait_ge(s["weighted"], at("weighted", m))
                            pe.wait_ge(s["acc_added"], at("acc_added", m - 2))
                            t.matmul(ps_u[i % 2][:, 0:UW], sel[:, 1 - par, i, :], w_ring[:, i % N_W, :],
                                     start=True, stop=True).then_inc(s["summed"], 1)

                over_chunks(pe, emit, lag=1)

            @block.vector
            def _(dve):
                v = nc.vector
                grant(dve, "ke_added", "ve_added", "kq_ready", "weighted", "acc_added", "softmax_done")
                v.memset(acc[:, :, :], 0.0).then_inc(s["setup"], 1)
                v.memset(ve[:, :, :, :], 1.0).then_inc(s["setup"], 1)
                v.memset(resets[:, :], 0.0).then_inc(s["setup"], 1)
                v.memset(max_prev[:, :], -BIG).then_inc(s["setup"], 1)
                v.memset(key_prev[:, :], -1.0).then_inc(s["setup"], 1)
                dve.wait_ge(s["iotas"], 2)
                v.tensor_scalar(head_m[:, :], head_i[:, :], H - 1, None, ALU.bitwise_and).then_inc(s["setup"], 1)
                v.tensor_copy(part8[:, :], pp8_i[:, :]).then_inc(s["setup"], 1)
                dve.wait_ge(s["setup"], 7)
                v.tensor_copy(head[:, :], head_m[:, :]).then_inc(s["setup"], 1)
                dve.wait_ge(s["setup"], 8)

                def by_head(ap, width):
                    return ap.rearrange("p (h c) -> p h c", c=width)

                def reduce(c, par, i):
                    dve.wait_ge(s["kq_ready"], at("kq_ready", c * CH + i))
                    v.tensor_reduce(alpha[par][:, i * H:(i + 1) * H], by_head(kqq[i % 2][:, :], C), AX_X,
                                    ALU.add).then_inc(s["alpha_ready"], 1)

                def score(c, par, i):
                    e = ps_e[i % 2][:, 0:D]
                    kv = kv_ring[:, i % N_KV, :]
                    dve.wait_ge(s["e_ready"], at("e_ready", c * CH + i))
                    dve.wait_ge(kv_loaded[i % N_KV], c * (16 * CH // N_KV) + 16 * (i // N_KV + 1))
                    v.tensor_tensor(kq[i % 2][:, :], kv[:, 0:D], e, ALU.add).then_inc(s["ke_added"], 1)
                    v.tensor_tensor(by_head(ve[:, par, i, :], CP)[:, :, 0:C], by_head(kv[:, D:2 * D], C), by_head(e, C),
                                    ALU.add).then_inc(s["ve_added"], 1)
                    if i:
                        reduce(c, par, i - 1)
                    dve.wait_ge(s["ke_added"], at("ke_added", c * CH + i))
                    v.tensor_tensor(kqq[i % 2][:, :], kq[i % 2][:, :], ps_e[i % 2][:, D:2 * D], ALU.mult).then_inc(s["kq_ready"], 1)
                    if i == CH - 1:
                        reduce(c, par, i)

                SM = [8, 6, 7, 8, 2]

                def softmax(c, par, part):
                    n = [0]

                    def step(ins):
                        n[0] += 1
                        ins.then_inc(s["sm_step"], 1)

                    def settle():
                        dve.wait_ge(s["sm_step"], (c - 1) * sum(SM) + (sum(SM[:part]) + n[0]))

                    run = run_c[1 - par]
                    if part == 0:
                        dve.wait_ge(s["alpha_ready"], at("alpha_ready", c * CH - 1))
                        v.scalar_tensor_tensor(out=by_head(am[:, :], H), in0=by_head(alpha[1 - par][:, :], H), scalar=SCALE,
                                               in1=mask[:, bass.ds((c - 1) * CH, CH)][:, :, None].to_broadcast([P, CH, H]),
                                               op0=ALU.mult, op1=ALU.add).then_inc(s["am_ready"], 1)
                        dve.wait_ge(run_loaded[1 - par], (c - (2 - par)) * 8 + 16)
                        step(v.tensor_scalar(key_f[:, :], run[:, 0:1], float(H), head[:, 0:1], ALU.mult, ALU.add))
                        step(v.tensor_scalar(key_l[:, :], run[:, P - 1:P], float(H), head[:, 0:1], ALU.mult, ALU.add))
                        step(v.tensor_tensor(resets[:, 1:P], run[:, 1:P], run[:, 0:P - 1], ALU.not_equal))
                        step(v.tensor_scalar(off_first[:, :], run[:, :], run[:, 0:1], -BIG, ALU.not_equal, ALU.mult))
                        step(v.tensor_scalar(off_last[:, :], run[:, :], run[:, P - 1:P], -BIG, ALU.not_equal, ALU.mult))
                        settle()
                        step(v.tensor_scalar(resets[:, 1:P], resets[:, 1:P], -BIG, None, ALU.mult))
                        step(v.tensor_scalar(diag_k[:, 0:P], ident[:, :], key_f[:, 0:1], None, ALU.mult))
                        step(v.tensor_scalar(diag_k[:, P:2 * P], ident[:, :], key_l[:, 0:1], None, ALU.mult))
                        v.tensor_scalar(diag_k[:, 2 * P:], ident[:, P - H:P], key_prev[:, 0:1], None, ALU.mult).then_inc(s["keyed"], 1)
                    elif part == 1:
                        dve.wait_ge(s["am_turned"], at("am_turned", c - 1))
                        settle()
                        step(v.tensor_tensor_scan(out=scan_f[:, :], data0=resets[:, 0:P], data1=ps_a, initial=-BIG, op0=ALU.add, op1=ALU.max))
                        settle()
                        step(v.tensor_tensor_scan(out=scan_b[:, ::-1], data0=resets[:, P:0:-1], data1=scan_f[:, ::-1], initial=-BIG,
                                                  op0=ALU.add, op1=ALU.max))
                        step(v.tensor_scalar(diag_r[:, P:2 * P], ident[:, :], scan_f[:, P - 1:P], None, ALU.mult))
                        step(v.tensor_scalar(diag_r[:, 2 * P:], ident[:, P - H:P], max_prev[:, 0:1], None, ALU.mult))
                        settle()
                        v.tensor_scalar(diag_r[:, 0:P], ident[:, :], scan_b[:, 0:1], None, ALU.mult).then_inc(s["r_ready"], 1)
                        step(v.tensor_scalar(not_f[:, :], ps_k, key_f[:, 0:1], -BIG, ALU.not_equal, ALU.mult))
                        step(v.tensor_scalar(not_l[:, :], ps_k, key_l[:, 0:1], -BIG, ALU.not_equal, ALU.mult))
                    elif part == 2:
                        step(v.tensor_copy(keys2[:, 0:1], ps_k[:, 0:1]))
                        step(v.tensor_copy(keys2[:, 1:2], ps_k[:, 2 * P:2 * P + 1]))
                        dve.wait_ge(s["max_spread"], at("max_spread", c - 1))
                        settle()
                        step(v.tensor_copy(carry[:, :], ps_r[:, 2 * P:]))
                        step(v.tensor_tensor(not_f[:, :], not_f[:, :], ps_r, ALU.add))
                        step(v.tensor_tensor(not_l[:, :], not_l[:, :], ps_r, ALU.add))
                        settle()
                        step(v.tensor_reduce(max_f[:, :], not_f[:, :], AX_X, ALU.max))
                        step(v.tensor_reduce(max_l[:, :], not_l[:, :], AX_X, ALU.max))
                        settle()
                        v.tensor_scalar(diag_f[:, :], ident[:, 0:H], max_f[:, 0:1], None, ALU.mult).then_inc(s["f_ready"], 1)
                    elif part == 3:
                        step(v.scalar_tensor_tensor(out=scan_b[:, :], in0=off_first[:, :], scalar=max_f[:, 0:1], in1=scan_b[:, :],
                                                    op0=ALU.add, op1=ALU.max))
                        step(v.tensor_tensor(same[:, :], keys2[:, 0:1], keys2[:, 1:2], ALU.is_equal))
                        step(v.tensor_scalar(node_key[:, :], chunk_tile[:, bass.ds(c - 1, 1)], float(P * H), part8[:, 0:1],
                                             ALU.mult, ALU.add))
                        settle()
                        step(v.scalar_tensor_tensor(out=off_last[:, :], in0=off_last[:, :], scalar=max_l[:, 0:1], in1=scan_b[:, :],
                                                    op0=ALU.add, op1=ALU.max))
                        step(v.tensor_scalar(pick[:, :], node_key[:, :], keys2[:, 0:1], same[:, 0:1], ALU.is_equal, ALU.mult))
                        step(v.tensor_copy(max_prev[:, :], max_l[:, :]))
                        step(v.tensor_copy(key_prev[:, :], key_l[:, :]))
                        settle()
                        dve.wait_ge(s["shifted_turned"], at("shifted_turned", c - 2))
                        v.tensor_tensor(shifted[:, :], ps_a, off_last[:, :], ALU.subtract).then_inc(s["shifted_ready"], 1)
                        step(v.tensor_scalar(unpick[:, :], pick[:, :], -1.0, 1.0, ALU.mult, ALU.add))
                    else:
                        dve.wait_ge(s["ea_ready"], at("ea_ready", c - 1))
                        v.tensor_tensor(carry_d[:, :], carry[:, :], ps_f, ALU.subtract).then_inc(s["carry_ready"], 1)
                        dve.wait_ge(s["carry_exp"], at("carry_exp", c - 1))
                        step(v.tensor_scalar(factor[:, :], carry_e[:, :], pick[:, 0:1], unpick[:, 0:1], ALU.mult, ALU.add))
                        n0 = dve.value_load(item_node_tile[0:1, bass.ds((c - 1) * CH, 1)], min_val=0, max_val=NT)
                        a = by_head(flat(acc[:, :, :])[:, bass.ds(n0 * UW, UW)], CP)
                        settle()
                        dve.wait_ge(s["acc_added"], at("acc_added", (c - 1) * CH - 1))
                        step(v.tensor_tensor(a, a, factor[:, :, None].to_broadcast([P, H, CP]), ALU.mult))
                        settle()
                        dve.sem_inc(s["softmax_done"], 1)
                    assert n[0] == SM[part], (part, n[0])

                def weigh(c, par, i):
                    m = (c - 1) * CH + i
                    dve.wait_ge(s["ea_ready"], at("ea_ready", c - 1))
                    dve.wait_ge(s["summed"], at("summed", m - N_W))
                    v.tensor_tensor(by_head(w_ring[:, i % N_W, :], CP), by_head(ve[:, 1 - par, i, :], CP),
                                    ea[1 - par][:, i * H:(i + 1) * H][:, :, None].to_broadcast([P, H, CP]),
                                    ALU.mult).then_inc(s["weighted"], 1)

                def add(c, i):
                    m = (c - 1) * CH + i
                    n = dve.value_load(item_node_tile[0:1, bass.ds(m, 1)], min_val=0, max_val=NT)
                    a = flat(acc[:, :, :])[:, bass.ds(n * UW, UW)]
                    dve.wait_ge(s["summed"], at("summed", m))
                    dve.wait_ge(s["acc_added"], at("acc_added", m - 1))
                    v.tensor_tensor(a, a, ps_u[i % 2][:, 0:UW], ALU.add).then_inc(s["acc_added"], 1)

                def emit(c, par, steps):
                    for kind, i in steps:
                        if kind == "score":
                            score(c, par, i)
                        elif kind == "softmax":
                            softmax(c, par, i)
                        elif kind == "weigh":
                            weigh(c, par, i)
                        else:
                            add(c, i)

                over_chunks(dve, emit)

        x1 = q_sb
        xn2 = acc
        with ExitStack() as c4:
            def sb4(name, shape, dt=F32):
                return sb(name, shape, dt, c4)

            wg_sb = sb4("wg_sb", [P, KD, NE])
            bg_sb = sb4("bg_sb", [P, NE])
            gb_sb = sb4("gb_sb", [P, NE])
            bias_sb = sb4("bias_sb", [P, NE])
            zeros = sb4("zeros", [P, 5 * D])
            skip = [sb4(f"skip{i}", [P, D]) for i in range(2)]
            den = sb4("den", [P, H])
            inv = sb4("inv", [P, H])
            att = sb4("att", [P, D])
            stat = sb4("stat4", [P, 6])
            mv = sb4("mv4", [P, 2])
            vp = sb4("vp4", [P, 1])
            sd = sb4("sd4", [P, 1])
            r0 = sb4("r04", [P, 1])
            r1 = sb4("r14", [P, 1])
            r2 = sb4("r24", [P, 1])
            r3 = sb4("r34", [P, 1])
            rstd = sb4("rstd4", [P, 1])
            xnT = [sb4(f"xnT4{i}", [P, D]) for i in range(2)]
            xnc = [sb4(f"xnc{i}", [P, D]) for i in range(2)]
            ps_t = [c4.enter_context(nc.psum_tensor(f"ps_t4{i}", [P, 512], F32)) for i in range(2)]
            ps_g = [c4.enter_context(nc.psum_tensor(f"ps_g4{i}", [P, 512], F32)) for i in range(2)]
            s, at, grant = counters(c4, loaded=0, zero_set=0, zeroed=0, skip_free=2, ln_step=0, var_ready=0, sd_ready=0,
                                    xn_ready=0, xn_turned=2, xn_kept=2, xnT_ready=2, gated=2, logits_ready=2, act_pace=0, dve_pace=0,
                                    bias_ready=0)
            skip_loaded = [sem(f"skip_loaded{i}", c4) for i in range(2)]
            block = c4.enter_context(nc.Block())

            def over_tiles4(eng, emit):
                with eng.Fori(0, NT // 2) as g:
                    emit(g * 2, 0)
                    emit(g * 2 + 1, 1)
                if NT % 2:
                    emit(NT - 1, 0)

            ZR = 5
            NZ = ceil_div(NB, ZR)

            @block.sync
            def _(sp):
                sp.dma_start(wg_sb[:, :, :], Wg.rearrange("(k p) n -> p k n", p=P)).then_inc(s["loaded"], 16)
                sp.dma_start(bg_sb[:, :], bg.rearrange("(o n) -> o n", o=1).to_broadcast([P, NE])).then_inc(s["loaded"], 16)
                sp.dma_start(gb_sb[:, :], gbias.rearrange("(o n) -> o n", o=1).to_broadcast([P, NE])).then_inc(s["loaded"], 16)

                def load(j, par):
                    sp.wait_ge(s["skip_free"], at("skip_free", j - 2))
                    sp.dma_start(skip[par][:, :], skip_table[bass.ds(j * P, P), :]).then_inc(skip_loaded[par], 16)

                over_tiles4(sp, load)
                sp.wait_ge(s["zero_set"], 1)
                zr = sorted_x.rearrange("(p r) d -> p (r d)", p=P)
                for z in range(NZ):
                    w = min(ZR, NB - z * ZR) * D
                    sp.dma_start(zr[:, z * ZR * D:z * ZR * D + w], zeros[:, 0:w]).then_inc(s["zeroed"], 16)
                sp.wait_ge(s["zeroed"], 16 * NZ)

            @block.scalar
            def _(act):
                grant(act, "xnT_ready", "xn_kept")

                def tile(j, par):
                    act.wait_ge(s["var_ready"], at("var_ready", j))
                    act.sem_inc(s["act_pace"], 1)
                    nc.scalar.activation(sd[:, :], vp[:, :], ACT.Sqrt).then_inc(s["sd_ready"], 1)
                    act.wait_ge(s["xn_ready"], at("xn_ready", j))
                    nc.scalar.copy(flat(xn2[:, :, :])[:, bass.ds(j * UW, D)], xnc[par][:, :]).then_inc(s["xn_kept"], 1)
                    act.wait_ge(s["xn_turned"], at("xn_turned", j))
                    act.wait_ge(s["gated"], at("gated", j - 2))
                    nc.scalar.copy(xnT[par][:, :], ps_t[par][:, 0:D]).then_inc(s["xnT_ready"], 1)

                over_tiles4(act, tile)

            @block.tensor
            def _(pe):
                grant(pe, "gated", "xn_turned")
                pe.wait_ge(s["loaded"], 16 * 3)

                def tile(j, par):
                    pe.wait_ge(s["xn_ready"], at("xn_ready", j))
                    pe.wait_ge(s["xnT_ready"], at("xnT_ready", j - 2))
                    for k in range(KD):
                        last = nc.tensor.transpose(ps_t[par][:, k * P:(k + 1) * P], xnc[par][:, k * P:(k + 1) * P], ident[:, :])
                    last.then_inc(s["xn_turned"], 1)
                    pe.wait_ge(s["xnT_ready"], at("xnT_ready", j))
                    pe.wait_ge(s["logits_ready"], at("logits_ready", j - 2))
                    for k in range(KD):
                        last = nc.tensor.matmul(ps_g[par][:, 0:NE], xnT[par][:, k * P:(k + 1) * P], wg_sb[:, k, :],
                                                start=(k == 0), stop=(k == KD - 1))
                    last.then_inc(s["gated"], 1)

                over_tiles4(pe, tile)

            LN_STEPS = 10

            @block.vector
            def _(dve):
                v = nc.vector
                grant(dve, "skip_free", "logits_ready")
                v.memset(zeros[:, :], 0.0).then_inc(s["zero_set"], 1)
                dve.wait_ge(s["loaded"], 16 * 3)
                v.tensor_tensor(bias_sb[:, :], bg_sb[:, :], gb_sb[:, :], ALU.add).then_inc(s["bias_ready"], 1)
                dve.wait_ge(s["bias_ready"], 1)

                def node_tile(j, par):
                    n = [0]

                    def then(ins):
                        n[0] += 1
                        ins.then_inc(s["ln_step"], 1)
                        dve.wait_ge(s["ln_step"], j * LN_STEPS + n[0])
                        dve.sem_inc(s["dve_pace"], 1)

                    u = flat(acc[:, :, :])[:, bass.ds(j * UW, UW)].rearrange("p (h c) -> p h c", c=CP)
                    xj = flat(x1[:, :, :])[:, bass.ds(j * D, D)]
                    then(v.tensor_scalar(den[:, :], u[:, :, C:CP].rearrange("p h c -> p (h c)"), 1e-16, None, ALU.add))
                    then(v.reciprocal(inv[:, :], den[:, :]))
                    then(v.tensor_tensor(att[:, :].rearrange("p (h c) -> p h c", c=C), u[:, :, 0:C],
                                         inv[:, :, None].to_broadcast([P, H, C]), ALU.mult))
                    dve.wait_ge(skip_loaded[par], (j - par) * 8 + 16)
                    v.tensor_tensor(xj, att[:, :], skip[par][:, :], ALU.add).then_inc(s["skip_free"], 1)
                    dve.wait_ge(s["skip_free"], at("skip_free", j))
                    dve.sem_inc(s["dve_pace"], 1)
                    then(v.bn_stats(stat[:, :], xj))
                    then(v.bn_aggr(mv[:, :], stat[:, :]))
                    v.tensor_scalar(vp[:, :], mv[:, 1:2], LN_EPS, None, ALU.add).then_inc(s["var_ready"], 1)
                    dve.wait_ge(s["sd_ready"], at("sd_ready", j))
                    then(v.reciprocal(r0[:, :], sd[:, :]))
                    then(v.tensor_tensor(r1[:, :], r0[:, :], r0[:, :], ALU.mult))
                    then(v.tensor_tensor(r2[:, :], r1[:, :], vp[:, :], ALU.mult))
                    then(v.tensor_scalar(r3[:, :], r2[:, :], -0.5, 1.5, ALU.mult, ALU.add))
                    then(v.tensor_tensor(rstd[:, :], r0[:, :], r3[:, :], ALU.mult))
                    assert n[0] == LN_STEPS, n[0]
                    dve.wait_ge(s["xn_turned"], at("xn_turned", j - 2))
                    dve.wait_ge(s["xn_kept"], at("xn_kept", j - 2))
                    v.tensor_scalar(xnc[par][:, :], xj, mv[:, 0:1], rstd[:, 0:1], ALU.subtract, ALU.mult).then_inc(s["xn_ready"], 1)

                def gate(j, par):
                    dve.wait_ge(s["gated"], at("gated", j))
                    v.tensor_tensor(flat(logits)[:, bass.ds(j * NE, NE)], ps_g[par][:, 0:NE], bias_sb[:, :],
                                    ALU.add).then_inc(s["logits_ready"], 1)

                node_tile(0, 0)
                with dve.Fori(0, NT // 2) as g:
                    node_tile(g * 2 + 1, 1)
                    gate(g * 2, 0)
                    node_tile(g * 2 + 2, 0)
                    gate(g * 2 + 1, 1)
                gate(NT - 1, 0)

        with ExitStack() as c5:
            def sb5(name, shape, dt=F32):
                return sb(name, shape, dt, c5)

            top8 = sb5("top8", [P, NT, 8])
            rank = sb5("rank", [P, NT, NE])
            more = sb5("more", [P, NT, NE])
            diff = sb5("diff", [P, NT])
            ex = sb5("ex", [P, NT])
            exp1 = sb5("exp1", [P, NT])
            taken = sb5("taken", [P, NT, NE])
            is_k = [sb5(f"is_k{k}", [P, NT, NE]) for k in range(TOP)]
            lower = sb5("lower", [P, P])
            totals = sb5("totals", [P, NE, NT])
            zeros_t = sb5("zeros_t", [P, NE, NT])
            running = sb5("running", [P, NE, NT])
            count_i = sb5("count_i", [P, NE], I32)
            blocks_i = sb5("blocks_i", [P, NE], I32)
            blocks = sb5("blocks", [P, NE])
            ends = sb5("ends", [P, NE])
            starts = sb5("starts", [P, NE])
            place = sb5("place", [P, NT, NE])
            place2 = sb5("place2", [P, NT, NE])
            slots = sb5("slots", [P, TOP, NT])
            bi_i = sb5("bi_i", [1, NB], I32)
            bi = sb5("bi", [1, NB])
            be = sb5("be", [1, NB])
            ps_pre = c5.enter_context(nc.psum_tensor("ps_pre", [P, 512], F32))
            ps_tot = c5.enter_context(nc.psum_tensor("ps_tot", [P, 512], F32))
            dve_step = sem("route_step", c5)
            diff_ready = sem("diff_ready", c5)
            exp_ready = sem("exp_ready", c5)
            taken_ready = sem("taken_ready", c5)
            counted = sem("counted", c5)
            bi_set = sem("bi_set", c5)
            block = c5.enter_context(nc.Block())
            assert NT * NE <= 512 and NE == 8

            @block.gpsimd
            def _(pool):
                nc.gpsimd.iota(bi_i[:, :], [[1, NB]], base=0, channel_multiplier=0).then_inc(bi_set, 1)

            @block.scalar
            def _(act):
                act.wait_ge(diff_ready, 1)
                nc.scalar.activation(ex[:, :], diff[:, :], ACT.Exp).then_inc(exp_ready, 1)

            @block.tensor
            def _(pe):
                pe.wait_ge(taken_ready, 1)
                tk = taken[:, :, :].rearrange("p j e -> p (j e)")
                nc.tensor.matmul(ps_pre[:, 0:NT * NE], lower[:, :], tk, start=True, stop=True)
                nc.tensor.matmul(ps_tot[:, 0:NT * NE], ones[:, :], tk, start=True, stop=True).then_inc(counted, 1)

            @block.vector
            def _(dve):
                v = nc.vector
                count = [0]

                def then(ins):
                    count[0] += 1
                    ins.then_inc(dve_step, 1)
                    dve.wait_ge(dve_step, count[0])

                for j in range(NT):
                    last = v.max(top8[:, j, :], logits[:, j, :])
                then(last)
                then(v.tensor_tensor(diff[:, :], top8[:, :, 1:2].rearrange("p j o -> p (j o)"),
                                     top8[:, :, 0:1].rearrange("p j o -> p (j o)"), ALU.subtract))
                dve.sem_inc(diff_ready, 1)
                then(v.memset(rank[:, :, :], 0.0))
                for f in range(NE):
                    lf = logits[:, :, f:f + 1]
                    if f:
                        v.tensor_tensor(more[:, :, 0:f], lf.to_broadcast([P, NT, f]), logits[:, :, 0:f], ALU.is_gt)
                    then(v.tensor_tensor(more[:, :, f:NE], lf.to_broadcast([P, NT, NE - f]), logits[:, :, f:NE], ALU.is_ge))
                    then(v.tensor_tensor(rank[:, :, :], rank[:, :, :], more[:, :, :], ALU.add))
                v.tensor_scalar(lower[:, :], iota_free[:, :], iota_part[:, 0:1], None, ALU.is_gt)
                v.tensor_scalar(is_k[0][:, :, :], rank[:, :, :], 1.0, None, ALU.is_equal)
                v.tensor_scalar(is_k[1][:, :, :], rank[:, :, :], 2.0, None, ALU.is_equal)
                v.tensor_scalar(taken[:, :, :], rank[:, :, :], TOP + 0.5, None, ALU.is_lt).then_inc(taken_ready, 1)
                dve.wait_ge(exp_ready, 1)
                then(v.tensor_scalar(exp1[:, :], ex[:, :], 1.0, None, ALU.add))
                then(v.reciprocal(gate_w[:, 0, :], exp1[:, :]))
                then(v.tensor_tensor(gate_w[:, 1, :], ex[:, :], gate_w[:, 0, :], ALU.mult))
                dve.wait_ge(counted, 1)
                v.memset(zeros_t[:, :, :], 0.0)
                then(v.tensor_copy(totals[:, :, :], ps_tot[:, 0:NT * NE].rearrange("p (j e) -> p e j", e=NE)))
                for e in range(NE):
                    last = v.tensor_tensor_scan(out=running[:, e, :], data0=zeros_t[:, e, :], data1=totals[:, e, :], initial=0.0,
                                                op0=ALU.add, op1=ALU.add)
                then(last)
                then(v.tensor_scalar(count_i[:, :], running[:, :, NT - 1:NT].rearrange("p e o -> p (e o)"), float(P - 1), None, ALU.add))
                then(v.tensor_scalar(blocks_i[:, :], count_i[:, :], P.bit_length() - 1, None, ALU.logical_shift_right))
                then(v.tensor_copy(blocks[:, :], blocks_i[:, :]))
                then(v.tensor_tensor_scan(out=ends[:, :], data0=zeros_t[:, :, :].rearrange("p e j -> p (e j)")[:, 0:NE], data1=blocks[:, :], initial=0.0, op0=ALU.add, op1=ALU.add))
                then(v.tensor_tensor(starts[:, :], ends[:, :], blocks[:, :], ALU.subtract))
                then(v.tensor_scalar(starts[:, :], starts[:, :], float(P), None, ALU.mult))
                then(v.tensor_tensor(place[:, :, :], running[:, :, :].rearrange("p e j -> p j e"),
                                     totals[:, :, :].rearrange("p e j -> p j e"), ALU.subtract))
                then(v.tensor_tensor(place2[:, :, :], place[:, :, :], ps_pre[:, 0:NT * NE].rearrange("p (j e) -> p j e", e=NE), ALU.add))
                then(v.tensor_tensor(place[:, :, :], place2[:, :, :], starts[:, None, :].to_broadcast([P, NT, NE]), ALU.add))
                for k in range(TOP):
                    then(v.tensor_tensor(place2[:, :, :], place[:, :, :], is_k[k][:, :, :], ALU.mult))
                    then(v.tensor_reduce(slots[:, k, :], place2[:, :, :], AX_X, ALU.add))
                v.tensor_copy(slot_i[:, :, :], slots[:, :, :])
                dve.wait_ge(bi_set, 1)
                then(v.tensor_copy(bi[:, :], bi_i[:, :]))
                then(v.memset(be[:, :], 0.0))
                for e in range(NE - 1):
                    then(v.scalar_tensor_tensor(out=be[:, :], in0=bi[:, :], scalar=ends[0:1, e:e + 1], in1=be[:, :], op0=ALU.is_ge, op1=ALU.add))
                v.tensor_copy(block_expert[:, :], be[:, :])

        with ExitStack() as c6:
            scattered = sem("scattered", c6)
            block = c6.enter_context(nc.Block())

            @block.gpsimd
            def _(pool):
                for j in range(NT):
                    for k in range(TOP):
                        nc.gpsimd.indirect_dma_start(
                            out=sorted_x, out_offset=bass.IndirectOffsetOnAxis(ap=slot_i[:, k, j:j + 1], axis=0),
                            in_=xn2[:, j, 0:D], in_offset=None).then_inc(scattered, 16)
                pool.wait_ge(scattered, 16 * NT * TOP)

        c_acc.close()

        with ExitStack() as c7:
            def sb7(name, shape, dt=F32):
                return sb(name, shape, dt, c7)

            w1_sb = sb7("w1_sb", [P, KD, NE * F])
            w2_sb = sb7("w2_sb", [P, KF, NE * D])
            b1_sb = sb7("b1_sb", [P, NE * F])
            b2_sb = sb7("b2_sb", [P, NE * D])
            t_in = [sb7(f"t_in{i}", [P, D]) for i in range(2)]
            tT = [sb7(f"tT{i}", [P, D]) for i in range(2)]
            hid = [sb7(f"hid{i}", [P, F]) for i in range(2)]
            hT = [sb7(f"hT{i}", [P, F]) for i in range(2)]
            y = [sb7(f"y{i}", [P, D]) for i in range(2)]
            ps_t = [c7.enter_context(nc.psum_tensor(f"ps_t7{i}", [P, 512], F32)) for i in range(2)]
            ps_h = [c7.enter_context(nc.psum_tensor(f"ps_h7{i}", [P, 512], F32)) for i in range(2)]
            ps_ht = [c7.enter_context(nc.psum_tensor(f"ps_ht7{i}", [P, 512], F32)) for i in range(2)]
            ps_y = [c7.enter_context(nc.psum_tensor(f"ps_y7{i}", [P, 512], F32)) for i in range(2)]
            s, at, grant = counters(c7, loaded=0, x_turned=2, tT_ready=2, h_summed=2, hid_ready=2, h_turned=2, hT_ready=2,
                                    y_summed=2, y_ready=2, act_pace=0)
            x_loaded = [sem(f"x_loaded{i}", c7) for i in range(2)]
            y_stored = [sem(f"y_stored{i}", c7) for i in range(2)]
            block = c7.enter_context(nc.Block())
            assert F == 512 and NB % 2 == 1

            def over_blocks(eng, emit):
                emit(0, 0)
                with eng.Fori(0, NB // 2) as g:
                    emit(g * 2 + 1, 1)
                    emit(g * 2 + 2, 0)

            @block.sync
            def _(sp):
                def load(b, par):
                    sp.wait_ge(s["x_turned"], at("x_turned", b - 2))
                    sp.dma_start(t_in[par][:, :], sorted_x[bass.ds(b * P, P), :]).then_inc(x_loaded[par], 16)

                load(0, 0)
                for k in range(KD):
                    sp.dma_start(w1_sb[:, k, :].rearrange("p (e f) -> p e f", e=NE),
                                 W1[:, k * P:(k + 1) * P, :].rearrange("e p f -> p e f")).then_inc(s["loaded"], 16)
                for k in range(KF):
                    sp.dma_start(w2_sb[:, k, :].rearrange("p (e f) -> p e f", e=NE),
                                 W2[:, k * P:(k + 1) * P, :].rearrange("e p f -> p e f")).then_inc(s["loaded"], 16)
                sp.dma_start(b1_sb[:, :], b1.rearrange("(o e) f -> o (e f)", o=1).to_broadcast([P, NE * F])).then_inc(s["loaded"], 16)
                sp.dma_start(b2_sb[:, :], b2.rearrange("(o e) f -> o (e f)", o=1).to_broadcast([P, NE * D])).then_inc(s["loaded"], 16)
                with sp.Fori(0, NB // 2) as g:
                    load(g * 2 + 1, 1)
                    load(g * 2 + 2, 0)

            @block.scalar
            def _(act):
                grant(act, "tT_ready", "hT_ready")

                def emit(b, par):
                    act.wait_ge(s["x_turned"], at("x_turned", b))
                    act.wait_ge(s["h_summed"], at("h_summed", b - 2))
                    nc.scalar.copy(tT[par][:, :], ps_t[par][:, 0:D]).then_inc(s["tT_ready"], 1)
                    act.wait_ge(s["h_turned"], at("h_turned", b))
                    act.sem_inc(s["act_pace"], 1)
                    act.wait_ge(s["y_summed"], at("y_summed", b - 2))
                    act.sem_inc(s["act_pace"], 1)
                    nc.scalar.activation(hT[par][:, :], ps_ht[par][:, :], ACT.Relu).then_inc(s["hT_ready"], 1)
                    act.wait_ge(s["y_ready"], at("y_ready", b))
                    act.dma_start(sorted_y[bass.ds(b * P, P), :], y[par][:, :]).then_inc(y_stored[par], 16)

                over_blocks(act, emit)
                act.wait_ge(y_stored[0], 16 + 16 * ceil_div(NB, 2))
                act.wait_ge(y_stored[1], 16 + 16 * (NB // 2))

            @block.tensor
            def _(pe):
                t = nc.tensor
                grant(pe, "x_turned", "h_summed", "h_turned", "y_summed")

                def emit(b, par):
                    pe.wait_ge(x_loaded[par], (b - par) * 8 + 16)
                    pe.wait_ge(s["tT_ready"], at("tT_ready", b - 2))
                    for k in range(KD):
                        last = t.transpose(ps_t[par][:, k * P:(k + 1) * P], t_in[par][:, k * P:(k + 1) * P], ident[:, :])
                    last.then_inc(s["x_turned"], 1)
                    if isinstance(b, int):
                        pe.wait_ge(s["loaded"], 16 * (KD + KF + 2))
                    ex = pe.value_load(block_expert[0:1, bass.ds(b, 1)], min_val=0, max_val=NE - 1)
                    pe.wait_ge(s["tT_ready"], at("tT_ready", b))
                    pe.wait_ge(s["hid_ready"], at("hid_ready", b - 2))
                    for k in range(KD):
                        last = t.matmul(ps_h[par][:, :], tT[par][:, k * P:(k + 1) * P], w1_sb[:, k, bass.ds(ex * F, F)],
                                        start=(k == 0), stop=(k == KD - 1))
                    last.then_inc(s["h_summed"], 1)
                    pe.wait_ge(s["hid_ready"], at("hid_ready", b))
                    pe.wait_ge(s["hT_ready"], at("hT_ready", b - 2))
                    for k in range(KF):
                        last = t.transpose(ps_ht[par][:, k * P:(k + 1) * P], hid[par][:, k * P:(k + 1) * P], ident[:, :])
                    last.then_inc(s["h_turned"], 1)
                    pe.wait_ge(s["hT_ready"], at("hT_ready", b))
                    pe.wait_ge(s["y_ready"], at("y_ready", b - 2))
                    for k in range(KF):
                        last = t.matmul(ps_y[par][:, 0:D], hT[par][:, k * P:(k + 1) * P], w2_sb[:, k, bass.ds(ex * D, D)],
                                        start=(k == 0), stop=(k == KF - 1))
                    last.then_inc(s["y_summed"], 1)

                over_blocks(pe, emit)

            @block.vector
            def _(dve):
                v = nc.vector
                grant(dve, "hid_ready", "y_ready")
                dve.sem_inc(y_stored[0], 16)
                dve.sem_inc(y_stored[1], 16)

                def emit(b, par):
                    if isinstance(b, int):
                        dve.wait_ge(s["loaded"], 16 * (KD + KF + 2))
                    ex = dve.value_load(block_expert[0:1, bass.ds(b, 1)], min_val=0, max_val=NE - 1)
                    dve.wait_ge(s["h_summed"], at("h_summed", b))
                    dve.wait_ge(s["h_turned"], at("h_turned", b - 2))
                    v.tensor_tensor(hid[par][:, :], ps_h[par][:, :], b1_sb[:, bass.ds(ex * F, F)], ALU.add).then_inc(s["hid_ready"], 1)
                    dve.wait_ge(s["y_summed"], at("y_summed", b))
                    dve.wait_ge(y_stored[par], (b - par) * 8 + 16)
                    v.tensor_tensor(y[par][:, :], ps_y[par][:, 0:D], b2_sb[:, bass.ds(ex * D, D)], ALU.add).then_inc(s["y_ready"], 1)

                over_blocks(dve, emit)

        with ExitStack() as c8:
            NG = 4
            got = [[sb(f"got{k}_{i}", [P, D], F32, c8) for i in range(NG)] for k in range(TOP)]
            half = [sb(f"half{i}", [P, D], F32, c8) for i in range(2)]
            o = [sb(f"o{i}", [P, D], F32, c8) for i in range(NG)]
            g_loaded = [sem(f"g_loaded{i}", c8) for i in range(NG)]
            halved = sem("halved", c8)
            summed = sem("out_summed", c8)
            out_stored = [sem(f"out_stored{i}", c8) for i in range(NG)]
            block = c8.enter_context(nc.Block())

            @block.gpsimd
            def _(pool):
                for j in range(NT):
                    if j >= NG:
                        pool.wait_ge(summed, j - NG + 1)
                    for k in range(TOP):
                        nc.gpsimd.indirect_dma_start(
                            out=got[k][j % NG][:, :], out_offset=None, in_=sorted_y,
                            in_offset=bass.IndirectOffsetOnAxis(ap=slot_i[:, k, j:j + 1], axis=0)).then_inc(g_loaded[j % NG], 16)

            @block.vector
            def _(dve):
                for j in range(NT):
                    dve.wait_ge(g_loaded[j % NG], 32 * (j // NG + 1))
                    nc.vector.scalar_tensor_tensor(out=half[j % 2][:, :], in0=got[0][j % NG][:, :], scalar=gate_w[:, 0, j:j + 1],
                                                   in1=x1[:, j, :], op0=ALU.mult, op1=ALU.add).then_inc(halved, 1)
                    dve.wait_ge(halved, j + 1)
                    if j >= NG:
                        dve.wait_ge(out_stored[j % NG], 16 * (j // NG))
                    nc.vector.scalar_tensor_tensor(out=o[j % NG][:, :], in0=got[1][j % NG][:, :], scalar=gate_w[:, 1, j:j + 1],
                                                   in1=half[j % 2][:, :], op0=ALU.mult, op1=ALU.add).then_inc(summed, 1)

            @block.sync
            def _(sp):
                for j in range(NT):
                    n = P if j < NT - 1 else NTAIL
                    sp.wait_ge(summed, j + 1)
                    sp.dma_start(out[j * P:j * P + n, :], o[j % NG][0:n, :]).then_inc(out_stored[j % NG], 16)
                for i in range(NG):
                    sp.wait_ge(out_stored[i], 16 * ((NT - i + NG - 1) // NG))


_INS = ["x", "src", "dst", "edge_attr_256", "L0_gnn_Wq", "L0_gnn_bq", "L0_gnn_Wk", "L0_gnn_bk", "L0_gnn_Wv", "L0_gnn_bv",
        "L0_gnn_We", "L0_gnn_Ws", "L0_gnn_bs", "L0_ffn_Wg", "L0_ffn_bg", "L0_ffn_bias", "L0_ffn_W1", "L0_ffn_b1",
        "L0_ffn_W2", "L0_ffn_b2"]


def kernel(**inputs):
    import numpy as _np
    import concourse.bacc as _bacc
    from concourse import mybir as _mybir
    from concourse.bass_utils import run_bass_kernel_spmd as _run

    nc = _bacc.Bacc("TRN2", target_bir_lowering=False, num_devices=1)
    arrays, args = {}, []
    for name in _INS:
        a = _np.ascontiguousarray(inputs[name])
        arrays[f"in_{name}"] = a
        args.append(nc.dram_tensor(f"in_{name}", a.shape, _mybir.dt.from_np(a.dtype), kind="ExternalInput").ap())
    n, d = inputs["x"].shape
    args.append(nc.dram_tensor("out_0", (n, d), F32, kind="ExternalOutput").ap())
    gnn_ffn(nc, *args)
    r = _run(nc, [arrays], core_ids=[0])
    return r.results[0]["out_0"]
```

```python
from contextlib import ExitStack

import concourse.bass as bass
from concourse import mybir

F32 = mybir.dt.float32
I32 = mybir.dt.int32
ALU = mybir.AluOpType
ACT = mybir.ActivationFunctionType
AX_X = mybir.AxisListType.X

P = 128
H = 8
CH = 16
BIG = 2.0 ** 100
PAD_DST = 1 << 20
LN_EPS = 1e-5
N_KV = 4
N_A = 4
N_W = 4
TOP = 2


def ceil_div(a, b):
    return -(-a // b)


def gnn_ffn(nc, x, src, dst, edge_attr, Wq, bq, Wk, bk, Wv, bv, We, Ws, bs, Wg, bg, gbias, W1, b1, W2, b2, out):
    N, D = x.shape
    E = edge_attr.shape[0]
    C = D // H
    KD = D // P
    NT = ceil_div(N, P)
    ET = ceil_div(E, P)
    NTAIL = N - (NT - 1) * P
    ETAIL = E - (ET - 1) * P
    NR = NT * P
    NCH = ceil_div(NT + ET - 1, CH)
    NCH += 1 - NCH % 2
    IT = NCH * CH
    IB = ceil_div(IT, P)
    RB = ceil_div(ET, P)
    SCALE = float(C) ** -0.5
    CP = C + 1
    UW = H * CP
    NE, _, F = W1.shape
    KF = F // P
    NB = (NR * TOP + NE * (P - 1)) // P
    assert D == 2 * P and H * C == D and 0 < ETAIL < P and NT < P

    with ExitStack() as ctx:
        def sb(name, shape, dt=F32, c=ctx):
            return c.enter_context(nc.sbuf_tensor(name, shape, dt))

        def sem(name, c=ctx):
            return c.enter_context(nc.semaphore(name))

        def counters(c, **credits):
            sems = {n: sem(n, c) for n in credits}

            def at(name, i):
                return i + (credits[name] + 1)

            def grant(eng, *names):
                for n in names:
                    eng.sem_inc(sems[n], credits[n])

            return sems, at, grant

        def dram(name, shape, dt=F32):
            return nc.dram_tensor(name, shape, dt, kind="Internal").ap()

        src_rows = dram("src_rows", (ET, P), I32)
        sel_rows = dram("sel_rows", (ET, P), I32)
        run_rows = dram("run_rows", (ET, P), I32)
        run_table = dram("run_table", (IT, H, P))
        kv_table = dram("kv_table", (NR, 2 * D))
        skip_table = dram("skip_table", (NR, D))
        sorted_x = dram("sorted_x", (NB * P, D))
        sorted_y = dram("sorted_y", (NB * P, D))

        ident = sb("ident", [P, P])
        ones = sb("ones", [P, P])
        iota_free = sb("iota_free", [P, P])
        iota_part = sb("iota_part", [P, 1])
        src_idx = sb("src_idx", [P, IT], I32)
        dst_loc = sb("dst_loc", [P, IT])
        mask = sb("mask", [P, IT])
        item_node_tile = sb("item_node_tile", [1, IT], I32)
        item_row = sb("item_row", [1, IT], I32)
        chunk_tile = sb("chunk_tile", [P, NCH])

        with ExitStack() as c1:
            def sb1(name, shape, dt=F32):
                return sb(name, shape, dt, c1)

            def ps1(name, shape):
                return c1.enter_context(nc.psum_tensor(name, shape, F32))

            dst_sb = sb1("dst_sb", [P, RB, P], I32)
            lasts = sb1("lasts", [P, RB])
            thr_i = sb1("thr_i", [P, NT], I32)
            thr = sb1("thr", [P, NT])
            below = sb1("below", [P, NT, RB])
            below_n = sb1("below_n", [P, NT])
            step_at = sb1("step_at", [NT, 1])
            ii_i = sb1("ii_i", [P, IT], I32)
            ii = sb1("ii", [P, IT])
            ip_i = sb1("ip_i", [P, IB], I32)
            ip = sb1("ip", [P, IB])
            if_i = sb1("if_i", [P, P], I32)
            pp_i = sb1("pp_i", [P, 1], I32)
            stepped = sb1("stepped", [NT, IT])
            node_tile_rep = sb1("node_tile_rep", [P, IT])
            t_rep = sb1("t_rep", [P, IT])
            r_rep = sb1("r_rep", [P, IT])
            t_item = sb1("t_item", [P, IB])
            t_idx = sb1("t_idx", [P, IB], I32)
            pad_dst = sb1("pad_dst", [1, P], I32)
            pad_src = sb1("pad_src", [1, P], I32)
            pad_run = sb1("pad_run", [1, P], I32)
            last_dst = sb1("last_dst", [1, 1], I32)
            src_g = sb1("src_g", [P, IB, P], I32)
            sel_g = sb1("sel_g", [P, IB, P], I32)
            run_g = sb1("run_g", [P, IB, P], I32)
            src_f = sb1("src_f", [P, IB, P])
            sel_f = sb1("sel_f", [P, IB, P])
            run_f = sb1("run_f", [P, IB, P])
            m_lo = sb1("m_lo", [P, IT])
            m_hi = sb1("m_hi", [P, IT])
            ps_rep = [ps1(f"ps_rep{i}", [P, 512]) for i in range(2)]
            ps_small = ps1("ps_small", [P, 512])
            ps_src = ps1("ps_src", [P, 512])
            ps_sel = ps1("ps_sel", [P, 512])

            dst_loaded = sem("dst_loaded", c1)
            rows_written = sem("rows_written", c1)
            pads_set = sem("pads_set", c1)
            last_loaded = sem("last_loaded", c1)
            iotas = sem("iotas", c1)
            dve_step = sem("dve_step", c1)
            below_ready = sem("below_ready", c1)
            step_summed = sem("step_summed", c1)
            stepped_ready = sem("stepped_ready", c1)
            rep_ready = sem("rep_ready", c1)
            item_ready = sem("item_ready", c1)
            t_idx_ready = sem("t_idx_ready", c1)
            gathered = [sem(f"gathered_{n}", c1) for n in ("run", "src", "sel")]
            floats_ready = sem("floats_ready", c1)
            turned = sem("turned", c1)
            turned_copied = sem("turned_copied", c1)
            run_written = sem("run_written", c1)
            full = ET - 1
            pad = P - ETAIL
            IH = IT // 2
            assert IH <= 512

            def rows_in(b, total=IT):
                return min(P, total - b * P)

            block = c1.enter_context(nc.Block())

            @block.sync
            def _(sp):
                with nc.allow_non_contiguous_dma(reason="the short tail row of the edge lists"):
                    nb = full // P
                    if nb:
                        sp.dma_start(dst_sb[:, 0:nb, :], dst[0:nb * P * P].rearrange("(b p e) -> p b e", p=P, e=P)).then_inc(dst_loaded, 16)
                    sp.dma_start(dst_sb[0:full - nb * P, nb, :],
                                 dst[nb * P * P:full * P].rearrange("(p e) -> p e", e=P)).then_inc(dst_loaded, 16)
                    sp.dma_start(last_dst[:, :], dst[full * P - 1:full * P].rearrange("(t e) -> t e", t=1)).then_inc(last_loaded, 16)
                    sp.wait_ge(pads_set, 3)
                    for rows, edges in ((src_rows, src), (sel_rows, dst), (run_rows, dst)):
                        sp.dma_start(rows[0:full, :], edges[0:full * P].rearrange("(t e) -> t e", e=P)).then_inc(rows_written, 16)
                        sp.dma_start(rows[full:ET, pad:P], edges[full * P:E].rearrange("(t e) -> t e", t=1)).then_inc(rows_written, 16)
                    sp.dma_start(src_rows[full:ET, 0:pad], pad_src[0:1, 0:pad]).then_inc(rows_written, 16)
                    sp.dma_start(sel_rows[full:ET, 0:pad], pad_dst[0:1, 0:pad]).then_inc(rows_written, 16)
                    sp.dma_start(run_rows[full:ET, 0:pad],
                                 pad_run[0:1, 0:pad]).then_inc(rows_written, 16)
                    sp.wait_ge(floats_ready, 3)
                    for b in range(IB):
                        n = rows_in(b)
                        sp.dma_start(run_table[b * P:b * P + n, :, :],
                                     run_f[0:n, b:b + 1, :].to_broadcast([n, H, P])).then_inc(run_written, 16)
                    sp.wait_ge(run_written, 16 * IB)

            @block.gpsimd
            def _(pool):
                nc.gpsimd.memset(pad_src[:, :], 0).then_inc(pads_set, 1)
                nc.gpsimd.memset(pad_dst[:, :], PAD_DST).then_inc(pads_set, 1)
                pool.wait_ge(last_loaded, 16)
                nc.gpsimd.tensor_copy(pad_run[:, :], last_dst[:, :].to_broadcast([1, P])).then_inc(pads_set, 1)
                nc.gpsimd.iota(if_i[:, :], [[1, P]], base=0, channel_multiplier=0).then_inc(iotas, 1)
                nc.gpsimd.iota(pp_i[:, :], [[1, 1]], base=0, channel_multiplier=1).then_inc(iotas, 1)
                nc.gpsimd.iota(thr_i[:, :], [[P, NT]], base=P, channel_multiplier=0).then_inc(iotas, 1)
                nc.gpsimd.iota(ii_i[:, :], [[1, IT]], base=0, channel_multiplier=0).then_inc(iotas, 1)
                nc.gpsimd.iota(ip_i[:, :], [[P, IB]], base=0, channel_multiplier=1).then_inc(iotas, 1)
                pool.wait_ge(rows_written, 16 * 9)
                pool.wait_ge(t_idx_ready, 2)
                for rows, got, got_sem in ((run_rows, run_g, gathered[0]), (src_rows, src_g, gathered[1]),
                                           (sel_rows, sel_g, gathered[2])):
                    for b in range(IB):
                        n = rows_in(b)
                        nc.gpsimd.indirect_dma_start(
                            out=got[0:n, b, :], out_offset=None, in_=rows,
                            in_offset=bass.IndirectOffsetOnAxis(ap=t_idx[0:n, b:b + 1], axis=0)).then_inc(got_sem, 16)

            @block.vector
            def _(dve):
                count = [0]

                def then(ins):
                    count[0] += 1
                    ins.then_inc(dve_step, 1)
                    dve.wait_ge(dve_step, count[0])

                v = nc.vector
                v.memset(ones[:, :], 1.0)
                then(v.memset(lasts[:, :], 1.0e9))
                dve.wait_ge(iotas, 5)
                v.tensor_copy(iota_free[:, :], if_i[:, :])
                v.tensor_copy(thr[:, :], thr_i[:, :])
                v.tensor_copy(ii[:, :], ii_i[:, :])
                v.tensor_copy(ip[:, :], ip_i[:, :])
                then(v.tensor_copy(iota_part[:, :], pp_i[:, :]))
                v.tensor_scalar(ident[:, :], iota_free[:, :], iota_part[:, 0:1], None, ALU.is_equal)
                nb = full // P
                dve.wait_ge(dst_loaded, 16 * (2 if nb else 1))
                if nb:
                    v.tensor_copy(lasts[:, 0:nb], dst_sb[:, 0:nb, P - 1])
                then(v.tensor_copy(lasts[0:full - nb * P, nb:nb + 1], dst_sb[0:full - nb * P, nb, P - 1:P]))
                then(v.tensor_tensor(below[:, :, :], lasts[:, None, :].to_broadcast([P, NT, RB]),
                                     thr[:, :, None].to_broadcast([P, NT, RB]), ALU.is_lt))
                v.tensor_reduce(below_n[:, :], below[:, :, :], AX_X, ALU.add).then_inc(below_ready, 1)
                dve.wait_ge(step_summed, 1)
                then(v.tensor_scalar(step_at[:, :], ps_small[0:NT, 0:1], float(ET - 1), iota_part[0:NT, 0:1], ALU.min, ALU.add))
                v.tensor_scalar(stepped[:, :], ii[0:NT, :], step_at[:, 0:1], None, ALU.is_gt).then_inc(stepped_ready, 1)
                dve.wait_ge(item_ready, 1)
                nf = IT // P
                if nf:
                    v.tensor_tensor(t_item[:, 0:nf], ip[:, 0:nf], ps_small[:, 8:8 + nf], ALU.subtract)
                if IB > nf:
                    n = rows_in(nf)
                    v.tensor_tensor(t_item[0:n, nf:IB], ip[0:n, nf:IB], ps_small[0:n, 8 + nf:8 + IB], ALU.subtract)
                then(v.memset(dst_sb[:, 0, 0:1], 0))
                if nf:
                    v.tensor_scalar(t_idx[:, 0:nf], t_item[:, 0:nf], float(ET - 1), None, ALU.min).then_inc(t_idx_ready, 1)
                else:
                    dve.sem_inc(t_idx_ready, 1)
                if IB > nf:
                    v.tensor_scalar(t_idx[0:n, nf:IB], t_item[0:n, nf:IB], float(ET - 1), None, ALU.min).then_inc(t_idx_ready, 1)
                else:
                    dve.sem_inc(t_idx_ready, 1)
                dve.wait_ge(rep_ready, 1)
                v.tensor_copy(node_tile_rep[:, 0:IH], ps_rep[0][:, 0:IH])
                then(v.tensor_copy(node_tile_rep[:, IH:IT], ps_rep[1][:, 0:IH]))
                v.tensor_copy(item_node_tile[:, :], node_tile_rep[0:1, :])
                v.tensor_copy(chunk_tile[:, :], node_tile_rep[:, 0:IT:CH])
                then(v.tensor_tensor(t_rep[:, :], ii[:, :], node_tile_rep[:, :], ALU.subtract))
                then(v.tensor_scalar(r_rep[:, :], t_rep[:, :], float(P), float(E - P), ALU.mult, ALU.min))
                v.tensor_copy(item_row[:, :], r_rep[0:1, :])
                for k, (got, flt) in enumerate(((run_g, run_f), (src_g, src_f), (sel_g, sel_f))):
                    dve.wait_ge(gathered[k], 16 * IB)
                    scale = BIG if k == 0 else 1.0
                    if nf:
                        v.tensor_scalar(flt[:, 0:nf, :], got[:, 0:nf, :], scale, None, ALU.mult).then_inc(floats_ready, 1)
                    if IB > nf:
                        v.tensor_scalar(flt[0:n, nf:IB, :], got[0:n, nf:IB, :], scale, None, ALU.mult).then_inc(floats_ready, 1)
                for b in range(IB):
                    n = rows_in(b)
                    dve.wait_ge(turned, b + 1)
                    v.tensor_copy(src_idx[:, b * P:b * P + n], ps_src[:, 0:n])
                    v.scalar_tensor_tensor(out=dst_loc[:, b * P:b * P + n], in0=node_tile_rep[:, b * P:b * P + n],
                                           scalar=-float(P), in1=ps_sel[:, 0:n], op0=ALU.mult,
                                           op1=ALU.add).then_inc(turned_copied, 1)
                dve.wait_ge(turned_copied, IB)
                v.tensor_scalar(m_lo[:, :], dst_loc[:, :], 0.0, -BIG, ALU.is_lt, ALU.mult)
                then(v.tensor_scalar(m_hi[:, :], dst_loc[:, :], P - 0.5, -BIG, ALU.is_gt, ALU.mult))
                then(v.tensor_tensor(mask[:, :], m_lo[:, :], m_hi[:, :], ALU.add))

            nfl = 2 if IT % P and IT >= P else 1

            @block.tensor
            def _(pe):
                pe.wait_ge(below_ready, 1)
                nc.tensor.matmul(ps_small[0:NT, 0:1], below_n[:, :], ones[:, 0:1], start=True, stop=True).then_inc(step_summed, 1)
                pe.wait_ge(stepped_ready, 1)
                for b in range(IB):
                    n = rows_in(b)
                    last = nc.tensor.matmul(ps_small[0:n, 8 + b:9 + b], stepped[:, b * P:b * P + n], ones[0:NT, 0:1], start=True, stop=True)
                last.then_inc(item_ready, 1)
                for h in range(2):
                    last = nc.tensor.matmul(ps_rep[h][:, 0:IH], ones[0:NT, :], stepped[:, h * IH:(h + 1) * IH], start=True, stop=True)
                last.then_inc(rep_ready, 1)
                pe.wait_ge(floats_ready, 3 * nfl)
                for b in range(IB):
                    n = rows_in(b)
                    if b:
                        pe.wait_ge(turned_copied, b)
                    nc.tensor.transpose(ps_src[:, 0:n], src_f[0:n, b, :], ident[0:n, 0:n])
                    nc.tensor.transpose(ps_sel[:, 0:n], sel_f[0:n, b, :], ident[0:n, 0:n]).then_inc(turned, 1)

        c_keep = ctx.enter_context(ExitStack())
        assert NT * NE <= IT and TOP * NT <= IT and NB <= IT
        slot_i = src_idx[:, 0:TOP * NT].rearrange("p (k j) -> p k j", k=TOP)
        gate_w = dst_loc[:, 0:TOP * NT].rearrange("p (k j) -> p k j", k=TOP)
        logits = mask[:, 0:NT * NE].rearrange("p (j e) -> p j e", e=NE)
        block_expert = item_row[0:1, 0:NB]
        q_sb = sb("q_sb", [P, NT + 1, D], F32, c_keep)
        c_acc = c_keep.enter_context(ExitStack())
        acc = sb("acc", [P, NT + 1, UW], F32, c_acc)

        def flat(ap):
            return ap.rearrange("p j d -> p (j d)")

        with ExitStack() as c2:
            def sb2(name, shape, dt=F32):
                return sb(name, shape, dt, c2)

            def ps2(name, shape):
                return c2.enter_context(nc.psum_tensor(name, shape, F32))

            x_sb = sb2("x_sb", [P, NT, D])
            w4 = sb2("w4", [P, KD, 4 * D])
            b4 = sb2("b4", [P, 4 * D])
            stat = sb2("stat", [P, 6])
            mv = sb2("mv", [P, 2])
            vp = sb2("vp", [P, 1])
            sd = sb2("sd", [P, 1])
            r0 = sb2("r0", [P, 1])
            r1 = sb2("r1", [P, 1])
            r2 = sb2("r2", [P, 1])
            r3 = sb2("r3", [P, 1])
            rstd = sb2("rstd", [P, 1])
            xn = [sb2(f"xn{i}", [P, D]) for i in range(2)]
            xnT = [sb2(f"xnT{i}", [P, D]) for i in range(2)]
            kv_out = [sb2(f"kv_out{i}", [P, 2 * D]) for i in range(2)]
            skip_out = [sb2(f"skip_out{i}", [P, D]) for i in range(2)]
            ps_t = [ps2(f"ps_t{i}", [P, 512]) for i in range(2)]
            ps_p = [ps2(f"ps_p{i}", [P, 1024]) for i in range(2)]
            s, at, grant = counters(c2, loaded=0, ln_step=0, var_ready=0, sd_ready=0, xn_ready=0, xn_turned=2, xnT_ready=2,
                                    projected=2, q_out=2, kv_out_ready=2, skip_half=2, skip_out_ready=0, tail_zeroed=0,
                                    stored0=0, stored1=0, dve_pace=0)
            stored = [s["stored0"], s["stored1"]]
            block = c2.enter_context(nc.Block())

            def over_tiles(eng, emit):
                with eng.Fori(0, NT // 2) as g:
                    emit(g * 2, 0)
                    emit(g * 2 + 1, 1)
                if NT % 2:
                    emit(NT - 1, 0)

            @block.sync
            def _(sp):
                for i, w in enumerate((Wq, Wk, Wv, Ws)):
                    sp.dma_start(w4[:, :, i * D:(i + 1) * D], w.rearrange("(k p) n -> p k n", p=P)).then_inc(s["loaded"], 16)
                for i, b in enumerate((bq, bk, bv, bs)):
                    sp.dma_start(b4[:, i * D:(i + 1) * D],
                                 b.rearrange("(o n) -> o n", o=1).to_broadcast([P, D])).then_inc(s["loaded"], 16)
                sp.dma_start(x_sb[:, 0:NT - 1, :], x[0:(NT - 1) * P, :].rearrange("(j p) d -> p j d", p=P)).then_inc(s["loaded"], 16)
                sp.wait_ge(s["tail_zeroed"], 1)
                sp.dma_start(x_sb[0:NTAIL, NT - 1, :], x[(NT - 1) * P:N, :]).then_inc(s["loaded"], 16)

                def store(j, par):
                    sp.wait_ge(s["kv_out_ready"], at("kv_out_ready", j))
                    sp.dma_start(kv_table[bass.ds(j * P, P), :], kv_out[par][:, :]).then_inc(stored[par], 16)
                    sp.wait_ge(s["skip_out_ready"], at("skip_out_ready", j))
                    sp.dma_start(skip_table[bass.ds(j * P, P), :], skip_out[par][:, :]).then_inc(stored[par], 16)

                over_tiles(sp, store)
                sp.wait_ge(stored[0], 32 * ceil_div(NT, 2))
                sp.wait_ge(stored[1], 32 * (NT // 2))

            @block.scalar
            def _(act):
                grant(act, "xnT_ready")
                act_pace = s["dve_pace"]

                def tile(j, par):
                    act.wait_ge(s["var_ready"], at("var_ready", j))
                    act.sem_inc(act_pace, 1)
                    nc.scalar.activation(sd[:, :], vp[:, :], ACT.Sqrt).then_inc(s["sd_ready"], 1)
                    act.wait_ge(s["xn_turned"], at("xn_turned", j))
                    act.wait_ge(s["projected"], at("projected", j - 2))
                    nc.scalar.copy(xnT[par][:, :], ps_t[par][:, 0:D]).then_inc(s["xnT_ready"], 1)

                over_tiles(act, tile)

            @block.tensor
            def _(pe):
                grant(pe, "xn_turned", "projected")
                pe.wait_ge(s["loaded"], 16 * 10)

                def tile(j, par):
                    pe.wait_ge(s["xn_ready"], at("xn_ready", j))
                    pe.wait_ge(s["xnT_ready"], at("xnT_ready", j - 2))
                    for k in range(KD):
                        last = nc.tensor.transpose(ps_t[par][:, k * P:(k + 1) * P], xn[par][:, k * P:(k + 1) * P], ident[:, :])
                    last.then_inc(s["xn_turned"], 1)
                    pe.wait_ge(s["xnT_ready"], at("xnT_ready", j))
                    pe.wait_ge(s["q_out"], at("q_out", j - 2))
                    pe.wait_ge(s["kv_out_ready"], at("kv_out_ready", j - 2))
                    pe.wait_ge(s["skip_half"], at("skip_half", j - 2))
                    for h in range(2):
                        for k in range(KD):
                            last = nc.tensor.matmul(ps_p[par][:, h * 512:(h + 1) * 512], xnT[par][:, k * P:(k + 1) * P],
                                                    w4[:, k, h * 512:(h + 1) * 512], start=(k == 0), stop=(k == KD - 1))
                    last.then_inc(s["projected"], 1)

                over_tiles(pe, tile)

            LN_STEPS = 7

            @block.vector
            def _(dve):
                v = nc.vector
                grant(dve, "q_out", "kv_out_ready", "skip_half")
                v.memset(x_sb[:, NT - 1, :], 0.0).then_inc(s["tail_zeroed"], 1)
                v.memset(q_sb[:, NT, :], 0.0)
                dve.wait_ge(s["loaded"], 16 * 10)

                def layernorm(j, par):
                    n = [0]

                    def then(ins):
                        n[0] += 1
                        ins.then_inc(s["ln_step"], 1)
                        dve.wait_ge(s["ln_step"], j * LN_STEPS + n[0])
                        dve.sem_inc(s["dve_pace"], 1)

                    xj = flat(x_sb[:, :, :])[:, bass.ds(j * D, D)]
                    then(v.bn_stats(stat[:, :], xj))
                    then(v.bn_aggr(mv[:, :], stat[:, :]))
                    v.tensor_scalar(vp[:, :], mv[:, 1:2], LN_EPS, None, ALU.add).then_inc(s["var_ready"], 1)
                    dve.wait_ge(s["sd_ready"], at("sd_ready", j))
                    then(v.reciprocal(r0[:, :], sd[:, :]))
                    then(v.tensor_tensor(r1[:, :], r0[:, :], r0[:, :], ALU.mult))
                    then(v.tensor_tensor(r2[:, :], r1[:, :], vp[:, :], ALU.mult))
                    then(v.tensor_scalar(r3[:, :], r2[:, :], -0.5, 1.5, ALU.mult, ALU.add))
                    then(v.tensor_tensor(rstd[:, :], r0[:, :], r3[:, :], ALU.mult))
                    assert n[0] == LN_STEPS
                    dve.wait_ge(s["xn_turned"], at("xn_turned", j - 2))
                    v.tensor_scalar(xn[par][:, :], xj, mv[:, 0:1], rstd[:, 0:1], ALU.subtract, ALU.mult).then_inc(s["xn_ready"], 1)

                def evacuate(j, par, first=False):
                    if not first:
                        dve.wait_ge(stored[par], (j - par) * 16)
                    dve.wait_ge(s["projected"], at("projected", j))
                    v.tensor_tensor(kv_out[par][:, :], ps_p[par][:, D:3 * D], b4[:, D:3 * D], ALU.add).then_inc(s["kv_out_ready"], 1)
                    v.tensor_tensor(skip_out[par][:, :], ps_p[par][:, 3 * D:4 * D], b4[:, 3 * D:4 * D], ALU.add).then_inc(s["skip_half"], 1)
                    v.tensor_tensor(flat(q_sb[:, :, :])[:, bass.ds(j * D, D)], ps_p[par][:, 0:D], b4[:, 0:D], ALU.add).then_inc(s["q_out"], 1)
                    dve.wait_ge(s["skip_half"], at("skip_half", j))
                    v.tensor_tensor(skip_out[par][:, :], skip_out[par][:, :], flat(x_sb[:, :, :])[:, bass.ds(j * D, D)],
                                    ALU.add).then_inc(s["skip_out_ready"], 1)

                layernorm(0, 0)
                layernorm(1, 1)
                evacuate(0, 0, True)
                layernorm(2, 0)
                evacuate(1, 1, True)
                pairs = (NT - 3) // 2
                with dve.Fori(0, pairs) as g:
                    layernorm(g * 2 + 3, 1)
                    evacuate(g * 2 + 2, 0)
                    layernorm(g * 2 + 4, 0)
                    evacuate(g * 2 + 3, 1)
                for j in range(2 * pairs + 2, NT):
                    if j + 1 < NT:
                        layernorm(j + 1, (j + 1) % 2)
                    evacuate(j, j % 2)

        with ExitStack() as c3:
            def sb3(name, shape, dt=F32):
                return sb(name, shape, dt, c3)

            def ps3(name, shape):
                return c3.enter_context(nc.psum_tensor(name, shape, F32))

            KW = 2 * P + H
            we_sb = sb3("we_sb", [P, KD, D])
            a_ring = sb3("a_ring", [P, N_A, D])
            kv_ring = sb3("kv_ring", [P, N_KV, 2 * D])
            aT = [sb3(f"aT{i}", [P, D + P]) for i in range(2)]
            kq = [sb3(f"kq{i}", [P, D]) for i in range(2)]
            kqq = [sb3(f"kqq{i}", [P, D]) for i in range(2)]
            ve = sb3("ve", [P, 2, CH, UW])
            sel = sb3("sel", [P, 2, CH, P])
            alpha = [sb3(f"alpha{i}", [P, P]) for i in range(2)]
            w_ring = sb3("w_ring", [P, N_W, UW])
            idx_c = sb3("idx_c", [P, 2, CH], I32)
            apart = [sb3(f"apart{i}", [P, P]) for i in range(2)]
            run_c = [sb3(f"run_c{i}", [P, P]) for i in range(2)]
            ea = [sb3(f"ea{i}", [P, P]) for i in range(2)]
            head_i = sb3("head_i", [P, 1], I32)
            head_m = sb3("head_m", [P, 1], I32)
            pp8_i = sb3("pp8_i", [P, 1], I32)
            head = sb3("head", [P, 1])
            part8 = sb3("part8", [P, 1])
            am = sb3("am", [P, P])
            resets = sb3("resets", [P, P + 1])
            off_first = sb3("off_first", [P, P])
            off_last = sb3("off_last", [P, P])
            key_f = sb3("key_f", [P, 1])
            key_l = sb3("key_l", [P, 1])
            key_prev = sb3("key_prev", [P, 1])
            max_prev = sb3("max_prev", [P, 1])
            diag_k = sb3("diag_k", [P, KW])
            diag_r = sb3("diag_r", [P, KW])
            diag_f = sb3("diag_f", [P, H])
            not_f = sb3("not_f", [P, KW])
            not_l = sb3("not_l", [P, KW])
            scan_f = sb3("scan_f", [P, P])
            scan_b = sb3("scan_b", [P, P])
            max_f = sb3("max_f", [P, 1])
            max_l = sb3("max_l", [P, 1])
            shifted = am
            keys2 = sb3("keys2", [P, 2])
            same = sb3("same", [P, 1])
            node_key = sb3("node_key", [P, 1])
            pick = sb3("pick", [P, 1])
            unpick = sb3("unpick", [P, 1])
            carry = sb3("carry", [P, H])
            carry_d = sb3("carry_d", [P, H])
            carry_e = sb3("carry_e", [P, H])
            factor = sb3("factor", [P, H])
            ps_t = [ps3(f"ps_t3{i}", [P, 512]) for i in range(2)]
            ps_e = [ps3(f"ps_e{i}", [P, 512]) for i in range(2)]
            ps_u = [ps3(f"ps_u{i}", [P, 512]) for i in range(2)]
            ps_ak = ps3("ps_ak", [P, 512])
            ps_rx = ps3("ps_rx", [P, 512])
            ps_a, ps_k = ps_ak[:, 0:P], ps_ak[:, P:P + KW]
            ps_r, ps_x, ps_f = ps_rx[:, 0:KW], ps_rx[:, KW:KW + P], ps_rx[:, KW + P:KW + P + H]

            s, at, grant = counters(c3, a_turned=N_A, aT_ready=2, e_ready=2, ke_added=0, ve_added=N_KV, kq_ready=2,
                                    alpha_ready=0, apart_ready=0, sel_ready=0, weighted=2 * CH, summed=2 * CH, acc_added=2,
                                    idx_copied=0, am_ready=0, am_turned=0, keyed=0, r_ready=0,
                                    max_spread=0, f_ready=0, shifted_ready=0, shifted_turned=1, ea_ready=0, rescaled=2,
                                    carry_ready=0, carry_exp=0, factor_ready=0, softmax_done=2,
                                    const_loaded=0, iotas=0, setup=0, sm_step=0,
                                    act_pace=0, pool_pace=0, softmax_pace=0)
            a_loaded = [sem(f"a_loaded{i}", c3) for i in range(N_A)]
            kv_loaded = [sem(f"kv_loaded{i}", c3) for i in range(N_KV)]
            run_loaded = [sem(f"run_loaded{i}", c3) for i in range(2)]
            block = c3.enter_context(nc.Block())

            FIRST_WEIGH = 11
            LAG = dict(weigh=FIRST_WEIGH + N_KV,
                       sum=FIRST_WEIGH + 2,
                       add=FIRST_WEIGH + 2)
            assert max(LAG.values()) < CH

            def plan(scores=True, softmax=True, new=True, old=True, parts={}, what=None):
                out = []
                for i in range(CH):
                    if scores:
                        out.append(("score", i, 0))
                    if softmax and i in parts:
                        out.append((parts[i], i, 1))
                    k = i - LAG.get(what, 0)
                    if what and k >= 0 and new:
                        out.append((what, k, 1))
                    elif what and k < 0 and old:
                        out.append((what, k + CH, 2))
                return out

            def by_head(ap, width):
                return ap.rearrange("p (h c) -> p h c", c=width)

            def over_chunks(eng, emit, **kw):
                emit(0, 0, plan(softmax=False, new=False, old=False, **kw))
                emit(1, 1, plan(old=False, **kw))
                pairs = (NCH - 2) // 2
                with eng.Fori(0, pairs) as g:
                    emit(g * 2 + 2, 0, plan(**kw))
                    emit(g * 2 + 3, 1, plan(**kw))
                for c in range(2 + 2 * pairs, NCH):
                    emit(c, c % 2, plan(**kw))
                emit(NCH, NCH % 2, plan(scores=False, **kw))
                emit(NCH + 1, (NCH + 1) % 2, plan(scores=False, softmax=False, new=False, **kw))

            @block.sync
            def _(sp):
                sp.dma_start(we_sb[:, :, :], We.rearrange("(k p) n -> p k n", p=P)).then_inc(s["const_loaded"], 16)

                def load(c, par, steps):
                    for kind, i, back in steps:
                        if kind != "score":
                            continue
                        if i == 0:
                            sp.wait_ge(s["softmax_done"], at("softmax_done", c - 2))
                            sp.dma_start(run_c[par][:, :],
                                         run_table[bass.ds(c * CH, CH), :, :].rearrange("i h e -> (i h) e")).then_inc(run_loaded[par], 16)
                        row = sp.value_load(item_row[0:1, bass.ds(c * CH + i, 1)], min_val=0, max_val=E - P)
                        sp.wait_ge(s["a_turned"], at("a_turned", c * CH + (i - N_A)))
                        sp.dma_start(a_ring[:, i % N_A, :], edge_attr[bass.ds(row, P), :]).then_inc(a_loaded[i % N_A], 16)

                over_chunks(sp, load)

            @block.gpsimd
            def _(pool):
                g = nc.gpsimd
                grant(pool, "weighted")
                g.iota(pp8_i[:, :], [[1, 1]], base=0, channel_multiplier=H).then_inc(s["iotas"], 1)
                g.iota(head_i[:, :], [[1, 1]], base=0, channel_multiplier=1).then_inc(s["iotas"], 1)

                def gather(c, par, i):
                    if i == 0:
                        g.tensor_copy(idx_c[:, par, :], src_idx[:, bass.ds(c * CH, CH)]).then_inc(s["idx_copied"], 1)
                        pool.wait_ge(s["idx_copied"], at("idx_copied", c))
                        pool.sem_inc(s["pool_pace"], 1)
                    pool.wait_ge(s["ve_added"], at("ve_added", c * CH + (i - N_KV)))
                    pool.sem_inc(s["pool_pace"], 1)
                    g.indirect_dma_start(out=kv_ring[:, i % N_KV, :], out_offset=None, in_=kv_table,
                                         in_offset=bass.IndirectOffsetOnAxis(ap=idx_c[:, par, i:i + 1], axis=0)
                                         ).then_inc(kv_loaded[i % N_KV], 16)

                def weigh(c, par, i):
                    m = c * CH + i
                    if i == 0:
                        pool.wait_ge(s["ea_ready"], at("ea_ready", c))
                        pool.sem_inc(s["pool_pace"], 1)
                    pool.wait_ge(s["summed"], at("summed", m - N_W))
                    g.tensor_tensor(by_head(w_ring[:, i % N_W, :], CP), by_head(ve[:, par, i, :], CP),
                                    ea[par][:, i * H:(i + 1) * H][:, :, None].to_broadcast([P, H, CP]),
                                    ALU.mult).then_inc(s["weighted"], 1)

                def emit(c, par, steps):
                    held = None
                    for kind, i, back in steps + [("end", 0, 0)]:
                        if kind == "weigh":
                            weigh(c - back, (par + back) % 2, i)
                        if held is not None:
                            gather(c, par, held)
                        held = i if kind == "score" else None

                over_chunks(pool, emit, what="weigh")

            @block.scalar
            def _(act):
                grant(act, "aT_ready")

                def select(c, par, i):
                    act.wait_ge(s["summed"], at("summed", c * CH + (i - 2 * CH)))
                    act.sem_inc(s["act_pace"], 1)
                    nc.scalar.activation(apart[i % 2][:, :], iota_free[:, :], ACT.Abs, scale=-1.0,
                                         bias=dst_loc[:, bass.ds(c * CH + i, 1)]).then_inc(s["apart_ready"], 1)
                    act.wait_ge(s["apart_ready"], at("apart_ready", c * CH + i))
                    act.sem_inc(s["act_pace"], 1)
                    nc.scalar.activation(sel[:, par, i, :], apart[i % 2][:, :], ACT.Relu, scale=-1.0,
                                         bias=1.0).then_inc(s["sel_ready"], 1)

                AHEAD = 2

                def emit(c, par, steps):
                    for kind, i, back in steps:
                        if kind == "score":
                            if isinstance(c, int) and c == 0 and i == 0:
                                for k in range(AHEAD):
                                    select(c, par, k)
                            act.wait_ge(s["a_turned"], at("a_turned", c * CH + i))
                            act.wait_ge(s["e_ready"], at("e_ready", c * CH + (i - 2)))
                            nc.scalar.copy(aT[i % 2][:, :], ps_t[i % 2][:, 0:D + P]).then_inc(s["aT_ready"], 1)
                            if i + AHEAD < CH:
                                select(c, par, i + AHEAD)
                            elif not (isinstance(c, int) and c == NCH - 1):
                                select(c + 1, 1 - par, i + AHEAD - CH)
                        elif kind == "exp":
                            act.wait_ge(s["weighted"], at("weighted", (c - 2) * CH - 1))
                            act.sem_inc(s["act_pace"], 1)
                            act.wait_ge(s["shifted_turned"], at("shifted_turned", c - 1))
                            act.sem_inc(s["act_pace"], 1)
                            nc.scalar.activation(ea[1 - par][:, :], ps_x, ACT.Exp).then_inc(s["ea_ready"], 1)
                        elif kind == "carry_exp":
                            act.wait_ge(s["carry_ready"], at("carry_ready", c - 1))
                            act.sem_inc(s["act_pace"], 1)
                            nc.scalar.activation(carry_e[:, :], carry_d[:, :], ACT.Exp).then_inc(s["carry_exp"], 1)

                over_chunks(act, emit, parts={12: "exp", 15: "carry_exp"})

            @block.tensor
            def _(pe):
                t = nc.tensor
                grant(pe, "a_turned", "e_ready", "summed", "shifted_turned")
                pe.wait_ge(s["const_loaded"], 16)

                def turn(c, par, i):
                    pe.wait_ge(a_loaded[i % N_A], c * (16 * CH // N_A) + 16 * (i // N_A + 1))
                    pe.wait_ge(s["sel_ready"], at("sel_ready", c * CH + i))
                    pe.wait_ge(s["aT_ready"], at("aT_ready", c * CH + (i - 2)))
                    for k in range(KD):
                        t.transpose(ps_t[i % 2][:, k * P:(k + 1) * P], a_ring[:, i % N_A, k * P:(k + 1) * P], ident[:, :])
                    t.transpose(ps_t[i % 2][:, D:D + P], sel[:, par, i, :], ident[:, :]).then_inc(s["a_turned"], 1)

                def node_tile_of(c, i):
                    return pe.value_load(item_node_tile[0:1, bass.ds(c * CH + i, 1)], min_val=0, max_val=NT)

                def project(c, i, n):
                    pe.wait_ge(s["aT_ready"], at("aT_ready", c * CH + i))
                    pe.wait_ge(s["ve_added"], at("ve_added", c * CH + (i - 2)))
                    pe.wait_ge(s["kq_ready"], at("kq_ready", c * CH + (i - 2)))
                    for k in range(KD):
                        t.matmul(ps_e[i % 2][:, 0:D], aT[i % 2][:, k * P:(k + 1) * P], we_sb[:, k, :], start=(k == 0), stop=(k == KD - 1))
                    t.matmul(ps_e[i % 2][:, D:2 * D], aT[i % 2][:, D:D + P], flat(q_sb[:, :, :])[:, bass.ds(n * D, D)],
                             start=True, stop=True).then_inc(s["e_ready"], 1)

                def emit(c, par, steps):
                    n = node_tile_of(c, 0) if steps[0][0] == "score" else None
                    for kind, i, back in steps:
                        if kind == "score":
                            if isinstance(c, int) and c == 0 and i == 0:
                                turn(c, par, 0)
                            if i + 1 < CH:
                                turn(c, par, i + 1)
                            elif not (isinstance(c, int) and c == NCH - 1):
                                turn(c + 1, 1 - par, 0)
                            project(c, i, n)
                            if i + 1 < CH:
                                n = node_tile_of(c, i + 1)
                        elif kind == "keys":
                            pe.wait_ge(s["keyed"], at("keyed", c - 1))
                            t.matmul(ps_k, ones[:, :], diag_k[:, :], start=True, stop=True)
                            pe.wait_ge(s["am_ready"], at("am_ready", c - 1))
                            t.transpose(ps_a, am[:, :], ident[:, :]).then_inc(s["am_turned"], 1)
                        elif kind == "maxima":
                            pe.wait_ge(s["r_ready"], at("r_ready", c - 1))
                            t.matmul(ps_r, ones[:, :], diag_r[:, :], start=True, stop=True).then_inc(s["max_spread"], 1)
                        elif kind == "turn_scores":
                            pe.wait_ge(s["f_ready"], at("f_ready", c - 1))
                            t.matmul(ps_f, ones[:, :], diag_f[:, :], start=True, stop=True)
                            pe.wait_ge(s["shifted_ready"], at("shifted_ready", c - 1))
                            t.transpose(ps_x, shifted[:, :], ident[:, :]).then_inc(s["shifted_turned"], 1)
                        elif kind == "sum":
                            m = (c - back) * CH + i
                            pe.wait_ge(s["weighted"], at("weighted", m))
                            pe.wait_ge(s["acc_added"], at("acc_added", m - 2))
                            t.matmul(ps_u[i % 2][:, 0:UW], sel[:, (par + back) % 2, i, :], w_ring[:, i % N_W, :],
                                     start=True, stop=True).then_inc(s["summed"], 1)

                over_chunks(pe, emit, what="sum", parts={3: "keys", 6: "maxima", 11: "turn_scores"})

            @block.vector
            def _(dve):
                v = nc.vector
                grant(dve, "ve_added", "kq_ready", "acc_added", "rescaled", "softmax_done")
                v.memset(acc[:, :, :], 0.0).then_inc(s["setup"], 1)
                v.memset(ve[:, :, :, :], 1.0).then_inc(s["setup"], 1)
                v.memset(resets[:, :], 0.0).then_inc(s["setup"], 1)
                v.memset(max_prev[:, :], -BIG).then_inc(s["setup"], 1)
                v.memset(key_prev[:, :], -1.0).then_inc(s["setup"], 1)
                dve.wait_ge(s["iotas"], 2)
                v.tensor_scalar(head_m[:, :], head_i[:, :], H - 1, None, ALU.bitwise_and).then_inc(s["setup"], 1)
                v.tensor_copy(part8[:, :], pp8_i[:, :]).then_inc(s["setup"], 1)
                dve.wait_ge(s["setup"], 7)
                v.tensor_copy(head[:, :], head_m[:, :]).then_inc(s["setup"], 1)
                dve.wait_ge(s["setup"], 8)

                def reduce(c, par, i):
                    dve.wait_ge(s["kq_ready"], at("kq_ready", c * CH + i))
                    v.tensor_reduce(alpha[par][:, i * H:(i + 1) * H], by_head(kqq[i % 2][:, :], C), AX_X,
                                    ALU.add).then_inc(s["alpha_ready"], 1)

                def score(c, par, i):
                    e = ps_e[i % 2][:, 0:D]
                    kv = kv_ring[:, i % N_KV, :]
                    dve.wait_ge(s["e_ready"], at("e_ready", c * CH + i))
                    dve.wait_ge(kv_loaded[i % N_KV], c * (16 * CH // N_KV) + 16 * (i // N_KV + 1))
                    v.tensor_tensor(kq[i % 2][:, :], kv[:, 0:D], e, ALU.add).then_inc(s["ke_added"], 1)
                    v.tensor_tensor(by_head(ve[:, par, i, :], CP)[:, :, 0:C], by_head(kv[:, D:2 * D], C), by_head(e, C),
                                    ALU.add).then_inc(s["ve_added"], 1)
                    if i:
                        reduce(c, par, i - 1)
                    dve.wait_ge(s["ke_added"], at("ke_added", c * CH + i))
                    v.tensor_tensor(kqq[i % 2][:, :], kq[i % 2][:, :], ps_e[i % 2][:, D:2 * D], ALU.mult).then_inc(s["kq_ready"], 1)
                    if i == CH - 1:
                        reduce(c, par, i)


                SM = dict(mask=2, keys=2, runs=3, scan=2, spread=2, not_key=2, own_max=5, run_max=2, own_off=4, shift=4, carry=0)
                SM_BEFORE = {k: sum(list(SM.values())[:j]) for j, k in enumerate(SM)}
                SM_ALL = sum(SM.values())

                def softmax(c, par, part):
                    n = [0]

                    def step(ins):
                        n[0] += 1
                        ins.then_inc(s["sm_step"], 1)

                    def settle():
                        dve.wait_ge(s["sm_step"], (c - 1) * SM_ALL + (SM_BEFORE[part] + n[0]))

                    run = run_c[1 - par]
                    if part == "mask":
                        dve.wait_ge(s["alpha_ready"], at("alpha_ready", c * CH - 1))
                        v.scalar_tensor_tensor(out=by_head(am[:, :], H), in0=by_head(alpha[1 - par][:, :], H), scalar=SCALE,
                                               in1=mask[:, bass.ds((c - 1) * CH, CH)][:, :, None].to_broadcast([P, CH, H]),
                                               op0=ALU.mult, op1=ALU.add).then_inc(s["am_ready"], 1)
                        dve.wait_ge(run_loaded[1 - par], (c - (2 - par)) * 8 + 16)
                        step(v.tensor_scalar(key_f[:, :], run[:, 0:1], H / BIG, head[:, 0:1], ALU.mult, ALU.add))
                        step(v.tensor_scalar(key_l[:, :], run[:, P - 1:P], H / BIG, head[:, 0:1], ALU.mult, ALU.add))
                    elif part == "keys":
                        settle()
                        step(v.tensor_scalar(diag_k[:, 0:P], ident[:, :], key_f[:, 0:1], None, ALU.mult))
                        step(v.tensor_scalar(diag_k[:, P:2 * P], ident[:, :], key_l[:, 0:1], None, ALU.mult))
                        v.tensor_scalar(diag_k[:, 2 * P:], ident[:, P - H:P], key_prev[:, 0:1], None, ALU.mult).then_inc(s["keyed"], 1)
                    elif part == "runs":
                        step(v.tensor_tensor(resets[:, 1:P], run[:, 0:P - 1], run[:, 1:P], ALU.subtract))
                        step(v.tensor_scalar(off_first[:, :], run[:, :], run[:, 0:1], -1.0, ALU.subtract, ALU.mult))
                        step(v.tensor_scalar(off_last[:, :], run[:, :], run[:, P - 1:P], None, ALU.subtract))
                    elif part == "scan":
                        dve.wait_ge(s["am_turned"], at("am_turned", c - 1))
                        settle()
                        step(v.tensor_tensor_scan(out=scan_f[:, :], data0=resets[:, 0:P], data1=ps_a, initial=-BIG, op0=ALU.add, op1=ALU.max))
                        settle()
                        step(v.tensor_tensor_scan(out=scan_b[:, ::-1], data0=resets[:, P:0:-1], data1=scan_f[:, ::-1], initial=-BIG,
                                                  op0=ALU.add, op1=ALU.max))
                    elif part == "spread":
                        step(v.tensor_scalar(diag_r[:, P:2 * P], ident[:, :], scan_f[:, P - 1:P], None, ALU.mult))
                        step(v.tensor_scalar(diag_r[:, 2 * P:], ident[:, P - H:P], max_prev[:, 0:1], None, ALU.mult))
                        settle()
                        v.tensor_scalar(diag_r[:, 0:P], ident[:, :], scan_b[:, 0:1], None, ALU.mult).then_inc(s["r_ready"], 1)
                    elif part == "not_key":
                        step(v.tensor_scalar(not_f[:, :], ps_k, key_f[:, 0:1], -BIG, ALU.not_equal, ALU.mult))
                        step(v.tensor_scalar(not_l[:, :], ps_k, key_l[:, 0:1], -BIG, ALU.not_equal, ALU.mult))
                    elif part == "own_max":
                        step(v.tensor_copy(keys2[:, 0:1], ps_k[:, 0:1]))
                        step(v.tensor_copy(keys2[:, 1:2], ps_k[:, 2 * P:2 * P + 1]))
                        dve.wait_ge(s["max_spread"], at("max_spread", c - 1))
                        settle()
                        step(v.tensor_copy(carry[:, :], ps_r[:, 2 * P:]))
                        step(v.tensor_tensor(not_f[:, :], not_f[:, :], ps_r, ALU.add))
                        step(v.tensor_tensor(not_l[:, :], not_l[:, :], ps_r, ALU.add))
                    elif part == "run_max":
                        settle()
                        step(v.tensor_reduce(max_f[:, :], not_f[:, :], AX_X, ALU.max))
                        step(v.tensor_reduce(max_l[:, :], not_l[:, :], AX_X, ALU.max))
                        settle()
                        v.tensor_scalar(diag_f[:, :], ident[:, 0:H], max_f[:, 0:1], None, ALU.mult).then_inc(s["f_ready"], 1)
                    elif part == "own_off":
                        step(v.scalar_tensor_tensor(out=scan_b[:, :], in0=off_first[:, :], scalar=max_f[:, 0:1], in1=scan_b[:, :],
                                                    op0=ALU.add, op1=ALU.max))
                        step(v.tensor_tensor(same[:, :], keys2[:, 0:1], keys2[:, 1:2], ALU.is_equal))
                        step(v.tensor_scalar(node_key[:, :], chunk_tile[:, bass.ds(c - 1, 1)], float(P * H), part8[:, 0:1],
                                             ALU.mult, ALU.add))
                        settle()
                        step(v.scalar_tensor_tensor(out=off_last[:, :], in0=off_last[:, :], scalar=max_l[:, 0:1], in1=scan_b[:, :],
                                                    op0=ALU.add, op1=ALU.max))
                    elif part == "shift":
                        settle()
                        dve.wait_ge(s["shifted_turned"], at("shifted_turned", c - 2))
                        v.tensor_tensor(shifted[:, :], ps_a, off_last[:, :], ALU.subtract).then_inc(s["shifted_ready"], 1)
                        step(v.tensor_scalar(pick[:, :], node_key[:, :], keys2[:, 0:1], same[:, 0:1], ALU.is_equal, ALU.mult))
                        step(v.tensor_copy(max_prev[:, :], max_l[:, :]))
                        step(v.tensor_copy(key_prev[:, :], key_l[:, :]))
                        settle()
                        step(v.tensor_scalar(unpick[:, :], pick[:, :], -1.0, 1.0, ALU.mult, ALU.add))
                    else:
                        dve.wait_ge(s["ea_ready"], at("ea_ready", c - 1))
                        v.tensor_tensor(carry_d[:, :], carry[:, :], ps_f, ALU.subtract).then_inc(s["carry_ready"], 1)
                        dve.sem_inc(s["softmax_done"], 1)
                    assert n[0] == SM[part], (part, n[0])

                def rescale(c):
                    dve.wait_ge(s["carry_exp"], at("carry_exp", c))
                    v.tensor_scalar(factor[:, :], carry_e[:, :], pick[:, 0:1], unpick[:, 0:1], ALU.mult, ALU.add).then_inc(s["factor_ready"], 1)
                    n0 = dve.value_load(item_node_tile[0:1, bass.ds(c * CH, 1)], min_val=0, max_val=NT)
                    a = by_head(flat(acc[:, :, :])[:, bass.ds(n0 * UW, UW)], CP)
                    dve.wait_ge(s["factor_ready"], at("factor_ready", c))
                    dve.wait_ge(s["acc_added"], at("acc_added", c * CH - 1))
                    v.tensor_tensor(a, a, factor[:, :, None].to_broadcast([P, H, CP]), ALU.mult).then_inc(s["rescaled"], 1)
                    dve.wait_ge(s["rescaled"], at("rescaled", c))
                    dve.sem_inc(s["softmax_pace"], 1)

                def node_tile_of(c, i):
                    return dve.value_load(item_node_tile[0:1, bass.ds(c * CH + i, 1)], min_val=0, max_val=NT)

                def add(c, i, n):
                    m = c * CH + i
                    a = flat(acc[:, :, :])[:, bass.ds(n * UW, UW)]
                    dve.wait_ge(s["summed"], at("summed", m))
                    dve.wait_ge(s["acc_added"], at("acc_added", m - 1))
                    v.tensor_tensor(a, a, ps_u[i % 2][:, 0:UW], ALU.add).then_inc(s["acc_added"], 1)

                def emit(c, par, steps):
                    n = None
                    for at_step, (kind, i, back) in enumerate(steps):
                        if kind == "score":
                            for later, k, b in steps[at_step + 1:at_step + 3]:
                                if later == "add":
                                    n = node_tile_of(c - b, k)
                                elif later == "score":
                                    break
                            score(c, par, i)
                        elif kind in SM:
                            softmax(c, par, kind)
                        elif kind == "add":
                            if i == 0:
                                rescale(c - back)
                            add(c - back, i, n if n is not None else node_tile_of(c - back, i))
                            n = None

                parts = {i: k for i, k in enumerate(list(SM)[:-1])}
                over_chunks(dve, emit, what="add", parts={**parts, FIRST_WEIGH + 1: "carry"})

        x1 = q_sb
        xn2 = acc
        with ExitStack() as c4:
            def sb4(name, shape, dt=F32):
                return sb(name, shape, dt, c4)

            wg_sb = sb4("wg_sb", [P, KD, NE])
            bg_sb = sb4("bg_sb", [P, NE])
            gb_sb = sb4("gb_sb", [P, NE])
            bias_sb = sb4("bias_sb", [P, NE])
            zeros = sb4("zeros", [P, 5 * D])
            skip = [sb4(f"skip{i}", [P, D]) for i in range(2)]
            den = sb4("den", [P, H])
            inv = sb4("inv", [P, H])
            att = sb4("att", [P, D])
            stat = sb4("stat4", [P, 6])
            mv = sb4("mv4", [P, 2])
            vp = sb4("vp4", [P, 1])
            sd = sb4("sd4", [P, 1])
            r0 = sb4("r04", [P, 1])
            r1 = sb4("r14", [P, 1])
            r2 = sb4("r24", [P, 1])
            r3 = sb4("r34", [P, 1])
            rstd = sb4("rstd4", [P, 1])
            xnT = [sb4(f"xnT4{i}", [P, D]) for i in range(2)]
            xnc = [sb4(f"xnc{i}", [P, D]) for i in range(2)]
            ps_t = [c4.enter_context(nc.psum_tensor(f"ps_t4{i}", [P, 512], F32)) for i in range(2)]
            ps_g = [c4.enter_context(nc.psum_tensor(f"ps_g4{i}", [P, 512], F32)) for i in range(2)]
            s, at, grant = counters(c4, loaded=0, zero_set=0, zeroed=0, skip_free=2, ln_step=0, var_ready=0, sd_ready=0,
                                    xn_ready=0, xn_turned=2, xn_kept=2, xnT_ready=2, gated=2, logits_ready=2, act_pace=0, dve_pace=0,
                                    bias_ready=0)
            skip_loaded = [sem(f"skip_loaded{i}", c4) for i in range(2)]
            block = c4.enter_context(nc.Block())

            def over_tiles4(eng, emit):
                with eng.Fori(0, NT // 2) as g:
                    emit(g * 2, 0)
                    emit(g * 2 + 1, 1)
                if NT % 2:
                    emit(NT - 1, 0)

            ZR = 5
            NZ = ceil_div(NB, ZR)

            @block.sync
            def _(sp):
                sp.dma_start(wg_sb[:, :, :], Wg.rearrange("(k p) n -> p k n", p=P)).then_inc(s["loaded"], 16)
                sp.dma_start(bg_sb[:, :], bg.rearrange("(o n) -> o n", o=1).to_broadcast([P, NE])).then_inc(s["loaded"], 16)
                sp.dma_start(gb_sb[:, :], gbias.rearrange("(o n) -> o n", o=1).to_broadcast([P, NE])).then_inc(s["loaded"], 16)

                def load(j, par):
                    sp.wait_ge(s["skip_free"], at("skip_free", j - 2))
                    sp.dma_start(skip[par][:, :], skip_table[bass.ds(j * P, P), :]).then_inc(skip_loaded[par], 16)

                over_tiles4(sp, load)
                sp.wait_ge(s["zero_set"], 1)
                zr = sorted_x.rearrange("(p r) d -> p (r d)", p=P)
                for z in range(NZ):
                    w = min(ZR, NB - z * ZR) * D
                    sp.dma_start(zr[:, z * ZR * D:z * ZR * D + w], zeros[:, 0:w]).then_inc(s["zeroed"], 16)
                sp.wait_ge(s["zeroed"], 16 * NZ)

            @block.scalar
            def _(act):
                grant(act, "xnT_ready", "xn_kept")

                def tile(j, par):
                    act.wait_ge(s["var_ready"], at("var_ready", j))
                    act.sem_inc(s["act_pace"], 1)
                    nc.scalar.activation(sd[:, :], vp[:, :], ACT.Sqrt).then_inc(s["sd_ready"], 1)
                    act.wait_ge(s["xn_ready"], at("xn_ready", j))
                    nc.scalar.copy(flat(xn2[:, :, :])[:, bass.ds(j * UW, D)], xnc[par][:, :]).then_inc(s["xn_kept"], 1)
                    act.wait_ge(s["xn_turned"], at("xn_turned", j))
                    act.wait_ge(s["gated"], at("gated", j - 2))
                    nc.scalar.copy(xnT[par][:, :], ps_t[par][:, 0:D]).then_inc(s["xnT_ready"], 1)

                over_tiles4(act, tile)

            @block.tensor
            def _(pe):
                grant(pe, "gated", "xn_turned")
                pe.wait_ge(s["loaded"], 16 * 3)

                def tile(j, par):
                    pe.wait_ge(s["xn_ready"], at("xn_ready", j))
                    pe.wait_ge(s["xnT_ready"], at("xnT_ready", j - 2))
                    for k in range(KD):
                        last = nc.tensor.transpose(ps_t[par][:, k * P:(k + 1) * P], xnc[par][:, k * P:(k + 1) * P], ident[:, :])
                    last.then_inc(s["xn_turned"], 1)
                    pe.wait_ge(s["xnT_ready"], at("xnT_ready", j))
                    pe.wait_ge(s["logits_ready"], at("logits_ready", j - 2))
                    for k in range(KD):
                        last = nc.tensor.matmul(ps_g[par][:, 0:NE], xnT[par][:, k * P:(k + 1) * P], wg_sb[:, k, :],
                                                start=(k == 0), stop=(k == KD - 1))
                    last.then_inc(s["gated"], 1)

                over_tiles4(pe, tile)

            LN_STEPS = 10

            @block.vector
            def _(dve):
                v = nc.vector
                grant(dve, "skip_free", "logits_ready")
                v.memset(zeros[:, :], 0.0).then_inc(s["zero_set"], 1)
                dve.wait_ge(s["loaded"], 16 * 3)
                v.tensor_tensor(bias_sb[:, :], bg_sb[:, :], gb_sb[:, :], ALU.add).then_inc(s["bias_ready"], 1)
                dve.wait_ge(s["bias_ready"], 1)

                def node_tile(j, par):
                    n = [0]

                    def then(ins):
                        n[0] += 1
                        ins.then_inc(s["ln_step"], 1)
                        dve.wait_ge(s["ln_step"], j * LN_STEPS + n[0])
                        dve.sem_inc(s["dve_pace"], 1)

                    u = flat(acc[:, :, :])[:, bass.ds(j * UW, UW)].rearrange("p (h c) -> p h c", c=CP)
                    xj = flat(x1[:, :, :])[:, bass.ds(j * D, D)]
                    then(v.tensor_scalar(den[:, :], u[:, :, C:CP].rearrange("p h c -> p (h c)"), 1e-16, None, ALU.add))
                    then(v.reciprocal(inv[:, :], den[:, :]))
                    then(v.tensor_tensor(att[:, :].rearrange("p (h c) -> p h c", c=C), u[:, :, 0:C],
                                         inv[:, :, None].to_broadcast([P, H, C]), ALU.mult))
                    dve.wait_ge(skip_loaded[par], (j - par) * 8 + 16)
                    v.tensor_tensor(xj, att[:, :], skip[par][:, :], ALU.add).then_inc(s["skip_free"], 1)
                    dve.wait_ge(s["skip_free"], at("skip_free", j))
                    dve.sem_inc(s["dve_pace"], 1)
                    then(v.bn_stats(stat[:, :], xj))
                    then(v.bn_aggr(mv[:, :], stat[:, :]))
                    v.tensor_scalar(vp[:, :], mv[:, 1:2], LN_EPS, None, ALU.add).then_inc(s["var_ready"], 1)
                    dve.wait_ge(s["sd_ready"], at("sd_ready", j))
                    then(v.reciprocal(r0[:, :], sd[:, :]))
                    then(v.tensor_tensor(r1[:, :], r0[:, :], r0[:, :], ALU.mult))
                    then(v.tensor_tensor(r2[:, :], r1[:, :], vp[:, :], ALU.mult))
                    then(v.tensor_scalar(r3[:, :], r2[:, :], -0.5, 1.5, ALU.mult, ALU.add))
                    then(v.tensor_tensor(rstd[:, :], r0[:, :], r3[:, :], ALU.mult))
                    assert n[0] == LN_STEPS, n[0]
                    dve.wait_ge(s["xn_turned"], at("xn_turned", j - 2))
                    dve.wait_ge(s["xn_kept"], at("xn_kept", j - 2))
                    v.tensor_scalar(xnc[par][:, :], xj, mv[:, 0:1], rstd[:, 0:1], ALU.subtract, ALU.mult).then_inc(s["xn_ready"], 1)

                def gate(j, par):
                    dve.wait_ge(s["gated"], at("gated", j))
                    v.tensor_tensor(flat(logits)[:, bass.ds(j * NE, NE)], ps_g[par][:, 0:NE], bias_sb[:, :],
                                    ALU.add).then_inc(s["logits_ready"], 1)

                node_tile(0, 0)
                with dve.Fori(0, NT // 2) as g:
                    node_tile(g * 2 + 1, 1)
                    gate(g * 2, 0)
                    node_tile(g * 2 + 2, 0)
                    gate(g * 2 + 1, 1)
                gate(NT - 1, 0)

        with ExitStack() as c5:
            def sb5(name, shape, dt=F32):
                return sb(name, shape, dt, c5)

            top8 = sb5("top8", [P, NT, 8])
            rank = sb5("rank", [P, NT, NE])
            more = sb5("more", [P, NT, NE])
            diff = sb5("diff", [P, NT])
            ex = sb5("ex", [P, NT])
            exp1 = sb5("exp1", [P, NT])
            taken = sb5("taken", [P, NT, NE])
            is_k = [sb5(f"is_k{k}", [P, NT, NE]) for k in range(TOP)]
            lower = sb5("lower", [P, P])
            totals = sb5("totals", [P, NE, NT])
            zeros_t = sb5("zeros_t", [P, NE, NT])
            running = sb5("running", [P, NE, NT])
            count_i = sb5("count_i", [P, NE], I32)
            blocks_i = sb5("blocks_i", [P, NE], I32)
            blocks = sb5("blocks", [P, NE])
            ends = sb5("ends", [P, NE])
            starts = sb5("starts", [P, NE])
            place = sb5("place", [P, NT, NE])
            place2 = sb5("place2", [P, NT, NE])
            slots = sb5("slots", [P, TOP, NT])
            bi_i = sb5("bi_i", [1, NB], I32)
            bi = sb5("bi", [1, NB])
            be = sb5("be", [1, NB])
            ps_pre = c5.enter_context(nc.psum_tensor("ps_pre", [P, 512], F32))
            ps_tot = c5.enter_context(nc.psum_tensor("ps_tot", [P, 512], F32))
            dve_step = sem("route_step", c5)
            diff_ready = sem("diff_ready", c5)
            exp_ready = sem("exp_ready", c5)
            taken_ready = sem("taken_ready", c5)
            counted = sem("counted", c5)
            bi_set = sem("bi_set", c5)
            block = c5.enter_context(nc.Block())
            assert NT * NE <= 512 and NE == 8

            @block.gpsimd
            def _(pool):
                nc.gpsimd.iota(bi_i[:, :], [[1, NB]], base=0, channel_multiplier=0).then_inc(bi_set, 1)

            @block.scalar
            def _(act):
                act.wait_ge(diff_ready, 1)
                nc.scalar.activation(ex[:, :], diff[:, :], ACT.Exp).then_inc(exp_ready, 1)

            @block.tensor
            def _(pe):
                pe.wait_ge(taken_ready, 1)
                tk = taken[:, :, :].rearrange("p j e -> p (j e)")
                nc.tensor.matmul(ps_pre[:, 0:NT * NE], lower[:, :], tk, start=True, stop=True)
                nc.tensor.matmul(ps_tot[:, 0:NT * NE], ones[:, :], tk, start=True, stop=True).then_inc(counted, 1)

            @block.vector
            def _(dve):
                v = nc.vector
                count = [0]

                def then(ins):
                    count[0] += 1
                    ins.then_inc(dve_step, 1)
                    dve.wait_ge(dve_step, count[0])

                for j in range(NT):
                    last = v.max(top8[:, j, :], logits[:, j, :])
                then(last)
                then(v.tensor_tensor(diff[:, :], top8[:, :, 1:2].rearrange("p j o -> p (j o)"),
                                     top8[:, :, 0:1].rearrange("p j o -> p (j o)"), ALU.subtract))
                dve.sem_inc(diff_ready, 1)
                then(v.memset(rank[:, :, :], 0.0))
                for f in range(NE):
                    lf = logits[:, :, f:f + 1]
                    if f:
                        v.tensor_tensor(more[:, :, 0:f], lf.to_broadcast([P, NT, f]), logits[:, :, 0:f], ALU.is_gt)
                    then(v.tensor_tensor(more[:, :, f:NE], lf.to_broadcast([P, NT, NE - f]), logits[:, :, f:NE], ALU.is_ge))
                    then(v.tensor_tensor(rank[:, :, :], rank[:, :, :], more[:, :, :], ALU.add))
                v.tensor_scalar(lower[:, :], iota_free[:, :], iota_part[:, 0:1], None, ALU.is_gt)
                v.tensor_scalar(is_k[0][:, :, :], rank[:, :, :], 1.0, None, ALU.is_equal)
                v.tensor_scalar(is_k[1][:, :, :], rank[:, :, :], 2.0, None, ALU.is_equal)
                v.tensor_scalar(taken[:, :, :], rank[:, :, :], TOP + 0.5, None, ALU.is_lt).then_inc(taken_ready, 1)
                dve.wait_ge(exp_ready, 1)
                then(v.tensor_scalar(exp1[:, :], ex[:, :], 1.0, None, ALU.add))
                then(v.reciprocal(gate_w[:, 0, :], exp1[:, :]))
                then(v.tensor_tensor(gate_w[:, 1, :], ex[:, :], gate_w[:, 0, :], ALU.mult))
                dve.wait_ge(counted, 1)
                v.memset(zeros_t[:, :, :], 0.0)
                then(v.tensor_copy(totals[:, :, :], ps_tot[:, 0:NT * NE].rearrange("p (j e) -> p e j", e=NE)))
                for e in range(NE):
                    last = v.tensor_tensor_scan(out=running[:, e, :], data0=zeros_t[:, e, :], data1=totals[:, e, :], initial=0.0,
                                                op0=ALU.add, op1=ALU.add)
                then(last)
                then(v.tensor_scalar(count_i[:, :], running[:, :, NT - 1:NT].rearrange("p e o -> p (e o)"), float(P - 1), None, ALU.add))
                then(v.tensor_scalar(blocks_i[:, :], count_i[:, :], P.bit_length() - 1, None, ALU.logical_shift_right))
                then(v.tensor_copy(blocks[:, :], blocks_i[:, :]))
                then(v.tensor_tensor_scan(out=ends[:, :], data0=zeros_t[:, :, :].rearrange("p e j -> p (e j)")[:, 0:NE], data1=blocks[:, :], initial=0.0, op0=ALU.add, op1=ALU.add))
                then(v.tensor_tensor(starts[:, :], ends[:, :], blocks[:, :], ALU.subtract))
                then(v.tensor_scalar(starts[:, :], starts[:, :], float(P), None, ALU.mult))
                then(v.tensor_tensor(place[:, :, :], running[:, :, :].rearrange("p e j -> p j e"),
                                     totals[:, :, :].rearrange("p e j -> p j e"), ALU.subtract))
                then(v.tensor_tensor(place2[:, :, :], place[:, :, :], ps_pre[:, 0:NT * NE].rearrange("p (j e) -> p j e", e=NE), ALU.add))
                then(v.tensor_tensor(place[:, :, :], place2[:, :, :], starts[:, None, :].to_broadcast([P, NT, NE]), ALU.add))
                for k in range(TOP):
                    then(v.tensor_tensor(place2[:, :, :], place[:, :, :], is_k[k][:, :, :], ALU.mult))
                    then(v.tensor_reduce(slots[:, k, :], place2[:, :, :], AX_X, ALU.add))
                v.tensor_copy(slot_i[:, :, :], slots[:, :, :])
                dve.wait_ge(bi_set, 1)
                then(v.tensor_copy(bi[:, :], bi_i[:, :]))
                then(v.memset(be[:, :], 0.0))
                for e in range(NE - 1):
                    then(v.scalar_tensor_tensor(out=be[:, :], in0=bi[:, :], scalar=ends[0:1, e:e + 1], in1=be[:, :], op0=ALU.is_ge, op1=ALU.add))
                v.tensor_copy(block_expert[:, :], be[:, :])

        with ExitStack() as c6:
            scattered = sem("scattered", c6)
            block = c6.enter_context(nc.Block())

            @block.gpsimd
            def _(pool):
                for j in range(NT):
                    for k in range(TOP):
                        nc.gpsimd.indirect_dma_start(
                            out=sorted_x, out_offset=bass.IndirectOffsetOnAxis(ap=slot_i[:, k, j:j + 1], axis=0),
                            in_=xn2[:, j, 0:D], in_offset=None).then_inc(scattered, 16)
                pool.wait_ge(scattered, 16 * NT * TOP)

        c_acc.close()

        with ExitStack() as c7:
            def sb7(name, shape, dt=F32):
                return sb(name, shape, dt, c7)

            w1_sb = sb7("w1_sb", [P, KD, NE * F])
            w2_sb = sb7("w2_sb", [P, KF, NE * D])
            b1_sb = sb7("b1_sb", [P, NE * F])
            b2_sb = sb7("b2_sb", [P, NE * D])
            t_in = [sb7(f"t_in{i}", [P, D]) for i in range(2)]
            tT = [sb7(f"tT{i}", [P, D]) for i in range(2)]
            hid = [sb7(f"hid{i}", [P, F]) for i in range(2)]
            hT = [sb7(f"hT{i}", [P, F]) for i in range(2)]
            y = [sb7(f"y{i}", [P, D]) for i in range(2)]
            ps_t = [c7.enter_context(nc.psum_tensor(f"ps_t7{i}", [P, 512], F32)) for i in range(2)]
            ps_h = [c7.enter_context(nc.psum_tensor(f"ps_h7{i}", [P, 512], F32)) for i in range(2)]
            ps_ht = [c7.enter_context(nc.psum_tensor(f"ps_ht7{i}", [P, 512], F32)) for i in range(2)]
            ps_y = [c7.enter_context(nc.psum_tensor(f"ps_y7{i}", [P, 512], F32)) for i in range(2)]
            s, at, grant = counters(c7, loaded=0, x_turned=2, tT_ready=2, h_summed=2, hid_ready=2, h_turned=2, hT_ready=2,
                                    y_summed=3, y_ready=2, act_pace=0, dve_pace=0)
            x_loaded = [sem(f"x_loaded{i}", c7) for i in range(2)]
            y_stored = [sem(f"y_stored{i}", c7) for i in range(2)]
            block = c7.enter_context(nc.Block())
            assert F == 512 and NB >= 4

            def live(k):
                return not isinstance(k, int) or 0 <= k < NB

            def over_blocks(eng, emit):
                emit(0, 0)
                emit(1, 1)
                pairs = (NB - 3) // 2
                with eng.Fori(0, pairs) as g:
                    emit(g * 2 + 2, 0)
                    emit(g * 2 + 3, 1)
                for b in range(2 + 2 * pairs, NB + 2):
                    emit(b, b % 2)

            def expert_of(eng, b):
                return eng.value_load(block_expert[0:1, bass.ds(b, 1)], min_val=0, max_val=NE - 1)

            @block.sync
            def _(sp):
                def load(b, par):
                    sp.wait_ge(s["x_turned"], at("x_turned", b - 2))
                    sp.dma_start(t_in[par][:, :], sorted_x[bass.ds(b * P, P), :]).then_inc(x_loaded[par], 16)

                load(0, 0)
                load(1, 1)
                for k in range(KD):
                    sp.dma_start(w1_sb[:, k, :].rearrange("p (e f) -> p e f", e=NE),
                                 W1[:, k * P:(k + 1) * P, :].rearrange("e p f -> p e f")).then_inc(s["loaded"], 16)
                for k in range(KF):
                    sp.dma_start(w2_sb[:, k, :].rearrange("p (e f) -> p e f", e=NE),
                                 W2[:, k * P:(k + 1) * P, :].rearrange("e p f -> p e f")).then_inc(s["loaded"], 16)
                sp.dma_start(b1_sb[:, :], b1.rearrange("(o e) f -> o (e f)", o=1).to_broadcast([P, NE * F])).then_inc(s["loaded"], 16)
                sp.dma_start(b2_sb[:, :], b2.rearrange("(o e) f -> o (e f)", o=1).to_broadcast([P, NE * D])).then_inc(s["loaded"], 16)
                with sp.Fori(0, (NB - 2) // 2) as g:
                    load(g * 2 + 2, 0)
                    load(g * 2 + 3, 1)
                if NB % 2:
                    load(NB - 1, 0)

            @block.scalar
            def _(act):
                grant(act, "tT_ready", "hT_ready")

                def turned_x(b, par):
                    act.wait_ge(s["x_turned"], at("x_turned", b))
                    act.wait_ge(s["h_summed"], at("h_summed", b - 2))
                    nc.scalar.copy(tT[par][:, :], ps_t[par][:, 0:D]).then_inc(s["tT_ready"], 1)

                def emit(b, par):
                    if isinstance(b, int) and b == 0:
                        turned_x(0, 0)
                    if live(b + 1):
                        turned_x(b + 1, 1 - par)
                    if live(b - 1):
                        act.wait_ge(s["h_turned"], at("h_turned", b - 1))
                        act.sem_inc(s["act_pace"], 1)
                        act.wait_ge(s["y_summed"], at("y_summed", b - 3))
                        act.sem_inc(s["act_pace"], 1)
                        nc.scalar.activation(hT[1 - par][:, :], ps_ht[1 - par][:, :], ACT.Relu).then_inc(s["hT_ready"], 1)
                    if live(b - 2):
                        act.wait_ge(s["y_ready"], at("y_ready", b - 2))
                        act.dma_start(sorted_y[bass.ds((b - 2) * P, P), :], y[par][:, :]).then_inc(y_stored[par], 16)

                over_blocks(act, emit)
                act.wait_ge(y_stored[0], 16 + 16 * ceil_div(NB, 2))
                act.wait_ge(y_stored[1], 16 + 16 * (NB // 2))

            @block.tensor
            def _(pe):
                t = nc.tensor
                grant(pe, "x_turned", "h_summed", "h_turned", "y_summed")

                def turn_x(b, par):
                    pe.wait_ge(x_loaded[par], (b - par) * 8 + 16)
                    pe.wait_ge(s["tT_ready"], at("tT_ready", b - 2))
                    for k in range(KD):
                        last = t.transpose(ps_t[par][:, k * P:(k + 1) * P], t_in[par][:, k * P:(k + 1) * P], ident[:, :])
                    last.then_inc(s["x_turned"], 1)

                def turn_h(b, par):
                    pe.wait_ge(s["hid_ready"], at("hid_ready", b))
                    pe.wait_ge(s["hT_ready"], at("hT_ready", b - 2))
                    for k in range(KF):
                        last = t.transpose(ps_ht[par][:, k * P:(k + 1) * P], hid[par][:, k * P:(k + 1) * P], ident[:, :])
                    last.then_inc(s["h_turned"], 1)

                def hidden(b, par, ex):
                    pe.wait_ge(s["tT_ready"], at("tT_ready", b))
                    pe.wait_ge(s["hid_ready"], at("hid_ready", b - 2))
                    for k in range(KD):
                        last = t.matmul(ps_h[par][:, :], tT[par][:, k * P:(k + 1) * P], w1_sb[:, k, bass.ds(ex * F, F)],
                                        start=(k == 0), stop=(k == KD - 1))
                    last.then_inc(s["h_summed"], 1)

                def output(b, par, ex):
                    pe.wait_ge(s["hT_ready"], at("hT_ready", b))
                    pe.wait_ge(s["y_ready"], at("y_ready", b - 2))
                    for k in range(KF):
                        last = t.matmul(ps_y[par][:, 0:D], hT[par][:, k * P:(k + 1) * P], w2_sb[:, k, bass.ds(ex * D, D)],
                                        start=(k == 0), stop=(k == KF - 1))
                    last.then_inc(s["y_summed"], 1)

                def emit(b, par):
                    ex = expert_of(pe, b) if live(b) else None
                    ex_before = expert_of(pe, b - 1) if live(b - 1) else None
                    if isinstance(b, int) and b == 0:
                        turn_x(0, 0)
                        pe.wait_ge(s["loaded"], 16 * (KD + KF + 2))
                    if live(b + 1):
                        turn_x(b + 1, 1 - par)
                    if live(b - 1):
                        turn_h(b - 1, 1 - par)
                    if live(b):
                        hidden(b, par, ex)
                    if live(b - 1):
                        output(b - 1, 1 - par, ex_before)

                over_blocks(pe, emit)

            @block.vector
            def _(dve):
                v = nc.vector
                grant(dve, "hid_ready", "y_ready")
                dve.sem_inc(y_stored[0], 16)
                dve.sem_inc(y_stored[1], 16)
                dve.wait_ge(s["loaded"], 16 * (KD + KF + 2))
                dve.sem_inc(s["dve_pace"], 1)

                def emit(b, par):
                    ex_before = expert_of(dve, b - 2) if live(b - 2) else None
                    ex = expert_of(dve, b) if live(b) else None
                    if live(b - 2):
                        dve.wait_ge(s["y_summed"], at("y_summed", b - 2))
                        dve.wait_ge(y_stored[par], (b - par) * 8)
                        v.tensor_tensor(y[par][:, :], ps_y[par][:, 0:D], b2_sb[:, bass.ds(ex_before * D, D)],
                                        ALU.add).then_inc(s["y_ready"], 1)
                    if live(b):
                        dve.wait_ge(s["h_summed"], at("h_summed", b))
                        dve.wait_ge(s["h_turned"], at("h_turned", b - 2))
                        v.tensor_tensor(hid[par][:, :], ps_h[par][:, :], b1_sb[:, bass.ds(ex * F, F)],
                                        ALU.add).then_inc(s["hid_ready"], 1)

                over_blocks(dve, emit)

        with ExitStack() as c8:
            NG = 4
            got = [[sb(f"got{k}_{i}", [P, D], F32, c8) for i in range(NG)] for k in range(TOP)]
            half = [sb(f"half{i}", [P, D], F32, c8) for i in range(2)]
            o = [sb(f"o{i}", [P, D], F32, c8) for i in range(NG)]
            g_loaded = [sem(f"g_loaded{i}", c8) for i in range(NG)]
            halved = sem("halved", c8)
            summed = sem("out_summed", c8)
            out_stored = [sem(f"out_stored{i}", c8) for i in range(NG)]
            block = c8.enter_context(nc.Block())

            @block.gpsimd
            def _(pool):
                for j in range(NT):
                    if j >= NG:
                        pool.wait_ge(summed, j - NG + 1)
                    for k in range(TOP):
                        nc.gpsimd.indirect_dma_start(
                            out=got[k][j % NG][:, :], out_offset=None, in_=sorted_y,
                            in_offset=bass.IndirectOffsetOnAxis(ap=slot_i[:, k, j:j + 1], axis=0)).then_inc(g_loaded[j % NG], 16)

            @block.vector
            def _(dve):
                for j in range(NT):
                    dve.wait_ge(g_loaded[j % NG], 32 * (j // NG + 1))
                    nc.vector.scalar_tensor_tensor(out=half[j % 2][:, :], in0=got[0][j % NG][:, :], scalar=gate_w[:, 0, j:j + 1],
                                                   in1=x1[:, j, :], op0=ALU.mult, op1=ALU.add).then_inc(halved, 1)
                    dve.wait_ge(halved, j + 1)
                    if j >= NG:
                        dve.wait_ge(out_stored[j % NG], 16 * (j // NG))
                    nc.vector.scalar_tensor_tensor(out=o[j % NG][:, :], in0=got[1][j % NG][:, :], scalar=gate_w[:, 1, j:j + 1],
                                                   in1=half[j % 2][:, :], op0=ALU.mult, op1=ALU.add).then_inc(summed, 1)

            @block.sync
            def _(sp):
                for j in range(NT):
                    n = P if j < NT - 1 else NTAIL
                    sp.wait_ge(summed, j + 1)
                    sp.dma_start(out[j * P:j * P + n, :], o[j % NG][0:n, :]).then_inc(out_stored[j % NG], 16)
                for i in range(NG):
                    sp.wait_ge(out_stored[i], 16 * ((NT - i + NG - 1) // NG))


_INS = ["x", "src", "dst", "edge_attr_256", "L0_gnn_Wq", "L0_gnn_bq", "L0_gnn_Wk", "L0_gnn_bk", "L0_gnn_Wv", "L0_gnn_bv",
        "L0_gnn_We", "L0_gnn_Ws", "L0_gnn_bs", "L0_ffn_Wg", "L0_ffn_bg", "L0_ffn_bias", "L0_ffn_W1", "L0_ffn_b1",
        "L0_ffn_W2", "L0_ffn_b2"]


def kernel(**inputs):
    import numpy as _np
    import concourse.bacc as _bacc
    from concourse import mybir as _mybir
    from concourse.bass_utils import run_bass_kernel_spmd as _run

    nc = _bacc.Bacc("TRN2", target_bir_lowering=False, num_devices=1)
    arrays, args = {}, []
    for name in _INS:
        a = _np.ascontiguousarray(inputs[name])
        arrays[f"in_{name}"] = a
        args.append(nc.dram_tensor(f"in_{name}", a.shape, _mybir.dt.from_np(a.dtype), kind="ExternalInput").ap())
    n, d = inputs["x"].shape
    args.append(nc.dram_tensor("out_0", (n, d), F32, kind="ExternalOutput").ap())
    gnn_ffn(nc, *args)
    r = _run(nc, [arrays], core_ids=[0])
    return r.results[0]["out_0"]
```

```python
from contextlib import ExitStack

import concourse.bass as bass
from concourse import mybir

F32 = mybir.dt.float32
I32 = mybir.dt.int32
ALU = mybir.AluOpType
ACT = mybir.ActivationFunctionType
AX_X = mybir.AxisListType.X

P = 128
H = 8
CH = 16
BIG = 2.0 ** 100
PAD_DST = 1 << 20
LN_EPS = 1e-5
N_KV = 4
N_A = 4
N_W = 4
TOP = 2


def ceil_div(a, b):
    return -(-a // b)


def gnn_ffn(nc, x, src, dst, edge_attr, Wq, bq, Wk, bk, Wv, bv, We, Ws, bs, Wg, bg, gbias, W1, b1, W2, b2, out):
    N, D = x.shape
    E = edge_attr.shape[0]
    C = D // H
    KD = D // P
    NT = ceil_div(N, P)
    ET = ceil_div(E, P)
    NTAIL = N - (NT - 1) * P
    ETAIL = E - (ET - 1) * P
    NR = NT * P
    NCH = ceil_div(NT + ET - 1, CH)
    NCH += 1 - NCH % 2
    IT = NCH * CH
    IB = ceil_div(IT, P)
    RB = ceil_div(ET, P)
    SCALE = float(C) ** -0.5
    CP = C + 1
    UW = H * CP
    NE, _, F = W1.shape
    KF = F // P
    NB = (NR * TOP + NE * (P - 1)) // P
    assert D == 2 * P and H * C == D and 0 < ETAIL < P and NT < P

    with ExitStack() as ctx:
        def sb(name, shape, dt=F32, c=ctx):
            return c.enter_context(nc.sbuf_tensor(name, shape, dt))

        def sem(name, c=ctx):
            return c.enter_context(nc.semaphore(name))

        def counters(c, **credits):
            sems = {n: sem(n, c) for n in credits}

            def at(name, i):
                return i + (credits[name] + 1)

            def grant(eng, *names):
                for n in names:
                    eng.sem_inc(sems[n], credits[n])

            return sems, at, grant

        def layernorm_stats(dve, over_tiles, s, rows, stat, mv, vp, sd, r, rstd):
            v = nc.vector
            r0, r1, r2, r3 = r

            def stats(j, par):
                v.bn_stats(flat(stat[:, :, :])[:, bass.ds(j * 6, 6)], rows[:, bass.ds(j * D, D)]).then_inc(s["stat_ready"], 1)

            def then(ins, count):
                ins.then_inc(s["ln_step"], 1)
                dve.wait_ge(s["ln_step"], count)

            over_tiles(dve, stats)
            dve.wait_ge(s["stat_ready"], NT)
            for j in range(NT):
                v.bn_aggr(mv[:, j, :], stat[:, j, :]).then_inc(s["aggregated"], 1)
            dve.wait_ge(s["aggregated"], NT)
            v.tensor_scalar(vp[:, :], mv[:, :, 1:2].rearrange("p j o -> p (j o)"), LN_EPS, None, ALU.add).then_inc(s["var_ready"], 1)
            dve.wait_ge(s["sd_ready"], 1)
            then(v.reciprocal(r0[:, :], sd[:, :]), 1)
            then(v.tensor_tensor(r1[:, :], r0[:, :], r0[:, :], ALU.mult), 2)
            then(v.tensor_tensor(r2[:, :], r1[:, :], vp[:, :], ALU.mult), 3)
            then(v.tensor_scalar(r3[:, :], r2[:, :], -0.5, 1.5, ALU.mult, ALU.add), 4)
            then(v.tensor_tensor(rstd[:, :], r0[:, :], r3[:, :], ALU.mult), 5)
            dve.sem_inc(s["dve_pace"], 1)

        def dram(name, shape, dt=F32):
            return nc.dram_tensor(name, shape, dt, kind="Internal").ap()

        src_rows = dram("src_rows", (ET, P), I32)
        sel_rows = dram("sel_rows", (ET, P), I32)
        run_rows = dram("run_rows", (ET, P), I32)
        run_table = dram("run_table", (IT, H, P))
        kv_table = dram("kv_table", (NR, 2 * D))
        skip_table = dram("skip_table", (NR, D))
        sorted_x = dram("sorted_x", (NB * P, D))
        sorted_y = dram("sorted_y", (NB * P, D))

        ident = sb("ident", [P, P])
        ones = sb("ones", [P, P])
        iota_free = sb("iota_free", [P, P])
        iota_part = sb("iota_part", [P, 1])
        src_idx = sb("src_idx", [P, IT], I32)
        dst_loc = sb("dst_loc", [P, IT])
        mask = sb("mask", [P, IT])
        item_node_tile = sb("item_node_tile", [1, IT], I32)
        item_row = sb("item_row", [1, IT], I32)
        chunk_tile = sb("chunk_tile", [P, NCH])
        assert NT * NE <= IT and TOP * NT <= IT and NB <= IT
        slot_i = src_idx[:, 0:TOP * NT].rearrange("p (k j) -> p k j", k=TOP)
        gate_w = dst_loc[:, 0:TOP * NT].rearrange("p (k j) -> p k j", k=TOP)
        logits = mask[:, 0:NT * NE].rearrange("p (j e) -> p j e", e=NE)
        block_expert = item_row[0:1, 0:NB]
        q_sb = sb("q_sb", [P, NT + 1, D])
        acc = sb("acc", [P, NT + 1, UW])

        def flat(ap):
            return ap.rearrange("p j d -> p (j d)")

        x_sb = flat(acc[:, :, :])[:, 0:NT * D].rearrange("p (j d) -> p j d", d=D)
        c_w4 = ctx.enter_context(ExitStack())
        w4 = sb("w4", [P, KD, 4 * D], F32, c_w4)
        b4 = sb("b4", [P, 4 * D], F32, c_w4)
        tail_zeroed = sem("tail_zeroed", c_w4)
        proj_loaded = sem("proj_loaded", c_w4)

        with ExitStack() as c1:
            def sb1(name, shape, dt=F32):
                return sb(name, shape, dt, c1)

            def ps1(name, shape):
                return c1.enter_context(nc.psum_tensor(name, shape, F32))

            dst_sb = sb1("dst_sb", [P, RB, P], I32)
            lasts = sb1("lasts", [P, RB])
            thr_i = sb1("thr_i", [P, NT], I32)
            thr = sb1("thr", [P, NT])
            below = sb1("below", [P, NT, RB])
            below_n = sb1("below_n", [P, NT])
            step_at = sb1("step_at", [NT, 1])
            ii_i = sb1("ii_i", [P, IT], I32)
            ii = sb1("ii", [P, IT])
            ip_i = sb1("ip_i", [P, IB], I32)
            ip = sb1("ip", [P, IB])
            if_i = sb1("if_i", [P, P], I32)
            pp_i = sb1("pp_i", [P, 1], I32)
            stepped = sb1("stepped", [NT, IT])
            node_tile_rep = sb1("node_tile_rep", [P, IT])
            t_rep = sb1("t_rep", [P, IT])
            r_rep = sb1("r_rep", [P, IT])
            t_item = sb1("t_item", [P, IB])
            t_idx = sb1("t_idx", [P, IB], I32)
            pad_dst = sb1("pad_dst", [1, P], I32)
            pad_src = sb1("pad_src", [1, P], I32)
            pad_run = sb1("pad_run", [1, P], I32)
            last_dst = sb1("last_dst", [1, 1], I32)
            src_g = sb1("src_g", [P, IB, P], I32)
            sel_g = sb1("sel_g", [P, IB, P], I32)
            run_g = sb1("run_g", [P, IB, P], I32)
            src_f = sb1("src_f", [P, IB, P])
            sel_f = sb1("sel_f", [P, IB, P])
            run_f = sb1("run_f", [P, IB, P])
            m_lo = sb1("m_lo", [P, IT])
            m_hi = sb1("m_hi", [P, IT])
            ps_rep = [ps1(f"ps_rep{i}", [P, 512]) for i in range(2)]
            ps_small = ps1("ps_small", [P, 512])
            ps_src = ps1("ps_src", [P, 512])
            ps_sel = ps1("ps_sel", [P, 512])

            dst_loaded = sem("dst_loaded", c1)
            rows_written = sem("rows_written", c1)
            pads_set = sem("pads_set", c1)
            last_loaded = sem("last_loaded", c1)
            iotas = sem("iotas", c1)
            dve_step = sem("dve_step", c1)
            below_ready = sem("below_ready", c1)
            step_summed = sem("step_summed", c1)
            stepped_ready = sem("stepped_ready", c1)
            rep_ready = sem("rep_ready", c1)
            item_ready = sem("item_ready", c1)
            t_idx_ready = sem("t_idx_ready", c1)
            gathered = [sem(f"gathered_{n}", c1) for n in ("run", "src", "sel")]
            floats_ready = sem("floats_ready", c1)
            turned = sem("turned", c1)
            turned_copied = sem("turned_copied", c1)
            run_written = sem("run_written", c1)
            full = ET - 1
            pad = P - ETAIL
            IH = IT // 2
            assert IH <= 512

            def rows_in(b, total=IT):
                return min(P, total - b * P)

            block = c1.enter_context(nc.Block())

            @block.sync
            def _(sp):
                with nc.allow_non_contiguous_dma(reason="the short tail row of the edge lists"):
                    nb = full // P
                    if nb:
                        sp.dma_start(dst_sb[:, 0:nb, :], dst[0:nb * P * P].rearrange("(b p e) -> p b e", p=P, e=P)).then_inc(dst_loaded, 16)
                    sp.dma_start(dst_sb[0:full - nb * P, nb, :],
                                 dst[nb * P * P:full * P].rearrange("(p e) -> p e", e=P)).then_inc(dst_loaded, 16)
                    sp.dma_start(last_dst[:, :], dst[full * P - 1:full * P].rearrange("(t e) -> t e", t=1)).then_inc(last_loaded, 16)
                for i, w in enumerate((Wq, Wk, Wv, Ws)):
                    sp.dma_start(w4[:, :, i * D:(i + 1) * D], w.rearrange("(k p) n -> p k n", p=P)).then_inc(proj_loaded, 16)
                for i, b in enumerate((bq, bk, bv, bs)):
                    sp.dma_start(b4[:, i * D:(i + 1) * D],
                                 b.rearrange("(o n) -> o n", o=1).to_broadcast([P, D])).then_inc(proj_loaded, 16)
                sp.dma_start(x_sb[:, 0:NT - 1, :], x[0:(NT - 1) * P, :].rearrange("(j p) d -> p j d", p=P)).then_inc(proj_loaded, 16)
                sp.wait_ge(tail_zeroed, 1)
                sp.dma_start(x_sb[0:NTAIL, NT - 1, :], x[(NT - 1) * P:N, :]).then_inc(proj_loaded, 16)
                with nc.allow_non_contiguous_dma(reason="the short tail row of the edge lists"):
                    sp.wait_ge(pads_set, 3)
                    for rows, edges in ((src_rows, src), (sel_rows, dst), (run_rows, dst)):
                        sp.dma_start(rows[0:full, :], edges[0:full * P].rearrange("(t e) -> t e", e=P)).then_inc(rows_written, 16)
                        sp.dma_start(rows[full:ET, pad:P], edges[full * P:E].rearrange("(t e) -> t e", t=1)).then_inc(rows_written, 16)
                    sp.dma_start(src_rows[full:ET, 0:pad], pad_src[0:1, 0:pad]).then_inc(rows_written, 16)
                    sp.dma_start(sel_rows[full:ET, 0:pad], pad_dst[0:1, 0:pad]).then_inc(rows_written, 16)
                    sp.dma_start(run_rows[full:ET, 0:pad],
                                 pad_run[0:1, 0:pad]).then_inc(rows_written, 16)
                    sp.wait_ge(floats_ready, 3)
                    for b in range(IB):
                        n = rows_in(b)
                        sp.dma_start(run_table[b * P:b * P + n, :, :],
                                     run_f[0:n, b:b + 1, :].to_broadcast([n, H, P])).then_inc(run_written, 16)
                    sp.wait_ge(run_written, 16 * IB)

            @block.gpsimd
            def _(pool):
                nc.gpsimd.memset(pad_src[:, :], 0).then_inc(pads_set, 1)
                nc.gpsimd.memset(pad_dst[:, :], PAD_DST).then_inc(pads_set, 1)
                pool.wait_ge(last_loaded, 16)
                nc.gpsimd.tensor_copy(pad_run[:, :], last_dst[:, :].to_broadcast([1, P])).then_inc(pads_set, 1)
                nc.gpsimd.iota(if_i[:, :], [[1, P]], base=0, channel_multiplier=0).then_inc(iotas, 1)
                nc.gpsimd.iota(pp_i[:, :], [[1, 1]], base=0, channel_multiplier=1).then_inc(iotas, 1)
                nc.gpsimd.iota(thr_i[:, :], [[P, NT]], base=P, channel_multiplier=0).then_inc(iotas, 1)
                nc.gpsimd.iota(ii_i[:, :], [[1, IT]], base=0, channel_multiplier=0).then_inc(iotas, 1)
                nc.gpsimd.iota(ip_i[:, :], [[P, IB]], base=0, channel_multiplier=1).then_inc(iotas, 1)
                pool.wait_ge(rows_written, 16 * 9)
                pool.wait_ge(t_idx_ready, 2)
                for rows, got, got_sem in ((run_rows, run_g, gathered[0]), (src_rows, src_g, gathered[1]),
                                           (sel_rows, sel_g, gathered[2])):
                    for b in range(IB):
                        n = rows_in(b)
                        nc.gpsimd.indirect_dma_start(
                            out=got[0:n, b, :], out_offset=None, in_=rows,
                            in_offset=bass.IndirectOffsetOnAxis(ap=t_idx[0:n, b:b + 1], axis=0)).then_inc(got_sem, 16)

            @block.vector
            def _(dve):
                count = [0]

                def then(ins):
                    count[0] += 1
                    ins.then_inc(dve_step, 1)
                    dve.wait_ge(dve_step, count[0])

                v = nc.vector
                v.memset(x_sb[:, NT - 1, :], 0.0).then_inc(tail_zeroed, 1)
                v.memset(ones[:, :], 1.0)
                then(v.memset(lasts[:, :], 1.0e9))
                dve.wait_ge(iotas, 5)
                v.tensor_copy(iota_free[:, :], if_i[:, :])
                v.tensor_copy(thr[:, :], thr_i[:, :])
                v.tensor_copy(ii[:, :], ii_i[:, :])
                v.tensor_copy(ip[:, :], ip_i[:, :])
                then(v.tensor_copy(iota_part[:, :], pp_i[:, :]))
                v.tensor_scalar(ident[:, :], iota_free[:, :], iota_part[:, 0:1], None, ALU.is_equal)
                nb = full // P
                dve.wait_ge(dst_loaded, 16 * (2 if nb else 1))
                if nb:
                    v.tensor_copy(lasts[:, 0:nb], dst_sb[:, 0:nb, P - 1])
                then(v.tensor_copy(lasts[0:full - nb * P, nb:nb + 1], dst_sb[0:full - nb * P, nb, P - 1:P]))
                then(v.tensor_tensor(below[:, :, :], lasts[:, None, :].to_broadcast([P, NT, RB]),
                                     thr[:, :, None].to_broadcast([P, NT, RB]), ALU.is_lt))
                v.tensor_reduce(below_n[:, :], below[:, :, :], AX_X, ALU.add).then_inc(below_ready, 1)
                dve.wait_ge(step_summed, 1)
                then(v.tensor_scalar(step_at[:, :], ps_small[0:NT, 0:1], float(ET - 1), iota_part[0:NT, 0:1], ALU.min, ALU.add))
                v.tensor_scalar(stepped[:, :], ii[0:NT, :], step_at[:, 0:1], None, ALU.is_gt).then_inc(stepped_ready, 1)
                dve.wait_ge(item_ready, 1)
                nf = IT // P
                if nf:
                    v.tensor_tensor(t_item[:, 0:nf], ip[:, 0:nf], ps_small[:, 8:8 + nf], ALU.subtract)
                if IB > nf:
                    n = rows_in(nf)
                    v.tensor_tensor(t_item[0:n, nf:IB], ip[0:n, nf:IB], ps_small[0:n, 8 + nf:8 + IB], ALU.subtract)
                then(v.memset(dst_sb[:, 0, 0:1], 0))
                if nf:
                    v.tensor_scalar(t_idx[:, 0:nf], t_item[:, 0:nf], float(ET - 1), None, ALU.min).then_inc(t_idx_ready, 1)
                else:
                    dve.sem_inc(t_idx_ready, 1)
                if IB > nf:
                    v.tensor_scalar(t_idx[0:n, nf:IB], t_item[0:n, nf:IB], float(ET - 1), None, ALU.min).then_inc(t_idx_ready, 1)
                else:
                    dve.sem_inc(t_idx_ready, 1)
                dve.wait_ge(rep_ready, 1)
                v.tensor_copy(node_tile_rep[:, 0:IH], ps_rep[0][:, 0:IH])
                then(v.tensor_copy(node_tile_rep[:, IH:IT], ps_rep[1][:, 0:IH]))
                v.tensor_copy(item_node_tile[:, :], node_tile_rep[0:1, :])
                v.tensor_copy(chunk_tile[:, :], node_tile_rep[:, 0:IT:CH])
                then(v.tensor_tensor(t_rep[:, :], ii[:, :], node_tile_rep[:, :], ALU.subtract))
                then(v.tensor_scalar(r_rep[:, :], t_rep[:, :], float(P), float(E - P), ALU.mult, ALU.min))
                v.tensor_copy(item_row[:, :], r_rep[0:1, :])
                for k, (got, flt) in enumerate(((run_g, run_f), (src_g, src_f), (sel_g, sel_f))):
                    dve.wait_ge(gathered[k], 16 * IB)
                    scale = BIG if k == 0 else 1.0
                    if nf:
                        v.tensor_scalar(flt[:, 0:nf, :], got[:, 0:nf, :], scale, None, ALU.mult).then_inc(floats_ready, 1)
                    if IB > nf:
                        v.tensor_scalar(flt[0:n, nf:IB, :], got[0:n, nf:IB, :], scale, None, ALU.mult).then_inc(floats_ready, 1)
                for b in range(IB):
                    n = rows_in(b)
                    dve.wait_ge(turned, b + 1)
                    v.tensor_copy(src_idx[:, b * P:b * P + n], ps_src[:, 0:n])
                    v.scalar_tensor_tensor(out=dst_loc[:, b * P:b * P + n], in0=node_tile_rep[:, b * P:b * P + n],
                                           scalar=-float(P), in1=ps_sel[:, 0:n], op0=ALU.mult,
                                           op1=ALU.add).then_inc(turned_copied, 1)
                dve.wait_ge(turned_copied, IB)
                v.tensor_scalar(m_lo[:, :], dst_loc[:, :], 0.0, -BIG, ALU.is_lt, ALU.mult)
                then(v.tensor_scalar(m_hi[:, :], dst_loc[:, :], P - 0.5, -BIG, ALU.is_gt, ALU.mult))
                then(v.tensor_tensor(mask[:, :], m_lo[:, :], m_hi[:, :], ALU.add))

            nfl = 2 if IT % P and IT >= P else 1

            @block.tensor
            def _(pe):
                pe.wait_ge(below_ready, 1)
                nc.tensor.matmul(ps_small[0:NT, 0:1], below_n[:, :], ones[:, 0:1], start=True, stop=True).then_inc(step_summed, 1)
                pe.wait_ge(stepped_ready, 1)
                for b in range(IB):
                    n = rows_in(b)
                    last = nc.tensor.matmul(ps_small[0:n, 8 + b:9 + b], stepped[:, b * P:b * P + n], ones[0:NT, 0:1], start=True, stop=True)
                last.then_inc(item_ready, 1)
                for h in range(2):
                    last = nc.tensor.matmul(ps_rep[h][:, 0:IH], ones[0:NT, :], stepped[:, h * IH:(h + 1) * IH], start=True, stop=True)
                last.then_inc(rep_ready, 1)
                pe.wait_ge(floats_ready, 3 * nfl)
                for b in range(IB):
                    n = rows_in(b)
                    if b:
                        pe.wait_ge(turned_copied, b)
                    nc.tensor.transpose(ps_src[:, 0:n], src_f[0:n, b, :], ident[0:n, 0:n])
                    nc.tensor.transpose(ps_sel[:, 0:n], sel_f[0:n, b, :], ident[0:n, 0:n]).then_inc(turned, 1)

        with ExitStack() as c2:
            def sb2(name, shape, dt=F32):
                return sb(name, shape, dt, c2)

            def ps2(name, shape):
                return c2.enter_context(nc.psum_tensor(name, shape, F32))

            stat = sb2("stat", [P, NT, 6])
            mv = sb2("mv", [P, NT, 2])
            vp = sb2("vp", [P, NT])
            sd = sb2("sd", [P, NT])
            r0 = sb2("r0", [P, NT])
            r1 = sb2("r1", [P, NT])
            r2 = sb2("r2", [P, NT])
            r3 = sb2("r3", [P, NT])
            rstd = sb2("rstd", [P, NT])
            xn = [sb2(f"xn{i}", [P, D]) for i in range(2)]
            xnT = [sb2(f"xnT{i}", [P, D]) for i in range(2)]
            kv_out = [sb2(f"kv_out{i}", [P, 2 * D]) for i in range(2)]
            skip_out = [sb2(f"skip_out{i}", [P, D]) for i in range(2)]
            ps_t = [ps2(f"ps_t{i}", [P, 512]) for i in range(2)]
            ps_p = [ps2(f"ps_p{i}", [P, 1024]) for i in range(2)]
            s, at, grant = counters(c2, stat_ready=0, aggregated=0, ln_step=0, var_ready=0, sd_ready=0, xn_ready=0, xn_turned=2,
                                    xnT_ready=2, projected=2, q_out=2, kv_out_ready=2, skip_half=2, skip_out_ready=0,
                                    stored0=16, stored1=16, dve_pace=0)
            stored = [s["stored0"], s["stored1"]]
            block = c2.enter_context(nc.Block())

            def over_tiles(eng, emit):
                with eng.Fori(0, NT // 2) as g:
                    emit(g * 2, 0)
                    emit(g * 2 + 1, 1)
                if NT % 2:
                    emit(NT - 1, 0)

            @block.sync
            def _(sp):
                def store(j, par):
                    sp.wait_ge(s["kv_out_ready"], at("kv_out_ready", j))
                    sp.dma_start(kv_table[bass.ds(j * P, P), :], kv_out[par][:, :]).then_inc(stored[par], 16)
                    sp.wait_ge(s["skip_out_ready"], at("skip_out_ready", j))
                    sp.dma_start(skip_table[bass.ds(j * P, P), :], skip_out[par][:, :]).then_inc(stored[par], 16)

                over_tiles(sp, store)
                sp.wait_ge(stored[0], 16 + 32 * ceil_div(NT, 2))
                sp.wait_ge(stored[1], 16 + 32 * (NT // 2))

            @block.scalar
            def _(act):
                grant(act, "xnT_ready")
                act.wait_ge(s["var_ready"], 1)
                nc.scalar.activation(sd[:, :], vp[:, :], ACT.Sqrt).then_inc(s["sd_ready"], 1)

                def tile(j, par):
                    act.wait_ge(s["xn_turned"], at("xn_turned", j))
                    act.wait_ge(s["projected"], at("projected", j - 2))
                    nc.scalar.copy(xnT[par][:, :], ps_t[par][:, 0:D]).then_inc(s["xnT_ready"], 1)

                over_tiles(act, tile)

            @block.tensor
            def _(pe):
                grant(pe, "xn_turned", "projected")
                pe.wait_ge(proj_loaded, 16 * 10)

                def turn(j, par):
                    pe.wait_ge(s["xn_ready"], at("xn_ready", j))
                    pe.wait_ge(s["xnT_ready"], at("xnT_ready", j - 2))
                    for k in range(KD):
                        last = nc.tensor.transpose(ps_t[par][:, k * P:(k + 1) * P], xn[par][:, k * P:(k + 1) * P], ident[:, :])
                    last.then_inc(s["xn_turned"], 1)

                def project(j, par):
                    pe.wait_ge(s["xnT_ready"], at("xnT_ready", j))
                    pe.wait_ge(s["q_out"], at("q_out", j - 2))
                    pe.wait_ge(s["kv_out_ready"], at("kv_out_ready", j - 2))
                    pe.wait_ge(s["skip_half"], at("skip_half", j - 2))
                    for h in range(2):
                        for k in range(KD):
                            last = nc.tensor.matmul(ps_p[par][:, h * 512:(h + 1) * 512], xnT[par][:, k * P:(k + 1) * P],
                                                    w4[:, k, h * 512:(h + 1) * 512], start=(k == 0), stop=(k == KD - 1))
                    last.then_inc(s["projected"], 1)

                turn(0, 0)
                with pe.Fori(0, (NT - 1) // 2) as g:
                    turn(g * 2 + 1, 1)
                    project(g * 2, 0)
                    turn(g * 2 + 2, 0)
                    project(g * 2 + 1, 1)
                for j in range(NT - 1 - (NT - 1) % 2, NT):
                    if j + 1 < NT:
                        turn(j + 1, (j + 1) % 2)
                    project(j, j % 2)

            @block.vector
            def _(dve):
                v = nc.vector
                grant(dve, "q_out", "kv_out_ready", "skip_half", "stored0", "stored1")
                v.memset(q_sb[:, NT, :], 0.0)
                dve.wait_ge(proj_loaded, 16 * 10)
                dve.sem_inc(s["dve_pace"], 1)
                layernorm_stats(dve, over_tiles, s, flat(x_sb[:, :, :]), stat, mv, vp, sd, (r0, r1, r2, r3), rstd)

                def normalise(j, par):
                    dve.wait_ge(s["xn_turned"], at("xn_turned", j - 2))
                    v.tensor_scalar(xn[par][:, :], flat(x_sb[:, :, :])[:, bass.ds(j * D, D)], flat(mv[:, :, :])[:, bass.ds(j * 2, 1)],
                                    rstd[:, bass.ds(j, 1)], ALU.subtract, ALU.mult).then_inc(s["xn_ready"], 1)

                def evacuate(j, par):
                    dve.wait_ge(stored[par], (j - par) * 16 + 16)
                    dve.wait_ge(s["projected"], at("projected", j))
                    v.tensor_tensor(kv_out[par][:, :], ps_p[par][:, D:3 * D], b4[:, D:3 * D], ALU.add).then_inc(s["kv_out_ready"], 1)
                    v.tensor_tensor(skip_out[par][:, :], ps_p[par][:, 3 * D:4 * D], b4[:, 3 * D:4 * D], ALU.add).then_inc(s["skip_half"], 1)
                    v.tensor_tensor(flat(q_sb[:, :, :])[:, bass.ds(j * D, D)], ps_p[par][:, 0:D], b4[:, 0:D], ALU.add).then_inc(s["q_out"], 1)
                    dve.wait_ge(s["skip_half"], at("skip_half", j))
                    v.tensor_tensor(skip_out[par][:, :], skip_out[par][:, :], flat(x_sb[:, :, :])[:, bass.ds(j * D, D)],
                                    ALU.add).then_inc(s["skip_out_ready"], 1)

                normalise(0, 0)
                normalise(1, 1)
                with dve.Fori(0, (NT - 2) // 2) as g:
                    normalise(g * 2 + 2, 0)
                    evacuate(g * 2, 0)
                    normalise(g * 2 + 3, 1)
                    evacuate(g * 2 + 1, 1)
                for j in range(2 * ((NT - 2) // 2), NT):
                    if j + 2 < NT:
                        normalise(j + 2, j % 2)
                    evacuate(j, j % 2)

        c_w4.close()

        with ExitStack() as c3:
            def sb3(name, shape, dt=F32):
                return sb(name, shape, dt, c3)

            def ps3(name, shape):
                return c3.enter_context(nc.psum_tensor(name, shape, F32))

            KW = 2 * P + H
            we_sb = sb3("we_sb", [P, KD, D])
            a_ring = sb3("a_ring", [P, N_A, D])
            kv_ring = sb3("kv_ring", [P, N_KV, 2 * D])
            aT = [sb3(f"aT{i}", [P, D + P]) for i in range(2)]
            kq = [sb3(f"kq{i}", [P, D]) for i in range(2)]
            kqq = [sb3(f"kqq{i}", [P, D]) for i in range(2)]
            ve = sb3("ve", [P, 2, CH, UW])
            sel = sb3("sel", [P, 2, CH, P])
            alpha = [sb3(f"alpha{i}", [P, P]) for i in range(2)]
            w_ring = sb3("w_ring", [P, N_W, UW])
            idx_c = sb3("idx_c", [P, 2, CH], I32)
            apart = [sb3(f"apart{i}", [P, P]) for i in range(2)]
            run_c = [sb3(f"run_c{i}", [P, P]) for i in range(2)]
            ea = [sb3(f"ea{i}", [P, P]) for i in range(2)]
            head_i = sb3("head_i", [P, 1], I32)
            head_m = sb3("head_m", [P, 1], I32)
            pp8_i = sb3("pp8_i", [P, 1], I32)
            head = sb3("head", [P, 1])
            part8 = sb3("part8", [P, 1])
            am = sb3("am", [P, P])
            resets = sb3("resets", [P, P + 1])
            off_first = sb3("off_first", [P, P])
            off_last = sb3("off_last", [P, P])
            key_f = sb3("key_f", [P, 1])
            key_l = sb3("key_l", [P, 1])
            key_prev = sb3("key_prev", [P, 1])
            max_prev = sb3("max_prev", [P, 1])
            diag_k = sb3("diag_k", [P, KW])
            diag_r = sb3("diag_r", [P, KW])
            diag_f = sb3("diag_f", [P, H])
            not_f = sb3("not_f", [P, KW])
            not_l = sb3("not_l", [P, KW])
            scan_f = sb3("scan_f", [P, P])
            scan_b = sb3("scan_b", [P, P])
            max_f = sb3("max_f", [P, 1])
            max_l = sb3("max_l", [P, 1])
            shifted = am
            keys2 = sb3("keys2", [P, 2])
            same = sb3("same", [P, 1])
            node_key = sb3("node_key", [P, 1])
            pick = sb3("pick", [P, 1])
            unpick = sb3("unpick", [P, 1])
            carry = sb3("carry", [P, H])
            carry_d = sb3("carry_d", [P, H])
            carry_e = sb3("carry_e", [P, H])
            factor = sb3("factor", [P, H])
            ps_t = [ps3(f"ps_t3{i}", [P, 512]) for i in range(2)]
            ps_e = [ps3(f"ps_e{i}", [P, 512]) for i in range(2)]
            ps_u = [ps3(f"ps_u{i}", [P, 512]) for i in range(2)]
            ps_ak = ps3("ps_ak", [P, 512])
            ps_rx = ps3("ps_rx", [P, 512])
            ps_a, ps_k = ps_ak[:, 0:P], ps_ak[:, P:P + KW]
            ps_r, ps_x, ps_f = ps_rx[:, 0:KW], ps_rx[:, KW:KW + P], ps_rx[:, KW + P:KW + P + H]

            s, at, grant = counters(c3, a_turned=N_A, aT_ready=2, e_ready=2, ke_added=0, ve_added=N_KV, kq_ready=2,
                                    alpha_ready=0, apart_ready=0, sel_ready=0, weighted=2 * CH, summed=2 * CH, acc_added=2,
                                    idx_copied=0, am_ready=0, am_turned=0, keyed=0, r_ready=0,
                                    max_spread=0, f_ready=0, shifted_ready=0, shifted_turned=1, ea_ready=0, rescaled=2,
                                    carry_ready=0, carry_exp=0, factor_ready=0, softmax_done=2,
                                    const_loaded=0, iotas=0, setup=0, sm_step=0,
                                    act_pace=0, pool_pace=0, softmax_pace=0)
            a_loaded = [sem(f"a_loaded{i}", c3) for i in range(N_A)]
            kv_loaded = [sem(f"kv_loaded{i}", c3) for i in range(N_KV)]
            run_loaded = [sem(f"run_loaded{i}", c3) for i in range(2)]
            block = c3.enter_context(nc.Block())

            FIRST_WEIGH = 11
            LAG = dict(weigh=FIRST_WEIGH + N_KV,
                       sum=FIRST_WEIGH + 2,
                       add=FIRST_WEIGH + 2)
            assert max(LAG.values()) < CH

            def plan(scores=True, softmax=True, new=True, old=True, parts={}, what=None):
                out = []
                for i in range(CH):
                    if scores:
                        out.append(("score", i, 0))
                    if softmax and i in parts:
                        out.append((parts[i], i, 1))
                    k = i - LAG.get(what, 0)
                    if what and k >= 0 and new:
                        out.append((what, k, 1))
                    elif what and k < 0 and old:
                        out.append((what, k + CH, 2))
                return out

            def by_head(ap, width):
                return ap.rearrange("p (h c) -> p h c", c=width)

            def over_chunks(eng, emit, **kw):
                emit(0, 0, plan(softmax=False, new=False, old=False, **kw))
                emit(1, 1, plan(old=False, **kw))
                pairs = (NCH - 2) // 2
                with eng.Fori(0, pairs) as g:
                    emit(g * 2 + 2, 0, plan(**kw))
                    emit(g * 2 + 3, 1, plan(**kw))
                for c in range(2 + 2 * pairs, NCH):
                    emit(c, c % 2, plan(**kw))
                emit(NCH, NCH % 2, plan(scores=False, **kw))
                emit(NCH + 1, (NCH + 1) % 2, plan(scores=False, softmax=False, new=False, **kw))

            @block.sync
            def _(sp):
                sp.dma_start(we_sb[:, :, :], We.rearrange("(k p) n -> p k n", p=P)).then_inc(s["const_loaded"], 16)

                def load(c, par, steps):
                    for kind, i, back in steps:
                        if kind != "score":
                            continue
                        if i == 0:
                            sp.wait_ge(s["softmax_done"], at("softmax_done", c - 2))
                            sp.dma_start(run_c[par][:, :],
                                         run_table[bass.ds(c * CH, CH), :, :].rearrange("i h e -> (i h) e")).then_inc(run_loaded[par], 16)
                        row = sp.value_load(item_row[0:1, bass.ds(c * CH + i, 1)], min_val=0, max_val=E - P)
                        sp.wait_ge(s["a_turned"], at("a_turned", c * CH + (i - N_A)))
                        sp.dma_start(a_ring[:, i % N_A, :], edge_attr[bass.ds(row, P), :]).then_inc(a_loaded[i % N_A], 16)

                over_chunks(sp, load)

            @block.gpsimd
            def _(pool):
                g = nc.gpsimd
                grant(pool, "weighted")
                g.iota(pp8_i[:, :], [[1, 1]], base=0, channel_multiplier=H).then_inc(s["iotas"], 1)
                g.iota(head_i[:, :], [[1, 1]], base=0, channel_multiplier=1).then_inc(s["iotas"], 1)

                def gather(c, par, i):
                    if i == 0:
                        g.tensor_copy(idx_c[:, par, :], src_idx[:, bass.ds(c * CH, CH)]).then_inc(s["idx_copied"], 1)
                        pool.wait_ge(s["idx_copied"], at("idx_copied", c))
                        pool.sem_inc(s["pool_pace"], 1)
                    pool.wait_ge(s["ve_added"], at("ve_added", c * CH + (i - N_KV)))
                    pool.sem_inc(s["pool_pace"], 1)
                    g.indirect_dma_start(out=kv_ring[:, i % N_KV, :], out_offset=None, in_=kv_table,
                                         in_offset=bass.IndirectOffsetOnAxis(ap=idx_c[:, par, i:i + 1], axis=0)
                                         ).then_inc(kv_loaded[i % N_KV], 16)

                def weigh(c, par, i):
                    m = c * CH + i
                    if i == 0:
                        pool.wait_ge(s["ea_ready"], at("ea_ready", c))
                        pool.sem_inc(s["pool_pace"], 1)
                    pool.wait_ge(s["summed"], at("summed", m - N_W))
                    g.tensor_tensor(by_head(w_ring[:, i % N_W, :], CP), by_head(ve[:, par, i, :], CP),
                                    ea[par][:, i * H:(i + 1) * H][:, :, None].to_broadcast([P, H, CP]),
                                    ALU.mult).then_inc(s["weighted"], 1)

                def emit(c, par, steps):
                    held = None
                    for kind, i, back in steps + [("end", 0, 0)]:
                        if kind == "weigh":
                            weigh(c - back, (par + back) % 2, i)
                        if held is not None:
                            gather(c, par, held)
                        held = i if kind == "score" else None

                over_chunks(pool, emit, what="weigh")

            @block.scalar
            def _(act):
                grant(act, "aT_ready")

                def select(c, par, i):
                    act.wait_ge(s["summed"], at("summed", c * CH + (i - 2 * CH)))
                    act.sem_inc(s["act_pace"], 1)
                    nc.scalar.activation(apart[i % 2][:, :], iota_free[:, :], ACT.Abs, scale=-1.0,
                                         bias=dst_loc[:, bass.ds(c * CH + i, 1)]).then_inc(s["apart_ready"], 1)
                    act.wait_ge(s["apart_ready"], at("apart_ready", c * CH + i))
                    act.sem_inc(s["act_pace"], 1)
                    nc.scalar.activation(sel[:, par, i, :], apart[i % 2][:, :], ACT.Relu, scale=-1.0,
                                         bias=1.0).then_inc(s["sel_ready"], 1)

                AHEAD = 2

                def emit(c, par, steps):
                    for kind, i, back in steps:
                        if kind == "score":
                            if isinstance(c, int) and c == 0 and i == 0:
                                for k in range(AHEAD):
                                    select(c, par, k)
                            act.wait_ge(s["a_turned"], at("a_turned", c * CH + i))
                            act.wait_ge(s["e_ready"], at("e_ready", c * CH + (i - 2)))
                            nc.scalar.copy(aT[i % 2][:, :], ps_t[i % 2][:, 0:D + P]).then_inc(s["aT_ready"], 1)
                            if i + AHEAD < CH:
                                select(c, par, i + AHEAD)
                            elif not (isinstance(c, int) and c == NCH - 1):
                                select(c + 1, 1 - par, i + AHEAD - CH)
                        elif kind == "exp":
                            act.wait_ge(s["weighted"], at("weighted", (c - 2) * CH - 1))
                            act.sem_inc(s["act_pace"], 1)
                            act.wait_ge(s["shifted_turned"], at("shifted_turned", c - 1))
                            act.sem_inc(s["act_pace"], 1)
                            nc.scalar.activation(ea[1 - par][:, :], ps_x, ACT.Exp).then_inc(s["ea_ready"], 1)
                        elif kind == "carry_exp":
                            act.wait_ge(s["carry_ready"], at("carry_ready", c - 1))
                            act.sem_inc(s["act_pace"], 1)
                            nc.scalar.activation(carry_e[:, :], carry_d[:, :], ACT.Exp).then_inc(s["carry_exp"], 1)

                over_chunks(act, emit, parts={12: "exp", 15: "carry_exp"})

            @block.tensor
            def _(pe):
                t = nc.tensor
                grant(pe, "a_turned", "e_ready", "summed", "shifted_turned")
                pe.wait_ge(s["const_loaded"], 16)

                def turn(c, par, i):
                    pe.wait_ge(a_loaded[i % N_A], c * (16 * CH // N_A) + 16 * (i // N_A + 1))
                    pe.wait_ge(s["sel_ready"], at("sel_ready", c * CH + i))
                    pe.wait_ge(s["aT_ready"], at("aT_ready", c * CH + (i - 2)))
                    for k in range(KD):
                        t.transpose(ps_t[i % 2][:, k * P:(k + 1) * P], a_ring[:, i % N_A, k * P:(k + 1) * P], ident[:, :])
                    t.transpose(ps_t[i % 2][:, D:D + P], sel[:, par, i, :], ident[:, :]).then_inc(s["a_turned"], 1)

                def node_tile_of(c, i):
                    return pe.value_load(item_node_tile[0:1, bass.ds(c * CH + i, 1)], min_val=0, max_val=NT)

                def project(c, i, n):
                    pe.wait_ge(s["aT_ready"], at("aT_ready", c * CH + i))
                    pe.wait_ge(s["ve_added"], at("ve_added", c * CH + (i - 2)))
                    pe.wait_ge(s["kq_ready"], at("kq_ready", c * CH + (i - 2)))
                    for k in range(KD):
                        t.matmul(ps_e[i % 2][:, 0:D], aT[i % 2][:, k * P:(k + 1) * P], we_sb[:, k, :], start=(k == 0), stop=(k == KD - 1))
                    t.matmul(ps_e[i % 2][:, D:2 * D], aT[i % 2][:, D:D + P], flat(q_sb[:, :, :])[:, bass.ds(n * D, D)],
                             start=True, stop=True).then_inc(s["e_ready"], 1)

                def emit(c, par, steps):
                    n = node_tile_of(c, 0) if steps[0][0] == "score" else None
                    for kind, i, back in steps:
                        if kind == "score":
                            if isinstance(c, int) and c == 0 and i == 0:
                                turn(c, par, 0)
                            if i + 1 < CH:
                                turn(c, par, i + 1)
                            elif not (isinstance(c, int) and c == NCH - 1):
                                turn(c + 1, 1 - par, 0)
                            project(c, i, n)
                            if i + 1 < CH:
                                n = node_tile_of(c, i + 1)
                        elif kind == "keys":
                            pe.wait_ge(s["keyed"], at("keyed", c - 1))
                            t.matmul(ps_k, ones[:, :], diag_k[:, :], start=True, stop=True)
                            pe.wait_ge(s["am_ready"], at("am_ready", c - 1))
                            t.transpose(ps_a, am[:, :], ident[:, :]).then_inc(s["am_turned"], 1)
                        elif kind == "maxima":
                            pe.wait_ge(s["r_ready"], at("r_ready", c - 1))
                            t.matmul(ps_r, ones[:, :], diag_r[:, :], start=True, stop=True).then_inc(s["max_spread"], 1)
                        elif kind == "turn_scores":
                            pe.wait_ge(s["f_ready"], at("f_ready", c - 1))
                            t.matmul(ps_f, ones[:, :], diag_f[:, :], start=True, stop=True)
                            pe.wait_ge(s["shifted_ready"], at("shifted_ready", c - 1))
                            t.transpose(ps_x, shifted[:, :], ident[:, :]).then_inc(s["shifted_turned"], 1)
                        elif kind == "sum":
                            m = (c - back) * CH + i
                            pe.wait_ge(s["weighted"], at("weighted", m))
                            pe.wait_ge(s["acc_added"], at("acc_added", m - 2))
                            t.matmul(ps_u[i % 2][:, 0:UW], sel[:, (par + back) % 2, i, :], w_ring[:, i % N_W, :],
                                     start=True, stop=True).then_inc(s["summed"], 1)

                over_chunks(pe, emit, what="sum", parts={3: "keys", 6: "maxima", 11: "turn_scores"})

            @block.vector
            def _(dve):
                v = nc.vector
                grant(dve, "ve_added", "kq_ready", "acc_added", "rescaled", "softmax_done")
                v.memset(acc[:, :, :], 0.0).then_inc(s["setup"], 1)
                v.memset(ve[:, :, :, :], 1.0).then_inc(s["setup"], 1)
                v.memset(resets[:, :], 0.0).then_inc(s["setup"], 1)
                v.memset(max_prev[:, :], -BIG).then_inc(s["setup"], 1)
                v.memset(key_prev[:, :], -1.0).then_inc(s["setup"], 1)
                dve.wait_ge(s["iotas"], 2)
                v.tensor_scalar(head_m[:, :], head_i[:, :], H - 1, None, ALU.bitwise_and).then_inc(s["setup"], 1)
                v.tensor_copy(part8[:, :], pp8_i[:, :]).then_inc(s["setup"], 1)
                dve.wait_ge(s["setup"], 7)
                v.tensor_copy(head[:, :], head_m[:, :]).then_inc(s["setup"], 1)
                dve.wait_ge(s["setup"], 8)

                def reduce(c, par, i):
                    dve.wait_ge(s["kq_ready"], at("kq_ready", c * CH + i))
                    v.tensor_reduce(alpha[par][:, i * H:(i + 1) * H], by_head(kqq[i % 2][:, :], C), AX_X,
                                    ALU.add).then_inc(s["alpha_ready"], 1)

                def score(c, par, i):
                    e = ps_e[i % 2][:, 0:D]
                    kv = kv_ring[:, i % N_KV, :]
                    dve.wait_ge(s["e_ready"], at("e_ready", c * CH + i))
                    dve.wait_ge(kv_loaded[i % N_KV], c * (16 * CH // N_KV) + 16 * (i // N_KV + 1))
                    v.tensor_tensor(kq[i % 2][:, :], kv[:, 0:D], e, ALU.add).then_inc(s["ke_added"], 1)
                    v.tensor_tensor(by_head(ve[:, par, i, :], CP)[:, :, 0:C], by_head(kv[:, D:2 * D], C), by_head(e, C),
                                    ALU.add).then_inc(s["ve_added"], 1)
                    if i:
                        reduce(c, par, i - 1)
                    dve.wait_ge(s["ke_added"], at("ke_added", c * CH + i))
                    v.tensor_tensor(kqq[i % 2][:, :], kq[i % 2][:, :], ps_e[i % 2][:, D:2 * D], ALU.mult).then_inc(s["kq_ready"], 1)
                    if i == CH - 1:
                        reduce(c, par, i)


                SM = dict(mask=2, keys=2, runs=3, scan=2, spread=2, not_key=2, own_max=5, run_max=2, own_off=4, shift=4, carry=0)
                SM_BEFORE = {k: sum(list(SM.values())[:j]) for j, k in enumerate(SM)}
                SM_ALL = sum(SM.values())

                def softmax(c, par, part):
                    n = [0]

                    def step(ins):
                        n[0] += 1
                        ins.then_inc(s["sm_step"], 1)

                    def settle():
                        dve.wait_ge(s["sm_step"], (c - 1) * SM_ALL + (SM_BEFORE[part] + n[0]))

                    run = run_c[1 - par]
                    if part == "mask":
                        dve.wait_ge(s["alpha_ready"], at("alpha_ready", c * CH - 1))
                        v.scalar_tensor_tensor(out=by_head(am[:, :], H), in0=by_head(alpha[1 - par][:, :], H), scalar=SCALE,
                                               in1=mask[:, bass.ds((c - 1) * CH, CH)][:, :, None].to_broadcast([P, CH, H]),
                                               op0=ALU.mult, op1=ALU.add).then_inc(s["am_ready"], 1)
                        dve.wait_ge(run_loaded[1 - par], (c - (2 - par)) * 8 + 16)
                        step(v.tensor_scalar(key_f[:, :], run[:, 0:1], H / BIG, head[:, 0:1], ALU.mult, ALU.add))
                        step(v.tensor_scalar(key_l[:, :], run[:, P - 1:P], H / BIG, head[:, 0:1], ALU.mult, ALU.add))
                    elif part == "keys":
                        settle()
                        step(v.tensor_scalar(diag_k[:, 0:P], ident[:, :], key_f[:, 0:1], None, ALU.mult))
                        step(v.tensor_scalar(diag_k[:, P:2 * P], ident[:, :], key_l[:, 0:1], None, ALU.mult))
                        v.tensor_scalar(diag_k[:, 2 * P:], ident[:, P - H:P], key_prev[:, 0:1], None, ALU.mult).then_inc(s["keyed"], 1)
                    elif part == "runs":
                        step(v.tensor_tensor(resets[:, 1:P], run[:, 0:P - 1], run[:, 1:P], ALU.subtract))
                        step(v.tensor_scalar(off_first[:, :], run[:, :], run[:, 0:1], -1.0, ALU.subtract, ALU.mult))
                        step(v.tensor_scalar(off_last[:, :], run[:, :], run[:, P - 1:P], None, ALU.subtract))
                    elif part == "scan":
                        dve.wait_ge(s["am_turned"], at("am_turned", c - 1))
                        settle()
                        step(v.tensor_tensor_scan(out=scan_f[:, :], data0=resets[:, 0:P], data1=ps_a, initial=-BIG, op0=ALU.add, op1=ALU.max))
                        settle()
                        step(v.tensor_tensor_scan(out=scan_b[:, ::-1], data0=resets[:, P:0:-1], data1=scan_f[:, ::-1], initial=-BIG,
                                                  op0=ALU.add, op1=ALU.max))
                    elif part == "spread":
                        step(v.tensor_scalar(diag_r[:, P:2 * P], ident[:, :], scan_f[:, P - 1:P], None, ALU.mult))
                        step(v.tensor_scalar(diag_r[:, 2 * P:], ident[:, P - H:P], max_prev[:, 0:1], None, ALU.mult))
                        settle()
                        v.tensor_scalar(diag_r[:, 0:P], ident[:, :], scan_b[:, 0:1], None, ALU.mult).then_inc(s["r_ready"], 1)
                    elif part == "not_key":
                        step(v.tensor_scalar(not_f[:, :], ps_k, key_f[:, 0:1], -BIG, ALU.not_equal, ALU.mult))
                        step(v.tensor_scalar(not_l[:, :], ps_k, key_l[:, 0:1], -BIG, ALU.not_equal, ALU.mult))
                    elif part == "own_max":
                        step(v.tensor_copy(keys2[:, 0:1], ps_k[:, 0:1]))
                        step(v.tensor_copy(keys2[:, 1:2], ps_k[:, 2 * P:2 * P + 1]))
                        dve.wait_ge(s["max_spread"], at("max_spread", c - 1))
                        settle()
                        step(v.tensor_copy(carry[:, :], ps_r[:, 2 * P:]))
                        step(v.tensor_tensor(not_f[:, :], not_f[:, :], ps_r, ALU.add))
                        step(v.tensor_tensor(not_l[:, :], not_l[:, :], ps_r, ALU.add))
                    elif part == "run_max":
                        settle()
                        step(v.tensor_reduce(max_f[:, :], not_f[:, :], AX_X, ALU.max))
                        step(v.tensor_reduce(max_l[:, :], not_l[:, :], AX_X, ALU.max))
                        settle()
                        v.tensor_scalar(diag_f[:, :], ident[:, 0:H], max_f[:, 0:1], None, ALU.mult).then_inc(s["f_ready"], 1)
                    elif part == "own_off":
                        step(v.scalar_tensor_tensor(out=scan_b[:, :], in0=off_first[:, :], scalar=max_f[:, 0:1], in1=scan_b[:, :],
                                                    op0=ALU.add, op1=ALU.max))
                        step(v.tensor_tensor(same[:, :], keys2[:, 0:1], keys2[:, 1:2], ALU.is_equal))
                        step(v.tensor_scalar(node_key[:, :], chunk_tile[:, bass.ds(c - 1, 1)], float(P * H), part8[:, 0:1],
                                             ALU.mult, ALU.add))
                        settle()
                        step(v.scalar_tensor_tensor(out=off_last[:, :], in0=off_last[:, :], scalar=max_l[:, 0:1], in1=scan_b[:, :],
                                                    op0=ALU.add, op1=ALU.max))
                    elif part == "shift":
                        settle()
                        dve.wait_ge(s["shifted_turned"], at("shifted_turned", c - 2))
                        v.tensor_tensor(shifted[:, :], ps_a, off_last[:, :], ALU.subtract).then_inc(s["shifted_ready"], 1)
                        step(v.tensor_scalar(pick[:, :], node_key[:, :], keys2[:, 0:1], same[:, 0:1], ALU.is_equal, ALU.mult))
                        step(v.tensor_copy(max_prev[:, :], max_l[:, :]))
                        step(v.tensor_copy(key_prev[:, :], key_l[:, :]))
                        settle()
                        step(v.tensor_scalar(unpick[:, :], pick[:, :], -1.0, 1.0, ALU.mult, ALU.add))
                    else:
                        dve.wait_ge(s["ea_ready"], at("ea_ready", c - 1))
                        v.tensor_tensor(carry_d[:, :], carry[:, :], ps_f, ALU.subtract).then_inc(s["carry_ready"], 1)
                        dve.sem_inc(s["softmax_done"], 1)
                    assert n[0] == SM[part], (part, n[0])

                def rescale(c):
                    dve.wait_ge(s["carry_exp"], at("carry_exp", c))
                    v.tensor_scalar(factor[:, :], carry_e[:, :], pick[:, 0:1], unpick[:, 0:1], ALU.mult, ALU.add).then_inc(s["factor_ready"], 1)
                    n0 = dve.value_load(item_node_tile[0:1, bass.ds(c * CH, 1)], min_val=0, max_val=NT)
                    a = by_head(flat(acc[:, :, :])[:, bass.ds(n0 * UW, UW)], CP)
                    dve.wait_ge(s["factor_ready"], at("factor_ready", c))
                    dve.wait_ge(s["acc_added"], at("acc_added", c * CH - 1))
                    v.tensor_tensor(a, a, factor[:, :, None].to_broadcast([P, H, CP]), ALU.mult).then_inc(s["rescaled"], 1)
                    dve.wait_ge(s["rescaled"], at("rescaled", c))
                    dve.sem_inc(s["softmax_pace"], 1)

                def node_tile_of(c, i):
                    return dve.value_load(item_node_tile[0:1, bass.ds(c * CH + i, 1)], min_val=0, max_val=NT)

                def add(c, i, n):
                    m = c * CH + i
                    a = flat(acc[:, :, :])[:, bass.ds(n * UW, UW)]
                    dve.wait_ge(s["summed"], at("summed", m))
                    dve.wait_ge(s["acc_added"], at("acc_added", m - 1))
                    v.tensor_tensor(a, a, ps_u[i % 2][:, 0:UW], ALU.add).then_inc(s["acc_added"], 1)

                def emit(c, par, steps):
                    n = None
                    for at_step, (kind, i, back) in enumerate(steps):
                        if kind == "score":
                            for later, k, b in steps[at_step + 1:at_step + 3]:
                                if later == "add":
                                    n = node_tile_of(c - b, k)
                                elif later == "score":
                                    break
                            score(c, par, i)
                        elif kind in SM:
                            softmax(c, par, kind)
                        elif kind == "add":
                            if i == 0:
                                rescale(c - back)
                            add(c - back, i, n if n is not None else node_tile_of(c - back, i))
                            n = None

                parts = {i: k for i, k in enumerate(list(SM)[:-1])}
                over_chunks(dve, emit, what="add", parts={**parts, FIRST_WEIGH + 1: "carry"})

        x1 = q_sb
        xn2 = acc
        w1_sb = sb("w1_sb", [P, KD, NE * F])
        w2_sb = sb("w2_sb", [P, KF, NE * D])
        experts_loaded = sem("experts_loaded")
        with ExitStack() as c4:
            def sb4(name, shape, dt=F32):
                return sb(name, shape, dt, c4)

            wg_sb = sb4("wg_sb", [P, KD, NE])
            bg_sb = sb4("bg_sb", [P, NE])
            gb_sb = sb4("gb_sb", [P, NE])
            bias_sb = sb4("bias_sb", [P, NE])
            zeros = sb4("zeros", [P, 5 * D])
            SG = 4
            skip = [sb4(f"skip{i}", [P, SG, D]) for i in range(2)]
            den = sb4("den", [P, NT * H])
            inv = sb4("inv", [P, NT * H])
            stat = sb4("stat4", [P, NT, 6])
            mv = sb4("mv4", [P, NT, 2])
            vp = sb4("vp4", [P, NT])
            sd = sb4("sd4", [P, NT])
            r0 = sb4("r04", [P, NT])
            r1 = sb4("r14", [P, NT])
            r2 = sb4("r24", [P, NT])
            r3 = sb4("r34", [P, NT])
            rstd = sb4("rstd4", [P, NT])
            xnT = [sb4(f"xnT4{i}", [P, D]) for i in range(2)]
            xnc = [sb4(f"xnc{i}", [P, D]) for i in range(2)]
            ps_t = [c4.enter_context(nc.psum_tensor(f"ps_t4{i}", [P, 512], F32)) for i in range(2)]
            ps_g = [c4.enter_context(nc.psum_tensor(f"ps_g4{i}", [P, 512], F32)) for i in range(2)]
            s, at, grant = counters(c4, loaded=0, zero_set=0, zeroed=0, den_step=0, att_ready=0, x1_ready=0, stat_ready=0, aggregated=0,
                                    ln_step=0, var_ready=0, sd_ready=0, xn_ready=0, xn_turned=2, xn_kept=2, xnT_ready=2, gated=2,
                                    logits_ready=2, dve_pace=0, bias_ready=0)
            skip_loaded = [sem(f"skip_loaded{i}", c4) for i in range(2)]
            block = c4.enter_context(nc.Block())

            def over_tiles4(eng, emit):
                with eng.Fori(0, NT // 2) as g:
                    emit(g * 2, 0)
                    emit(g * 2 + 1, 1)
                if NT % 2:
                    emit(NT - 1, 0)

            ZR = 5
            NZ = ceil_div(NB, ZR)

            @block.sync
            def _(sp):
                sp.dma_start(wg_sb[:, :, :], Wg.rearrange("(k p) n -> p k n", p=P)).then_inc(s["loaded"], 16)
                sp.dma_start(bg_sb[:, :], bg.rearrange("(o n) -> o n", o=1).to_broadcast([P, NE])).then_inc(s["loaded"], 16)
                sp.dma_start(gb_sb[:, :], gbias.rearrange("(o n) -> o n", o=1).to_broadcast([P, NE])).then_inc(s["loaded"], 16)

                for g, j in enumerate(range(0, NT, SG)):
                    n = min(SG, NT - j)
                    if g >= 2:
                        sp.wait_ge(s["x1_ready"], g - 1)
                    sp.dma_start(skip[g % 2][:, 0:n, :],
                                 skip_table[j * P:(j + n) * P, :].rearrange("(j p) d -> p j d", p=P)).then_inc(skip_loaded[g % 2], 16)
                sp.wait_ge(s["zero_set"], 1)
                zr = sorted_x.rearrange("(p r) d -> p (r d)", p=P)
                for z in range(NZ):
                    w = min(ZR, NB - z * ZR) * D
                    sp.dma_start(zr[:, z * ZR * D:z * ZR * D + w], zeros[:, 0:w]).then_inc(s["zeroed"], 16)
                for k in range(KD):
                    sp.dma_start(w1_sb[:, k, :].rearrange("p (e f) -> p e f", e=NE),
                                 W1[:, k * P:(k + 1) * P, :].rearrange("e p f -> p e f")).then_inc(experts_loaded, 16)
                for k in range(KF):
                    sp.dma_start(w2_sb[:, k, :].rearrange("p (e f) -> p e f", e=NE),
                                 W2[:, k * P:(k + 1) * P, :].rearrange("e p f -> p e f")).then_inc(experts_loaded, 16)
                sp.wait_ge(s["zeroed"], 16 * NZ)

            @block.scalar
            def _(act):
                grant(act, "xnT_ready", "xn_kept")
                act.wait_ge(s["var_ready"], 1)
                nc.scalar.activation(sd[:, :], vp[:, :], ACT.Sqrt).then_inc(s["sd_ready"], 1)

                def tile(j, par):
                    act.wait_ge(s["xn_ready"], at("xn_ready", j))
                    nc.scalar.copy(flat(xn2[:, :, :])[:, bass.ds(j * UW, D)], xnc[par][:, :]).then_inc(s["xn_kept"], 1)
                    act.wait_ge(s["xn_turned"], at("xn_turned", j))
                    act.wait_ge(s["gated"], at("gated", j - 2))
                    nc.scalar.copy(xnT[par][:, :], ps_t[par][:, 0:D]).then_inc(s["xnT_ready"], 1)

                over_tiles4(act, tile)

            @block.tensor
            def _(pe):
                grant(pe, "gated", "xn_turned")
                pe.wait_ge(s["loaded"], 16 * 3)

                def turn(j, par):
                    pe.wait_ge(s["xn_ready"], at("xn_ready", j))
                    pe.wait_ge(s["xnT_ready"], at("xnT_ready", j - 2))
                    for k in range(KD):
                        last = nc.tensor.transpose(ps_t[par][:, k * P:(k + 1) * P], xnc[par][:, k * P:(k + 1) * P], ident[:, :])
                    last.then_inc(s["xn_turned"], 1)

                def gate(j, par):
                    pe.wait_ge(s["xnT_ready"], at("xnT_ready", j))
                    pe.wait_ge(s["logits_ready"], at("logits_ready", j - 2))
                    for k in range(KD):
                        last = nc.tensor.matmul(ps_g[par][:, 0:NE], xnT[par][:, k * P:(k + 1) * P], wg_sb[:, k, :],
                                                start=(k == 0), stop=(k == KD - 1))
                    last.then_inc(s["gated"], 1)

                turn(0, 0)
                with pe.Fori(0, (NT - 1) // 2) as g:
                    turn(g * 2 + 1, 1)
                    gate(g * 2, 0)
                    turn(g * 2 + 2, 0)
                    gate(g * 2 + 1, 1)
                for j in range(NT - 1 - (NT - 1) % 2, NT):
                    if j + 1 < NT:
                        turn(j + 1, (j + 1) % 2)
                    gate(j, j % 2)

            @block.vector
            def _(dve):
                v = nc.vector
                grant(dve, "logits_ready")
                v.memset(zeros[:, :], 0.0).then_inc(s["zero_set"], 1)
                dve.wait_ge(s["loaded"], 16 * 3)
                v.tensor_tensor(bias_sb[:, :], bg_sb[:, :], gb_sb[:, :], ALU.add).then_inc(s["bias_ready"], 1)
                dve.wait_ge(s["bias_ready"], 1)

                heads = flat(acc[:, :, :]).rearrange("p (n c) -> p n c", c=CP)[:, 0:NT * H, :]
                x1_heads = flat(x1[:, :, :]).rearrange("p (n c) -> p n c", c=C)
                v.tensor_scalar(den[:, :], heads[:, :, C:CP].rearrange("p n c -> p (n c)"), 1e-16, None, ALU.add).then_inc(s["den_step"], 1)
                dve.wait_ge(s["den_step"], 1)
                v.reciprocal(inv[:, :], den[:, :]).then_inc(s["den_step"], 1)
                dve.wait_ge(s["den_step"], 2)
                for g, j in enumerate(range(0, NT, SG)):
                    a, b = j * H, min(j + SG, NT) * H
                    v.tensor_tensor(x1_heads[:, a:b, :], heads[:, a:b, 0:C], inv[:, a:b][:, :, None].to_broadcast([P, b - a, C]),
                                    ALU.mult).then_inc(s["att_ready"], 1)
                    dve.wait_ge(s["att_ready"], g + 1)
                    dve.wait_ge(skip_loaded[g % 2], 16 * (g // 2 + 1))
                    n = min(SG, NT - j)
                    v.tensor_tensor(x1[:, j:j + n, :], x1[:, j:j + n, :], skip[g % 2][:, 0:n, :], ALU.add).then_inc(s["x1_ready"], 1)
                dve.wait_ge(s["x1_ready"], ceil_div(NT, SG))
                dve.sem_inc(s["dve_pace"], 1)
                layernorm_stats(dve, over_tiles4, s, flat(x1[:, :, :]), stat, mv, vp, sd, (r0, r1, r2, r3), rstd)

                def node_tile(j, par):
                    dve.wait_ge(s["xn_turned"], at("xn_turned", j - 2))
                    dve.wait_ge(s["xn_kept"], at("xn_kept", j - 2))
                    v.tensor_scalar(xnc[par][:, :], flat(x1[:, :, :])[:, bass.ds(j * D, D)], flat(mv[:, :, :])[:, bass.ds(j * 2, 1)],
                                    rstd[:, bass.ds(j, 1)], ALU.subtract, ALU.mult).then_inc(s["xn_ready"], 1)

                def gate(j, par):
                    dve.wait_ge(s["gated"], at("gated", j))
                    v.tensor_tensor(flat(logits)[:, bass.ds(j * NE, NE)], ps_g[par][:, 0:NE], bias_sb[:, :],
                                    ALU.add).then_inc(s["logits_ready"], 1)

                node_tile(0, 0)
                node_tile(1, 1)
                with dve.Fori(0, (NT - 2) // 2) as g:
                    node_tile(g * 2 + 2, 0)
                    gate(g * 2, 0)
                    node_tile(g * 2 + 3, 1)
                    gate(g * 2 + 1, 1)
                for j in range(2 * ((NT - 2) // 2), NT):
                    if j + 2 < NT:
                        node_tile(j + 2, j % 2)
                    gate(j, j % 2)

        with ExitStack() as c5:
            def sb5(name, shape, dt=F32):
                return sb(name, shape, dt, c5)

            top8 = sb5("top8", [P, NT, 8])
            rank = sb5("rank", [P, NT, NE])
            more = sb5("more", [P, NT, NE])
            diff = sb5("diff", [P, NT])
            ex = sb5("ex", [P, NT])
            exp1 = sb5("exp1", [P, NT])
            taken = sb5("taken", [P, NT, NE])
            is_k = [sb5(f"is_k{k}", [P, NT, NE]) for k in range(TOP)]
            lower = sb5("lower", [P, P])
            totals = sb5("totals", [P, NE, NT])
            zeros_t = sb5("zeros_t", [P, NE, NT])
            running = sb5("running", [P, NE, NT])
            count_i = sb5("count_i", [P, NE], I32)
            blocks_i = sb5("blocks_i", [P, NE], I32)
            blocks = sb5("blocks", [P, NE])
            ends = sb5("ends", [P, NE])
            starts = sb5("starts", [P, NE])
            place = sb5("place", [P, NT, NE])
            place2 = sb5("place2", [P, NT, NE])
            slots = sb5("slots", [P, TOP, NT])
            bi_i = sb5("bi_i", [1, NB], I32)
            bi = sb5("bi", [1, NB])
            be = sb5("be", [1, NB])
            ps_pre = c5.enter_context(nc.psum_tensor("ps_pre", [P, 512], F32))
            ps_tot = c5.enter_context(nc.psum_tensor("ps_tot", [P, 512], F32))
            dve_step = sem("route_step", c5)
            diff_ready = sem("diff_ready", c5)
            exp_ready = sem("exp_ready", c5)
            taken_ready = sem("taken_ready", c5)
            counted = sem("counted", c5)
            bi_set = sem("bi_set", c5)
            block = c5.enter_context(nc.Block())
            assert NT * NE <= 512 and NE == 8

            @block.gpsimd
            def _(pool):
                nc.gpsimd.iota(bi_i[:, :], [[1, NB]], base=0, channel_multiplier=0).then_inc(bi_set, 1)

            @block.scalar
            def _(act):
                act.wait_ge(diff_ready, 1)
                nc.scalar.activation(ex[:, :], diff[:, :], ACT.Exp).then_inc(exp_ready, 1)

            @block.tensor
            def _(pe):
                pe.wait_ge(taken_ready, 1)
                tk = taken[:, :, :].rearrange("p j e -> p (j e)")
                nc.tensor.matmul(ps_pre[:, 0:NT * NE], lower[:, :], tk, start=True, stop=True)
                nc.tensor.matmul(ps_tot[:, 0:NT * NE], ones[:, :], tk, start=True, stop=True).then_inc(counted, 1)

            @block.vector
            def _(dve):
                v = nc.vector
                count = [0]

                def then(ins):
                    count[0] += 1
                    ins.then_inc(dve_step, 1)
                    dve.wait_ge(dve_step, count[0])

                for j in range(NT):
                    last = v.max(top8[:, j, :], logits[:, j, :])
                then(last)
                then(v.tensor_tensor(diff[:, :], top8[:, :, 1:2].rearrange("p j o -> p (j o)"),
                                     top8[:, :, 0:1].rearrange("p j o -> p (j o)"), ALU.subtract))
                dve.sem_inc(diff_ready, 1)
                then(v.memset(rank[:, :, :], 0.0))
                for f in range(NE):
                    lf = logits[:, :, f:f + 1]
                    if f:
                        v.tensor_tensor(more[:, :, 0:f], lf.to_broadcast([P, NT, f]), logits[:, :, 0:f], ALU.is_gt)
                    then(v.tensor_tensor(more[:, :, f:NE], lf.to_broadcast([P, NT, NE - f]), logits[:, :, f:NE], ALU.is_ge))
                    then(v.tensor_tensor(rank[:, :, :], rank[:, :, :], more[:, :, :], ALU.add))
                v.tensor_scalar(lower[:, :], iota_free[:, :], iota_part[:, 0:1], None, ALU.is_gt)
                v.tensor_scalar(is_k[0][:, :, :], rank[:, :, :], 1.0, None, ALU.is_equal)
                v.tensor_scalar(is_k[1][:, :, :], rank[:, :, :], 2.0, None, ALU.is_equal)
                v.tensor_scalar(taken[:, :, :], rank[:, :, :], TOP + 0.5, None, ALU.is_lt).then_inc(taken_ready, 1)
                dve.wait_ge(exp_ready, 1)
                then(v.tensor_scalar(exp1[:, :], ex[:, :], 1.0, None, ALU.add))
                then(v.reciprocal(gate_w[:, 0, :], exp1[:, :]))
                then(v.tensor_tensor(gate_w[:, 1, :], ex[:, :], gate_w[:, 0, :], ALU.mult))
                dve.wait_ge(counted, 1)
                v.memset(zeros_t[:, :, :], 0.0)
                then(v.tensor_copy(totals[:, :, :], ps_tot[:, 0:NT * NE].rearrange("p (j e) -> p e j", e=NE)))
                for e in range(NE):
                    last = v.tensor_tensor_scan(out=running[:, e, :], data0=zeros_t[:, e, :], data1=totals[:, e, :], initial=0.0,
                                                op0=ALU.add, op1=ALU.add)
                then(last)
                then(v.tensor_scalar(count_i[:, :], running[:, :, NT - 1:NT].rearrange("p e o -> p (e o)"), float(P - 1), None, ALU.add))
                then(v.tensor_scalar(blocks_i[:, :], count_i[:, :], P.bit_length() - 1, None, ALU.logical_shift_right))
                then(v.tensor_copy(blocks[:, :], blocks_i[:, :]))
                then(v.tensor_tensor_scan(out=ends[:, :], data0=zeros_t[:, :, :].rearrange("p e j -> p (e j)")[:, 0:NE], data1=blocks[:, :], initial=0.0, op0=ALU.add, op1=ALU.add))
                then(v.tensor_tensor(starts[:, :], ends[:, :], blocks[:, :], ALU.subtract))
                then(v.tensor_scalar(starts[:, :], starts[:, :], float(P), None, ALU.mult))
                then(v.tensor_tensor(place[:, :, :], running[:, :, :].rearrange("p e j -> p j e"),
                                     totals[:, :, :].rearrange("p e j -> p j e"), ALU.subtract))
                then(v.tensor_tensor(place2[:, :, :], place[:, :, :], ps_pre[:, 0:NT * NE].rearrange("p (j e) -> p j e", e=NE), ALU.add))
                then(v.tensor_tensor(place[:, :, :], place2[:, :, :], starts[:, None, :].to_broadcast([P, NT, NE]), ALU.add))
                for k in range(TOP):
                    then(v.tensor_tensor(place2[:, :, :], place[:, :, :], is_k[k][:, :, :], ALU.mult))
                    then(v.tensor_reduce(slots[:, k, :], place2[:, :, :], AX_X, ALU.add))
                v.tensor_copy(slot_i[:, :, :], slots[:, :, :])
                dve.wait_ge(bi_set, 1)
                then(v.tensor_copy(bi[:, :], bi_i[:, :]))
                then(v.memset(be[:, :], 0.0))
                for e in range(NE - 1):
                    then(v.scalar_tensor_tensor(out=be[:, :], in0=bi[:, :], scalar=ends[0:1, e:e + 1], in1=be[:, :], op0=ALU.is_ge, op1=ALU.add))
                v.tensor_copy(block_expert[:, :], be[:, :])

        with ExitStack() as c6:
            scattered = sem("scattered", c6)
            block = c6.enter_context(nc.Block())

            @block.gpsimd
            def _(pool):
                for j in range(NT):
                    for k in range(TOP):
                        nc.gpsimd.indirect_dma_start(
                            out=sorted_x, out_offset=bass.IndirectOffsetOnAxis(ap=slot_i[:, k, j:j + 1], axis=0),
                            in_=xn2[:, j, 0:D], in_offset=None).then_inc(scattered, 16)
                pool.wait_ge(scattered, 16 * NT * TOP)

        with ExitStack() as c7:
            def sb7(name, shape, dt=F32):
                return sb(name, shape, dt, c7)

            in_acc = NE * (F + D) <= (NT + 1) * UW
            biases = flat(acc[:, :, :]) if in_acc else sb7("biases", [P, NE * (F + D)])
            b1_sb = biases[:, 0:NE * F]
            b2_sb = biases[:, NE * F:NE * (F + D)]
            t_in = [sb7(f"t_in{i}", [P, D]) for i in range(2)]
            tT = [sb7(f"tT{i}", [P, D]) for i in range(2)]
            hid = [sb7(f"hid{i}", [P, F]) for i in range(2)]
            hT = [sb7(f"hT{i}", [P, F]) for i in range(2)]
            y = [sb7(f"y{i}", [P, D]) for i in range(2)]
            ps_t = [c7.enter_context(nc.psum_tensor(f"ps_t7{i}", [P, 512], F32)) for i in range(2)]
            ps_h = [c7.enter_context(nc.psum_tensor(f"ps_h7{i}", [P, 512], F32)) for i in range(2)]
            ps_ht = [c7.enter_context(nc.psum_tensor(f"ps_ht7{i}", [P, 512], F32)) for i in range(2)]
            ps_y = [c7.enter_context(nc.psum_tensor(f"ps_y7{i}", [P, 512], F32)) for i in range(2)]
            s, at, grant = counters(c7, loaded=0, x_turned=2, tT_ready=2, h_summed=2, hid_ready=2, h_turned=2, hT_ready=2,
                                    y_summed=3, y_ready=2, act_pace=0, dve_pace=0)
            x_loaded = [sem(f"x_loaded{i}", c7) for i in range(2)]
            y_stored = [sem(f"y_stored{i}", c7) for i in range(2)]
            block = c7.enter_context(nc.Block())
            assert F == 512 and NB >= 4

            def live(k):
                return not isinstance(k, int) or 0 <= k < NB

            def over_blocks(eng, emit):
                emit(0, 0)
                emit(1, 1)
                pairs = (NB - 3) // 2
                with eng.Fori(0, pairs) as g:
                    emit(g * 2 + 2, 0)
                    emit(g * 2 + 3, 1)
                for b in range(2 + 2 * pairs, NB + 2):
                    emit(b, b % 2)

            def expert_of(eng, b):
                return eng.value_load(block_expert[0:1, bass.ds(b, 1)], min_val=0, max_val=NE - 1)

            @block.sync
            def _(sp):
                def load(b, par):
                    sp.wait_ge(s["x_turned"], at("x_turned", b - 2))
                    sp.dma_start(t_in[par][:, :], sorted_x[bass.ds(b * P, P), :]).then_inc(x_loaded[par], 16)

                load(0, 0)
                load(1, 1)
                sp.dma_start(b1_sb[:, :], b1.rearrange("(o e) f -> o (e f)", o=1).to_broadcast([P, NE * F])).then_inc(s["loaded"], 16)
                sp.dma_start(b2_sb[:, :], b2.rearrange("(o e) f -> o (e f)", o=1).to_broadcast([P, NE * D])).then_inc(s["loaded"], 16)
                with sp.Fori(0, (NB - 2) // 2) as g:
                    load(g * 2 + 2, 0)
                    load(g * 2 + 3, 1)
                if NB % 2:
                    load(NB - 1, 0)

            @block.scalar
            def _(act):
                grant(act, "tT_ready", "hT_ready")

                def turned_x(b, par):
                    act.wait_ge(s["x_turned"], at("x_turned", b))
                    act.wait_ge(s["h_summed"], at("h_summed", b - 2))
                    nc.scalar.copy(tT[par][:, :], ps_t[par][:, 0:D]).then_inc(s["tT_ready"], 1)

                def emit(b, par):
                    if isinstance(b, int) and b == 0:
                        turned_x(0, 0)
                    if live(b + 1):
                        turned_x(b + 1, 1 - par)
                    if live(b - 1):
                        act.wait_ge(s["h_turned"], at("h_turned", b - 1))
                        act.sem_inc(s["act_pace"], 1)
                        act.wait_ge(s["y_summed"], at("y_summed", b - 3))
                        act.sem_inc(s["act_pace"], 1)
                        nc.scalar.activation(hT[1 - par][:, :], ps_ht[1 - par][:, :], ACT.Relu).then_inc(s["hT_ready"], 1)
                    if live(b - 2):
                        act.wait_ge(s["y_ready"], at("y_ready", b - 2))
                        act.dma_start(sorted_y[bass.ds((b - 2) * P, P), :], y[par][:, :]).then_inc(y_stored[par], 16)

                over_blocks(act, emit)
                act.wait_ge(y_stored[0], 16 + 16 * ceil_div(NB, 2))
                act.wait_ge(y_stored[1], 16 + 16 * (NB // 2))

            @block.tensor
            def _(pe):
                t = nc.tensor
                grant(pe, "x_turned", "h_summed", "h_turned", "y_summed")

                def turn_x(b, par):
                    pe.wait_ge(x_loaded[par], (b - par) * 8 + 16)
                    pe.wait_ge(s["tT_ready"], at("tT_ready", b - 2))
                    for k in range(KD):
                        last = t.transpose(ps_t[par][:, k * P:(k + 1) * P], t_in[par][:, k * P:(k + 1) * P], ident[:, :])
                    last.then_inc(s["x_turned"], 1)

                def turn_h(b, par):
                    pe.wait_ge(s["hid_ready"], at("hid_ready", b))
                    pe.wait_ge(s["hT_ready"], at("hT_ready", b - 2))
                    for k in range(KF):
                        last = t.transpose(ps_ht[par][:, k * P:(k + 1) * P], hid[par][:, k * P:(k + 1) * P], ident[:, :])
                    last.then_inc(s["h_turned"], 1)

                def hidden(b, par, ex):
                    pe.wait_ge(s["tT_ready"], at("tT_ready", b))
                    pe.wait_ge(s["hid_ready"], at("hid_ready", b - 2))
                    for k in range(KD):
                        last = t.matmul(ps_h[par][:, :], tT[par][:, k * P:(k + 1) * P], w1_sb[:, k, bass.ds(ex * F, F)],
                                        start=(k == 0), stop=(k == KD - 1))
                    last.then_inc(s["h_summed"], 1)

                def output(b, par, ex):
                    pe.wait_ge(s["hT_ready"], at("hT_ready", b))
                    pe.wait_ge(s["y_ready"], at("y_ready", b - 2))
                    for k in range(KF):
                        last = t.matmul(ps_y[par][:, 0:D], hT[par][:, k * P:(k + 1) * P], w2_sb[:, k, bass.ds(ex * D, D)],
                                        start=(k == 0), stop=(k == KF - 1))
                    last.then_inc(s["y_summed"], 1)

                def emit(b, par):
                    ex = expert_of(pe, b) if live(b) else None
                    ex_before = expert_of(pe, b - 1) if live(b - 1) else None
                    if isinstance(b, int) and b == 0:
                        turn_x(0, 0)
                        pe.wait_ge(experts_loaded, 16 * (KD + KF))
                    if live(b + 1):
                        turn_x(b + 1, 1 - par)
                    if live(b - 1):
                        turn_h(b - 1, 1 - par)
                    if live(b):
                        hidden(b, par, ex)
                    if live(b - 1):
                        output(b - 1, 1 - par, ex_before)

                over_blocks(pe, emit)

            @block.vector
            def _(dve):
                v = nc.vector
                grant(dve, "hid_ready", "y_ready")
                dve.sem_inc(y_stored[0], 16)
                dve.sem_inc(y_stored[1], 16)
                dve.wait_ge(s["loaded"], 16 * 2)
                dve.sem_inc(s["dve_pace"], 1)

                def emit(b, par):
                    ex_before = expert_of(dve, b - 2) if live(b - 2) else None
                    ex = expert_of(dve, b) if live(b) else None
                    if live(b - 2):
                        dve.wait_ge(s["y_summed"], at("y_summed", b - 2))
                        dve.wait_ge(y_stored[par], (b - par) * 8)
                        v.tensor_tensor(y[par][:, :], ps_y[par][:, 0:D], b2_sb[:, bass.ds(ex_before * D, D)],
                                        ALU.add).then_inc(s["y_ready"], 1)
                    if live(b):
                        dve.wait_ge(s["h_summed"], at("h_summed", b))
                        dve.wait_ge(s["h_turned"], at("h_turned", b - 2))
                        v.tensor_tensor(hid[par][:, :], ps_h[par][:, :], b1_sb[:, bass.ds(ex * F, F)],
                                        ALU.add).then_inc(s["hid_ready"], 1)

                over_blocks(dve, emit)

        with ExitStack() as c8:
            NG = 4
            got = [[sb(f"got{k}_{i}", [P, D], F32, c8) for i in range(NG)] for k in range(TOP)]
            half = [sb(f"half{i}", [P, D], F32, c8) for i in range(2)]
            o = [sb(f"o{i}", [P, D], F32, c8) for i in range(NG)]
            g_loaded = [sem(f"g_loaded{i}", c8) for i in range(NG)]
            halved = sem("halved", c8)
            summed = sem("out_summed", c8)
            out_stored = [sem(f"out_stored{i}", c8) for i in range(NG)]
            block = c8.enter_context(nc.Block())

            @block.gpsimd
            def _(pool):
                for j in range(NT):
                    if j >= NG:
                        pool.wait_ge(summed, j - NG + 1)
                    for k in range(TOP):
                        nc.gpsimd.indirect_dma_start(
                            out=got[k][j % NG][:, :], out_offset=None, in_=sorted_y,
                            in_offset=bass.IndirectOffsetOnAxis(ap=slot_i[:, k, j:j + 1], axis=0)).then_inc(g_loaded[j % NG], 16)

            @block.vector
            def _(dve):
                for j in range(NT):
                    dve.wait_ge(g_loaded[j % NG], 32 * (j // NG + 1))
                    nc.vector.scalar_tensor_tensor(out=half[j % 2][:, :], in0=got[0][j % NG][:, :], scalar=gate_w[:, 0, j:j + 1],
                                                   in1=x1[:, j, :], op0=ALU.mult, op1=ALU.add).then_inc(halved, 1)
                    dve.wait_ge(halved, j + 1)
                    if j >= NG:
                        dve.wait_ge(out_stored[j % NG], 16 * (j // NG))
                    nc.vector.scalar_tensor_tensor(out=o[j % NG][:, :], in0=got[1][j % NG][:, :], scalar=gate_w[:, 1, j:j + 1],
                                                   in1=half[j % 2][:, :], op0=ALU.mult, op1=ALU.add).then_inc(summed, 1)

            @block.sync
            def _(sp):
                for j in range(NT):
                    n = P if j < NT - 1 else NTAIL
                    sp.wait_ge(summed, j + 1)
                    sp.dma_start(out[j * P:j * P + n, :], o[j % NG][0:n, :]).then_inc(out_stored[j % NG], 16)
                for i in range(NG):
                    sp.wait_ge(out_stored[i], 16 * ((NT - i + NG - 1) // NG))


_INS = ["x", "src", "dst", "edge_attr_256", "L0_gnn_Wq", "L0_gnn_bq", "L0_gnn_Wk", "L0_gnn_bk", "L0_gnn_Wv", "L0_gnn_bv",
        "L0_gnn_We", "L0_gnn_Ws", "L0_gnn_bs", "L0_ffn_Wg", "L0_ffn_bg", "L0_ffn_bias", "L0_ffn_W1", "L0_ffn_b1",
        "L0_ffn_W2", "L0_ffn_b2"]


def kernel(**inputs):
    import numpy as _np
    import concourse.bacc as _bacc
    from concourse import mybir as _mybir
    from concourse.bass_utils import run_bass_kernel_spmd as _run

    nc = _bacc.Bacc("TRN2", target_bir_lowering=False, num_devices=1)
    arrays, args = {}, []
    for name in _INS:
        a = _np.ascontiguousarray(inputs[name])
        arrays[f"in_{name}"] = a
        args.append(nc.dram_tensor(f"in_{name}", a.shape, _mybir.dt.from_np(a.dtype), kind="ExternalInput").ap())
    n, d = inputs["x"].shape
    args.append(nc.dram_tensor("out_0", (n, d), F32, kind="ExternalOutput").ap())
    gnn_ffn(nc, *args)
    r = _run(nc, [arrays], core_ids=[0])
    return r.results[0]["out_0"]
```
